# Optimizing a Trainium2 kernel written in Bass

```python
import numpy as np
import jax
import jax.numpy as jnp

def _softmax(x, axis=-1):
    return jax.nn.softmax(x, axis=axis)

def _gelu(x):
    return jax.nn.gelu(x, approximate=True)

def _silu(x):
    return jax.nn.silu(x)

def _sigmoid(x):
    return jax.nn.sigmoid(x)

def _layernorm(x, axis=-1, eps=1e-05):
    m = jnp.mean(x, axis=axis, keepdims=True)
    v = jnp.var(x, axis=axis, keepdims=True)
    return (x - m) / jnp.sqrt(v + eps)

def _scatter_add(tgt, idx, src, axis=0):
    return tgt.at[idx].add(src)

def _segment_sum(src, seg, n):
    return jax.ops.segment_sum(src, seg, n)
kernel_name = 'mk_flamingo_gated_d2_seqx_r8_9feb47'

def setup_inputs(seed: int=0):
    np.random.seed(seed)
    _w = jnp.asarray

    def _rec_inputs():
        import jax
        import jax.numpy as jnp
        _rk = jax.random.key(seed)
        x = -0.000125 + 0.9999 * jax.random.normal(jax.random.fold_in(_rk, 1), (128, 64, 128), jnp.float32)
        _lenS = 64 - jax.random.randint(jax.random.fold_in(_rk, 7), (128,), 0, max(1, 64 // 4) + 1, jnp.int32)
        _lenS2 = 64 - jax.random.randint(jax.random.fold_in(_rk, 8), (128,), 0, max(1, 64 // 4) + 1, jnp.int32)
        _ctx_768P = jax.random.normal(jax.random.fold_in(_rk, 11), (128, 16, 96), jnp.float32)
        _ctx_768c = jax.random.dirichlet(jax.random.fold_in(_rk, 511), 0.3 * jnp.ones((16,), jnp.float32), (128, 64))
        _ctx_768t = jnp.einsum('bsk,bkd->bsd', _ctx_768c, _ctx_768P)
        _ctx_768t = _ctx_768t * jax.lax.rsqrt(jnp.mean(jnp.square(_ctx_768t)) + 1e-12) * 0.953939
        ctx_768 = 0.00272024 + 0.999456 * (_ctx_768t + 0.3 * jax.random.normal(jax.random.fold_in(_rk, 611), (128, 64, 96), jnp.float32))
        _g = jax.random.normal(jax.random.fold_in(_rk, 9001), (2, 2), jnp.float32)
        _g = jnp.sign(_g) * jnp.maximum(jnp.abs(_g), 1.0) + (_g == 0) * 1.0
        g_xattn = _g[0]
        g_ffn = _g[1]
        return (x, ctx_768, g_xattn, g_ffn)
    x, ctx_768, g_xattn, g_ffn = _rec_inputs()

    def _L0_xattn_setup():
        import jax, jax.numpy as jnp
        import numpy as np
        N_HEADS = 16
        DIM_EMBED = 128
        DIM_CROSS = 96
        DIM_HEAD = DIM_EMBED // N_HEADS
        key = jax.random.key(seed)
        ks = jax.random.split(key, 10)
        B, Sq, Sk = (8, 512, 77)
        s_e = 1.0 / np.sqrt(DIM_EMBED)
        s_c = 1.0 / np.sqrt(DIM_CROSS)
        return {'x': jax.random.normal(ks[0], (B, Sq, DIM_EMBED), jnp.float32), 'y': jax.random.normal(ks[1], (B, Sk, DIM_CROSS), jnp.float32), 'wq': jax.random.normal(ks[2], (DIM_EMBED, DIM_EMBED), jnp.float32) * s_e, 'bq': jax.random.normal(ks[3], (DIM_EMBED,), jnp.float32) * 0.01, 'wk': jax.random.normal(ks[4], (DIM_CROSS, DIM_EMBED), jnp.float32) * s_c, 'bk': jax.random.normal(ks[5], (DIM_EMBED,), jnp.float32) * 0.01, 'wv': jax.random.normal(ks[6], (DIM_CROSS, DIM_EMBED), jnp.float32) * s_c, 'bv': jax.random.normal(ks[7], (DIM_EMBED,), jnp.float32) * 0.01, 'wo': jax.random.normal(ks[8], (DIM_EMBED, DIM_EMBED), jnp.float32) * s_e, 'bo': jax.random.normal(ks[9], (DIM_EMBED,), jnp.float32) * 0.01}
    _L0_xattn_all = _L0_xattn_setup()
    _L0_xattn_in = {k: v for k, v in _L0_xattn_all.items() if k in ('wq', 'bq', 'wk', 'bk', 'wv', 'bv', 'wo', 'bo')}
    del _L0_xattn_all

    def _L0_ffn_setup():
        import jax, jax.numpy as jnp
        import numpy as np
        B, T, D_MODEL = (4, 256, 128)
        N_EXPERTS, TOP_K, D_EXPERT = (6, 2, 64)
        QUANT_TEMP = 0.3
        _ANCHOR_IDS = [63, 6, 0, 18, 45, 27]

        def _q6_idx_to_vertex(idx):
            bits = [idx >> 5 - b & 1 for b in range(6)]
            return [2.0 * b - 1.0 for b in bits]

        def _anchors():
            return jnp.asarray(np.array([_q6_idx_to_vertex(i) for i in _ANCHOR_IDS], dtype=np.float32))

        def _router(x, proj_w, anchors, routing_temp):
            z = jnp.einsum('btd,ed->bte', x, proj_w)
            q = jnp.tanh(z / QUANT_TEMP)
            dot = jnp.einsum('btd,ed->bte', q, anchors)
            hamming = (6.0 - dot) * 0.5
            logits = -hamming / jnp.clip(routing_temp, 0.1)
            topk_logits, topk_idx = jax.lax.top_k(logits, TOP_K)
            topk_w = jax.nn.softmax(topk_logits, axis=-1)
            onehot = jax.nn.one_hot(topk_idx, N_EXPERTS, dtype=x.dtype)
            expert_weights = jnp.einsum('btke,btk->bte', onehot, topk_w)
            return (expert_weights, q)
        key = jax.random.key(seed)
        k_x, k_p, k_w1, k_w2 = jax.random.split(key, 4)
        x = jax.random.normal(k_x, (B, T, D_MODEL), dtype=jnp.float32)
        proj_w = jax.random.normal(k_p, (6, D_MODEL), dtype=jnp.float32) * 0.02
        anchors = _anchors()
        routing_temp = jnp.array(1.0, dtype=jnp.float32)
        s1 = 1.0 / np.sqrt(D_MODEL)
        s2 = 1.0 / np.sqrt(D_EXPERT)
        w1 = jax.random.uniform(k_w1, (N_EXPERTS, D_MODEL, D_EXPERT), jnp.float32, -s1, s1)
        w2 = jax.random.uniform(k_w2, (N_EXPERTS, D_EXPERT, D_MODEL), jnp.float32, -s2, s2)
        return {'x': x, 'proj_w': proj_w, 'anchors': anchors, 'routing_temp': routing_temp, 'w1': w1, 'w2': w2}
    _L0_ffn_all = _L0_ffn_setup()
    _L0_ffn_in = {k: v for k, v in _L0_ffn_all.items() if k in ('proj_w', 'anchors', 'routing_temp', 'w1', 'w2')}
    del _L0_ffn_all

    def _L1_xattn_setup():
        import jax, jax.numpy as jnp
        import numpy as np
        IMG_DIM, TXT_DIM, HID = (128, 96, 128)
        B, LQ, LK = (8, 256, 256)
        key = jax.random.key(seed)
        ks = jax.random.split(key, 8)
        s_img = 1.0 / np.sqrt(IMG_DIM)
        s_txt = 1.0 / np.sqrt(TXT_DIM)
        return {'image_features': jax.random.normal(ks[0], (B, LQ, IMG_DIM), jnp.float32), 'text_features': jax.random.normal(ks[1], (B, LK, TXT_DIM), jnp.float32), 'Wq': jax.random.uniform(ks[2], (IMG_DIM, HID), jnp.float32, -s_img, s_img), 'bq': jax.random.uniform(ks[3], (HID,), jnp.float32, -s_img, s_img), 'Wk': jax.random.uniform(ks[4], (TXT_DIM, HID), jnp.float32, -s_txt, s_txt), 'bk': jax.random.uniform(ks[5], (HID,), jnp.float32, -s_txt, s_txt), 'Wv': jax.random.uniform(ks[6], (TXT_DIM, HID), jnp.float32, -s_txt, s_txt), 'bv': jax.random.uniform(ks[7], (HID,), jnp.float32, -s_txt, s_txt)}
    _L1_xattn_all = _L1_xattn_setup()
    _L1_xattn_in = {k: v for k, v in _L1_xattn_all.items() if k in ('Wq', 'bq', 'Wk', 'bk', 'Wv', 'bv')}
    del _L1_xattn_all

    def _L1_ffn_setup():
        import jax, jax.numpy as jnp
        import numpy as np
        E = 8
        TOP_K = 2
        D = 128
        H = 2 * D
        key = jax.random.key(seed)
        k0, k1, k2, k3, k4 = jax.random.split(key, 5)
        scale = 0.02
        x = jax.random.normal(k0, (4, 256, D), dtype=jnp.float32)
        Wg = jax.random.normal(k1, (D, E), dtype=jnp.float32) * scale
        W1 = jax.random.normal(k2, (E, D, H), dtype=jnp.float32) * scale
        W2 = jax.random.normal(k3, (E, D, H), dtype=jnp.float32) * scale
        W3 = jax.random.normal(k4, (E, H, D), dtype=jnp.float32) * scale
        return {'x': x, 'Wg': Wg, 'W1': W1, 'W2': W2, 'W3': W3}
    _L1_ffn_all = _L1_ffn_setup()
    _L1_ffn_in = {k: v for k, v in _L1_ffn_all.items() if k in ('Wg', 'W1', 'W2', 'W3')}
    del _L1_ffn_all
    return {'x': x, 'ctx_768': ctx_768, 'g_xattn': g_xattn, 'g_ffn': g_ffn, 'L0_xattn_wq': _L0_xattn_in['wq'], 'L0_xattn_bq': _L0_xattn_in['bq'], 'L0_xattn_wk': _L0_xattn_in['wk'], 'L0_xattn_bk': _L0_xattn_in['bk'], 'L0_xattn_wv': _L0_xattn_in['wv'], 'L0_xattn_bv': _L0_xattn_in['bv'], 'L0_xattn_wo': _L0_xattn_in['wo'], 'L0_xattn_bo': _L0_xattn_in['bo'], 'L0_ffn_proj_w': _L0_ffn_in['proj_w'], 'L0_ffn_anchors': _L0_ffn_in['anchors'], 'L0_ffn_routing_temp': _L0_ffn_in['routing_temp'], 'L0_ffn_w1': _L0_ffn_in['w1'], 'L0_ffn_w2': _L0_ffn_in['w2'], 'L1_xattn_Wq': _L1_xattn_in['Wq'], 'L1_xattn_bq': _L1_xattn_in['bq'], 'L1_xattn_Wk': _L1_xattn_in['Wk'], 'L1_xattn_bk': _L1_xattn_in['bk'], 'L1_xattn_Wv': _L1_xattn_in['Wv'], 'L1_xattn_bv': _L1_xattn_in['bv'], 'L1_ffn_Wg': _L1_ffn_in['Wg'], 'L1_ffn_W1': _L1_ffn_in['W1'], 'L1_ffn_W2': _L1_ffn_in['W2'], 'L1_ffn_W3': _L1_ffn_in['W3']}

def reference(x, ctx_768, g_xattn, g_ffn, L0_xattn_wq, L0_xattn_bq, L0_xattn_wk, L0_xattn_bk, L0_xattn_wv, L0_xattn_bv, L0_xattn_wo, L0_xattn_bo, L0_ffn_proj_w, L0_ffn_anchors, L0_ffn_routing_temp, L0_ffn_w1, L0_ffn_w2, L1_xattn_Wq, L1_xattn_bq, L1_xattn_Wk, L1_xattn_bk, L1_xattn_Wv, L1_xattn_bv, L1_ffn_Wg, L1_ffn_W1, L1_ffn_W2, L1_ffn_W3):
    import jax
    import jax.numpy as jnp

    def _L0_xattn_ref(x, y, wq, bq, wk, bk, wv, bv, wo, bo):
        import jax, jax.numpy as jnp
        import numpy as np
        N_HEADS = 16
        DIM_EMBED = 128
        DIM_CROSS = 96
        DIM_HEAD = DIM_EMBED // N_HEADS
        B, Sq, E = x.shape
        H, D = (N_HEADS, DIM_HEAD)
        q = (x @ wq + bq).reshape(B, Sq, H, D).transpose(0, 2, 1, 3)
        k = (y @ wk + bk).reshape(B, -1, H, D).transpose(0, 2, 1, 3)
        v = (y @ wv + bv).reshape(B, -1, H, D).transpose(0, 2, 1, 3)
        scores = jnp.einsum('bhqd,bhkd->bhqk', q, k) / jnp.sqrt(jnp.asarray(D, x.dtype))
        attn = jax.nn.softmax(scores, axis=-1)
        out = jnp.einsum('bhqk,bhkd->bhqd', attn, v)
        out = out.transpose(0, 2, 1, 3).reshape(B, Sq, E)
        return out @ wo + bo

    def _L0_ffn_ref(x, proj_w, anchors, routing_temp, w1, w2):
        import jax, jax.numpy as jnp
        import numpy as np
        B, T, D_MODEL = (4, 256, 128)
        N_EXPERTS, TOP_K, D_EXPERT = (6, 2, 64)
        QUANT_TEMP = 0.3
        _ANCHOR_IDS = [63, 6, 0, 18, 45, 27]

        def _q6_idx_to_vertex(idx):
            bits = [idx >> 5 - b & 1 for b in range(6)]
            return [2.0 * b - 1.0 for b in bits]

        def _anchors():
            return jnp.asarray(np.array([_q6_idx_to_vertex(i) for i in _ANCHOR_IDS], dtype=np.float32))

        def _router(x, proj_w, anchors, routing_temp):
            z = jnp.einsum('btd,ed->bte', x, proj_w)
            q = jnp.tanh(z / QUANT_TEMP)
            dot = jnp.einsum('btd,ed->bte', q, anchors)
            hamming = (6.0 - dot) * 0.5
            logits = -hamming / jnp.clip(routing_temp, 0.1)
            topk_logits, topk_idx = jax.lax.top_k(logits, TOP_K)
            topk_w = jax.nn.softmax(topk_logits, axis=-1)
            onehot = jax.nn.one_hot(topk_idx, N_EXPERTS, dtype=x.dtype)
            expert_weights = jnp.einsum('btke,btk->bte', onehot, topk_w)
            return (expert_weights, q)
        expert_weights, q = _router(x, proj_w, anchors, routing_temp)
        h = jax.nn.gelu(jnp.einsum('btd,edh->bteh', x, w1))
        out = jnp.einsum('bteh,ehd,bte->btd', h, w2, expert_weights)
        return out

    def _L1_xattn_ref(image_features, text_features, Wq, bq, Wk, bk, Wv, bv):
        import jax, jax.numpy as jnp
        import numpy as np
        IMG_DIM, TXT_DIM, HID = (128, 96, 128)
        B, LQ, LK = (8, 256, 256)
        query = jnp.einsum('bqi,ih->bqh', image_features, Wq) + bq
        key = jnp.einsum('bkt,th->bkh', text_features, Wk) + bk
        value = jnp.einsum('bkt,th->bkh', text_features, Wv) + bv
        scale = 1.0 / jnp.sqrt(jnp.asarray(HID, query.dtype))
        scores = jnp.einsum('bqh,bkh->bqk', query, key) * scale
        weights = jax.nn.softmax(scores, axis=-1)
        attended = jnp.einsum('bqk,bkh->bqh', weights, value)
        return attended

    def _L1_ffn_ref(x, Wg, W1, W2, W3):
        import jax, jax.numpy as jnp
        import numpy as np
        E = 8
        TOP_K = 2
        D = 128
        H = 2 * D
        logits = jnp.einsum('bsd,de->bse', x, Wg)
        top_vals, top_idx = jax.lax.top_k(logits, TOP_K)
        probs = jax.nn.softmax(top_vals, axis=-1)
        onehot = jax.nn.one_hot(top_idx, E, dtype=x.dtype)
        weights = jnp.einsum('bsk,bske->bse', probs, onehot)
        out = jnp.zeros_like(x)
        for e in range(E):
            u = jnp.einsum('bsd,dh->bsh', x, W1[e])
            v = jnp.einsum('bsd,dh->bsh', x, W2[e])
            h = u * jax.nn.sigmoid(u) * v
            y = jnp.einsum('bsh,hd->bsd', h, W3[e])
            out = out + y * weights[..., e][..., None]
        return out
    x = x + jnp.tanh(g_xattn[0]) * _L0_xattn_ref(_layernorm(x, axis=-1), ctx_768, L0_xattn_wq, L0_xattn_bq, L0_xattn_wk, L0_xattn_bk, L0_xattn_wv, L0_xattn_bv, L0_xattn_wo, L0_xattn_bo)
    x = x + jnp.tanh(g_ffn[0]) * _L0_ffn_ref(_layernorm(x, axis=-1), L0_ffn_proj_w, L0_ffn_anchors, L0_ffn_routing_temp, L0_ffn_w1, L0_ffn_w2)
    x = x + jnp.tanh(g_xattn[1]) * _L1_xattn_ref(_layernorm(x, axis=-1), ctx_768, L1_xattn_Wq, L1_xattn_bq, L1_xattn_Wk, L1_xattn_bk, L1_xattn_Wv, L1_xattn_bv)
    x = x + jnp.tanh(g_ffn[1]) * _L1_ffn_ref(_layernorm(x, axis=-1), L1_ffn_Wg, L1_ffn_W1, L1_ffn_W2, L1_ffn_W3)
    return x

_drawn_inputs = setup_inputs


def setup_inputs(seed=0):
    import zlib

    import numpy as np

    out = dict(_drawn_inputs(seed))
    spreads = {'g_ffn': (-1.0, 0.6)}
    factors = {'L0_xattn_bq': 8.0,
     'L0_xattn_bk': 8.0,
     'L0_xattn_bv': 6.258,
     'L0_xattn_bo': 6.368,
     'L1_xattn_bq': 8.0,
     'L1_xattn_bk': 8.0,
     'L1_ffn_Wg': 8.0,
     'L1_ffn_W1': 8.0,
     'L1_ffn_W2': 8.0,
     'L1_ffn_W3': 8.0}
    for name, (base, spread) in spreads.items():
        noise = np.random.default_rng([zlib.crc32(name.encode()), seed]).standard_normal(out[name].shape)
        drawn = base * np.exp(spread * noise) if base else spread * noise
        out[name] = jnp.asarray(drawn.astype(out[name].dtype))
    for name, factor in factors.items():
        out[name] = (out[name] * factor).astype(out[name].dtype)
    return out
```

```python
from contextlib import ExitStack

import concourse.bass as bass
from concourse import mybir

ALU = mybir.AluOpType
ACT = mybir.ActivationFunctionType
F32 = mybir.dt.float32
BF16 = mybir.dt.bfloat16
AX_X = mybir.AxisListType.X

P = 128
B, S, D = 128, 64, 128
DC = 96
TILES = B * S // P
GT = 4
G = TILES // GT
GB = GT * P // S
GW = GT * P
H, DH = 16, 8
HU = H // 2
SETS = 2
REC = 64
STRIP = 32
E0, HID0 = 6, 64
C0 = E0 * HID0 // P
E1, HID1 = 8, 256
EPS = 1e-5
SCALE0 = float(DH) ** -0.5
SCALE1 = float(D) ** -0.5
QUANT_TEMP = 0.3
FAR = 1e30


def static(t):
    return isinstance(t, int)


def loop_steps(eng, first_static, looped, last, step):
    period = 2 * GT
    for t in range(first_static):
        step(t, t % period, t // GT)
    with eng.Fori(first_static // period, first_static // period + looped) as i:
        for u in range(period):
            step(i * period + u, u, i * 2 + u // GT)
    for t in range(first_static + looped * period, last):
        step(t, t % period, t // GT)


def wait_alone(eng, semaphore, value):
    eng.wait_ge(semaphore, value)
    eng.nop(nofuse=True)


def inverse_deviation(pool, stats, minus_half, rstd, rstd_step, g):
    pool.tensor_scalar(rstd, stats[:, :, 1], EPS, None, ALU.add).then_inc(rstd_step, 1)
    wait_alone(pool, rstd_step, 2 * g + 1)
    pool.tensor_tensor(rstd, rstd, minus_half, ALU.pow).then_inc(rstd_step, 1)


class Shared:
    pass


def load_constants(nc, sb, psum, sem, c, a):
    c.minus_half = sb("minus_half", [P, GT], F32)
    c.ident = sb("ident", [P, P], F32)
    c.ident_bf = sb("ident_bf", [P, P], BF16)
    c.head_of_group = sb("head_of_group", [P, 4], F32)
    c.head_cols_f = sb("head_cols_f", [2 * H, H * S], F32)
    c.head_cols = sb("head_cols", [2 * H, H * S], BF16)
    c.expert_cols_f = sb("expert_cols_f", [3 * E0, C0, P], F32)
    c.expert_cols = sb("expert_cols", [3 * E0, C0, P], BF16)
    c.early = sb("early", [P, E1], F32)
    c.gates_in = sb("gates_in", [P, 4], F32)
    c.gates = sb("gates", [P, 4], F32)
    c.wq0 = sb("wq0", [D, D], F32)
    c.wk0 = sb("wk0", [DC, D], F32)
    c.wv0 = sb("wv0", [DC, D], F32)
    c.wo0_in = sb("wo0_in", [D, D], F32)
    c.wo0 = sb("wo0", [D, D], F32)
    c.bq0 = sb("bq0", [P, 2], F32)
    c.bk0 = sb("bk0", [P, 2], F32)
    c.wo0_strips_in = sb("wo0_strips_in", [P, SETS, D], F32)
    c.wo0_strips = sb("wo0_strips", [P, SETS, D], F32)
    c.bv0 = sb("bv0", [D, 1], F32)
    c.bv0_wide = sb("bv0_wide", [D, P], F32)
    c.bo0_rows = sb("bo0_rows", [P, D], F32)
    c.bo0_gated = sb("bo0_gated", [P, D], F32)
    c.out_bias0 = sb("out_bias0", [P, D], F32)
    c.w_route0_in = sb("w_route0_in", [E0, D], F32)
    c.w_route0 = sb("w_route0", [D, E0], F32)
    c.anchors = sb("anchors", [P, E0, E0], F32)
    c.temp_in = sb("temp_in", [P, 1], F32)
    c.temp = sb("temp", [P, 1], F32)
    c.half_over_temp = sb("half_over_temp", [P, 2], F32)
    c.w1_0 = sb("w1_0", [D, E0, HID0], F32)
    c.w2_0_in = sb("w2_0_in", [P, C0, D], F32)
    c.w2_0 = sb("w2_0", [P, C0, D], F32)
    c.wq1 = sb("wq1", [D, D], F32)
    c.wk1 = sb("wk1", [DC, D], F32)
    c.wv1_in = sb("wv1_in", [DC, D], F32)
    c.wv1 = sb("wv1", [DC, D], F32)
    c.bq1 = sb("bq1", [D, 1], F32)
    c.bk1 = sb("bk1", [D, 1], F32)
    c.bv1_rows = sb("bv1_rows", [P, D], F32)
    c.out_bias1 = sb("out_bias1", [P, D], F32)
    c.w_route1 = sb("w_route1", [D, E1], F32)
    c.w12 = sb("w12", [D, E1, 2, HID1], F32)
    c.w3_in = sb("w3_in", [P, E1, HID1 // P, D], F32)
    c.w3 = sb("w3", [P, E1, HID1 // P, D], F32)
    c.v_heads = [sb(f"v_heads{i}", [P, GB, HU, STRIP], F32) for i in range(2)]
    c.q_blocks = [sb(f"q_blocks{i}", [P, GT, 4, 2, S], F32) for i in range(2)]
    c.parts = sb("parts", [P, REC + 3 * H], BF16)
    c.strip_rows_f = sb("strip_rows_f", [P, SETS, P], F32)
    c.strip_rows = sb("strip_rows", [P, SETS, P], BF16)
    c.probs1 = sb("probs1", [P, GT, P], F32)
    c.values1 = [sb(f"values1_{i}", [P, GT, D + 1], F32) for i in range(2)]

    bank = psum("constants_bank", [P, 512], F32)
    loads = sem("loads")
    tanh_done = sem("tanh_done")
    zeroed = sem("zeroed")
    gated = sem("gated")
    bias_mm = sem("bias_mm")
    bv_wide_done = sem("bv_wide_done")
    temp_step = sem("temp_step")

    def column(row):
        return row.rearrange("(p a) -> p a", a=1)

    def spread(ap, n):
        return ap.rearrange("(a n) -> a n", a=1).broadcast_to([P, n])

    plan = [
        (c.ident[:], a["const_ident"]), (c.head_of_group[:], a["const_head_of_group"]),
        (c.head_cols_f[:], a["const_head_cols"]),
        (c.strip_rows_f[REC:REC + 3 * H, :, :], a["const_strip_rows"].rearrange("h (t r) -> h t r", t=SETS)),
        (c.expert_cols_f[:], a["const_expert_cols"].rearrange("p (c n) -> p c n", c=C0)),
        (c.early[:], spread(a["const_early"], E1)),
        (c.gates_in[:, 0:2], spread(a["g_xattn"], 2)), (c.gates_in[:, 2:4], spread(a["g_ffn"], 2)),
        (c.wq0[:], a["L0_xattn_wq"]), (c.wk0[:], a["L0_xattn_wk"]), (c.wv0[:], a["L0_xattn_wv"]),
        (c.wo0_in[:], a["L0_xattn_wo"]),
        *[(dst[half:half + D // 2, :], a[name].rearrange("(h r) -> r h", h=2))
          for dst, name in ((c.bq0, "L0_xattn_bq"), (c.bk0, "L0_xattn_bk")) for half in (0, D // 2)],
        *[(c.wo0_strips_in[STRIP * k:STRIP * k + 2 * DH, :, :],
           a["L0_xattn_wo"].rearrange("(t k r) d -> k r t d", t=SETS, k=4)[k]) for k in range(4)],
        (c.bv0[:], column(a["L0_xattn_bv"])), (c.bo0_rows[:], spread(a["L0_xattn_bo"], D)),
        (c.w_route0_in[:], a["L0_ffn_proj_w"]),
        (c.anchors[:].rearrange("p e d -> p (e d)"), spread(a["L0_ffn_anchors"].rearrange("e d -> (e d)"), E0 * E0)),
        (c.temp_in[:], spread(a["L0_ffn_routing_temp"], 1)),
        (c.w1_0[:], a["L0_ffn_w1"].rearrange("e d h -> d e h")),
        (c.w2_0_in[:], a["L0_ffn_w2"].rearrange("(c a) h d -> (a h) c d", c=C0)),
        (c.wq1[:], a["L1_xattn_Wq"]), (c.wk1[:], a["L1_xattn_Wk"]), (c.wv1_in[:], a["L1_xattn_Wv"]),
        (c.bq1[:], column(a["L1_xattn_bq"])), (c.bk1[:], column(a["L1_xattn_bk"])),
        (c.bv1_rows[:], spread(a["L1_xattn_bv"], D)),
        (c.w_route1[:], a["L1_ffn_Wg"]),
        (c.w12[:, :, 0, :], a["L1_ffn_W1"].rearrange("e d h -> d e h")),
        (c.w12[:, :, 1, :], a["L1_ffn_W2"].rearrange("e d h -> d e h")),
        (c.w3_in[:], a["L1_ffn_W3"].rearrange("e (b h) d -> h e b d", h=P)),
    ]

    with nc.Block() as block:
        @block.sync
        def _(sp):
            sp.wait_ge(zeroed, 1)
            for n, (dst, src) in enumerate(plan):
                sp.dma_start(dst, src, allow_slow_non_contiguous=True).then_inc(loads, 16)
            sp.wait_ge(loads, 16 * len(plan))

        @block.gpsimd
        def _(pool):
            pool.memset(c.wo0_strips_in[:], 0.0).then_inc(zeroed, 1)
            pool.memset(c.parts[:], 0.0)
            for v in c.v_heads:
                pool.memset(v[:], 0.0)
            for q in c.q_blocks:
                pool.memset(q[:], 0.0)
            pool.memset(c.probs1[:].rearrange("p t k -> p (t k)"), 0.0)
            pool.memset(c.minus_half[:], -0.5)
            for v in c.values1:
                pool.memset(v[:, :, D:D + 1], 1.0)

        @block.scalar
        def _(act):
            act.wait_ge(loads, 16 * len(plan))
            act.activation(c.gates[:], c.gates_in[:], ACT.Tanh).then_inc(tanh_done, 1)

        @block.vector
        def _(dve):
            dve.wait_ge(loads, 16 * len(plan))
            dve.tensor_copy(c.bv0_wide[:], c.bv0[:, 0:1].broadcast_to([D, P])).then_inc(bv_wide_done, 1)
            dve.tensor_copy(c.head_cols[:], c.head_cols_f[:])
            dve.tensor_copy(c.strip_rows[REC:REC + 3 * H, :, :], c.strip_rows_f[REC:REC + 3 * H, :, :])
            dve.tensor_copy(c.expert_cols[:], c.expert_cols_f[:])
            dve.tensor_copy(c.ident_bf[:], c.ident[:])
            dve.tensor_scalar(c.temp[:], c.temp_in[:], 0.1, None, ALU.max).then_inc(temp_step, 1)
            dve.wait_ge(temp_step, 1)
            dve.reciprocal(c.half_over_temp[:, 0:1], c.temp[:]).then_inc(temp_step, 1)
            dve.wait_ge(temp_step, 2)
            dve.tensor_scalar(c.half_over_temp[:, 1:2], c.half_over_temp[:, 0:1], 0.5, None, ALU.mult)
            dve.wait_ge(tanh_done, 1)
            dve.tensor_scalar(c.wo0[:], c.wo0_in[:], c.gates[:, 0:1], None, ALU.mult).then_inc(gated, 1)
            dve.tensor_scalar(c.wo0_strips[:].rearrange("p t d -> p (t d)"),
                              c.wo0_strips_in[:].rearrange("p t d -> p (t d)"), c.gates[:, 0:1], None, ALU.mult)
            dve.tensor_scalar(c.bo0_gated[:], c.bo0_rows[:], c.gates[:, 0:1], None, ALU.mult).then_inc(gated, 1)
            dve.tensor_scalar(c.w2_0[:].rearrange("p c d -> p (c d)"), c.w2_0_in[:].rearrange("p c d -> p (c d)"),
                              c.gates[:, 2:3], None, ALU.mult)
            dve.tensor_scalar(c.w3[:].rearrange("p e b d -> p (e b d)"), c.w3_in[:].rearrange("p e b d -> p (e b d)"),
                              c.gates[:, 3:4], None, ALU.mult)
            dve.tensor_scalar(c.wv1[:], c.wv1_in[:], c.gates[0:DC, 1:2], None, ALU.mult)
            dve.tensor_scalar(c.out_bias1[:], c.bv1_rows[:], c.gates[:, 1:2], None, ALU.mult)
            dve.wait_ge(bias_mm, 2)
            dve.tensor_copy(c.w_route0[:], bank[:, 256:256 + E0])
            dve.wait_ge(gated, 2)
            dve.tensor_tensor(c.out_bias0[:], bank[:, 0:D], c.bo0_gated[:], ALU.add)

        @block.tensor
        def _(pe):
            pe.wait_ge(loads, 16 * len(plan))
            pe.transpose(bank[:, 256:256 + E0], c.w_route0_in[:], c.ident[0:E0, 0:E0]).then_inc(bias_mm, 1)
            pe.wait_ge(bv_wide_done, 1)
            pe.wait_ge(gated, 1)
            pe.matmul(bank[:, 0:D], c.bv0_wide[:], c.wo0[:], start=True, stop=True).then_inc(bias_mm, 1)


def attention_of_layer0(nc, sb, psum, sem, c, a, X):
    stats6 = sb("a_stats6", [P, GT, 6], F32)
    stats = sb("a_stats", [P, GT, 2], F32)
    rstd = sb("a_rstd", [P, GT], F32)
    xn = sb("a_xn", [P, GT, D], F32)
    xnT = sb("a_xnT", [D, GW], F32)
    ctx_in = [sb(f"a_ctx{i}", [P, GT, DC], F32) for i in range(2)]
    ctxT = sb("a_ctxT", [DC, GW], F32)
    kT = sb("a_kT", [P, 2, GT, S], F32)
    k_heads = [sb(f"a_k_heads{i}", [P, GT, 2, 4, S], F32) for i in range(2)]
    neg_max = sb("a_neg_max", [P, H], F32)
    parts = c.parts
    rows = sb("a_rows", [REC + 3 * H, P], BF16)
    probs = [sb(f"a_probs{i}", [P, H * S], F32) for i in range(2)]
    probsT = [sb(f"a_probsT{i}", [P, HU, P], F32) for i in range(2)]
    denom = sb("a_denom", [P, H], F32)
    rec = sb("a_rec", [P, H], F32)
    rec_rest = sb("a_rec_rest", [P, H], F32)
    heads_raw = sb("a_heads_raw", [P, SETS, P], F32)
    heads_outT = sb("a_heads_outT", [P, SETS, P], F32)

    scores = [psum(f"a_scores{i}", [P, 2, 512], F32) for i in range(2)]
    probsT_bank = psum("a_probsT_bank", [P, 512], F32)
    prep = psum("a_prep", [P, 512], F32)
    small = psum("a_small", [P, 512], F32)
    pv = psum("a_pv", [P, 2, SETS, P], F32)
    y = small[:, 0:D]
    rows_ps = small[0:REC + 3 * H, D:D + P // 2].bitcast(BF16)

    loaded = [sem(f"a_loaded{i}") for i in range(2)]
    bn_done, stats_done = sem("a_bn_done"), sem("a_stats_done")
    rstd_step, xn_ready, bias_added = sem("a_rstd_step"), sem("a_xn_ready"), sem("a_bias_added")
    prep_mm, prep_ev, v_odd_ev = sem("a_prep_mm"), sem("a_prep_ev"), sem("a_v_odd_ev")
    q_odd_ev, k_heads_ready = sem("a_q_odd_ev"), sem("a_k_heads")
    scores_mm, max_done, part1_done, parts_ready = sem("a_scores_mm"), sem("a_max"), sem("a_part1"), sem("a_parts")
    sum_done, rec_done, rec1_done = sem("a_sum"), sem("a_rec_done"), sem("a_rec1")
    rest_done, rec2_done, raw_ready = sem("a_rest"), sem("a_rec2"), sem("a_raw_ready")
    rows_mm, rows_ready, sub_mm, exp_done = sem("a_rows_mm"), sem("a_rows_ready"), sem("a_sub_mm"), sem("a_exp")
    pT_mm, pT_ev = sem("a_pT_mm"), sem("a_pT_ev")
    pv_mm, spread_mm, o_ready = sem("a_pv_mm"), sem("a_spread_mm"), sem("a_o_ready")
    y_mm, x_updated = sem("a_y_mm"), sem("a_x_updated")
    PREP = 5
    PREP_AT = ((0, 1), (2,), (3,), (4,))
    LAST = TILES + 4

    def tile_now(t, lag):
        return None if static(t) and not 0 <= t - lag < TILES else t - lag

    def group_at(g0, more):
        return None if static(g0) and g0 + more >= G else g0 + more

    with nc.Block() as block:
        @block.sync
        def _(sp):
            def load(g, par):
                if not static(g) or g >= 2:
                    sp.wait_ge(prep_mm, PREP * (g - 2) + 2)
                sp.dma_start(X[:, bass.ts(g, GT), :],
                             a["x"].rearrange("(t b) s d -> (b s) t d", b=2)[:, bass.ts(g, GT), :]).then_inc(loaded[par], 16)
                sp.dma_start(ctx_in[par][:],
                             a["ctx_768"].rearrange("(t b) s d -> (b s) t d", b=2)[:, bass.ts(g, GT), :]).then_inc(loaded[par], 16)

            load(0, 0)
            load(1, 1)
            with sp.Fori(1, G // 2) as i:
                load(i * 2, 0)
                load(i * 2 + 1, 1)

        @block.vector
        def _(dve):
            def layer_stats(g, par):
                dve.wait_ge(loaded[par], 32 * ((g - par) // 2) + 32)
                if not static(g) or g >= 1:
                    dve.wait_ge(xn_ready, g)
                for j in range(GT):
                    last = dve.bn_stats(stats6[:, j, :], X[:, g * GT + j, :])
                last.then_inc(bn_done, 1)
                wait_alone(dve, bn_done, g + 1)
                for j in range(GT):
                    last = dve.bn_aggr(stats[:, j, :], stats6[:, j, :])
                last.then_inc(stats_done, 1)

            def layer_norm(g):
                dve.wait_ge(rstd_step, 2 * g + 2)
                if not static(g) or g >= 1:
                    dve.wait_ge(prep_mm, PREP * (g - 1) + 1)
                for j in range(GT):
                    last = dve.tensor_scalar(xn[:, j, :], X[:, g * GT + j, :], stats[:, j, 0:1], rstd[:, j:j + 1],
                                             ALU.subtract, ALU.mult)
                last.then_inc(xn_ready, 1)

            def q_odd(g, par):
                dve.wait_ge(prep_mm, PREP * g + 4)
                if not static(g) or g >= 2:
                    dve.wait_ge(scores_mm, GT * (g - 1))
                for h in range(2):
                    for s in range(2):
                        rows_in = slice(64 + 32 * s, 96 + 32 * s)
                        last = dve.tensor_scalar(c.q_blocks[par][rows_in, :, 2 * h + s, 1, :],
                                                 prep[rows_in, bass.ts(h, GW // 2)].rearrange("p (t q) -> p t q", q=S),
                                                 c.bq0[rows_in, h:h + 1], None, ALU.add)
                last.then_inc(q_odd_ev, 1)

            def v_odd(g, par):
                dve.wait_ge(prep_mm, PREP * g + 5)
                if not static(g) or g >= 2:
                    dve.wait_ge(pv_mm, GT * (g - 1))
                dve.tensor_copy(c.v_heads[par][S:P, :, :, DH:2 * DH].rearrange("p b u w -> p (b u) w"),
                                prep[S:P, :].rearrange("p (b u w) -> p (b u) w", b=GB, u=HU)).then_inc(v_odd_ev, 1)

            def step(t, u, g0):
                n, m = tile_now(t, 0), tile_now(t, 2)
                if n is not None:
                    dve.wait_ge(scores_mm, n + 1)
                    dve.tensor_reduce(neg_max[:], scores[u % 2][:].rearrange("p a (h k) -> p (a h) k", k=S), AX_X,
                                      ALU.max, negate=True).then_inc(max_done, 1)
                w = tile_now(t, 4)
                if w is not None:
                    if u % GT == 0:
                        dve.wait_ge(bias_added, g0)
                    dve.wait_ge(y_mm, w + 1)
                    dve.tensor_tensor(X[:, w, :], y, X[:, w, :], ALU.add).then_inc(x_updated, 1)
                if m is not None:
                    dve.wait_ge(exp_done, m + 1)
                    dve.reduce_sum(denom[:], probs[u % 2][:].rearrange("p (h k) -> p h k", k=S), AX_X).then_inc(sum_done, 1)
                if (n is not None or m is not None) and (not static(t) or t >= 1):
                    dve.wait_ge(rows_mm, t)
                if n is not None:
                    dve.wait_ge(max_done, n + 1)
                    dve.tensor_copy(parts[:, 0:H], neg_max[:]).then_inc(part1_done, 1)
                if m is not None:
                    dve.wait_ge(sum_done, m + 1)
                    dve.reciprocal(rec[:], denom[:]).then_inc(rec_done, 1)
                if n is not None:
                    dve.wait_ge(part1_done, n + 1)
                    last = dve.tensor_tensor(parts[:, H:2 * H], neg_max[:], parts[:, 0:H], ALU.subtract)
                if m is not None:
                    dve.wait_ge(rec_done, m + 1)
                    dve.tensor_copy(parts[:, REC:REC + H], rec[:]).then_inc(rec1_done, 1)
                if m is not None:
                    dve.wait_ge(rec1_done, m + 1)
                    dve.tensor_tensor(rec_rest[:], rec[:], parts[:, REC:REC + H], ALU.subtract).then_inc(rest_done, 1)
                    dve.wait_ge(rest_done, m + 1)
                    dve.tensor_copy(parts[:, REC + H:REC + 2 * H], rec_rest[:]).then_inc(rec2_done, 1)
                    dve.wait_ge(rec2_done, m + 1)
                    last = dve.tensor_tensor(parts[:, REC + 2 * H:REC + 3 * H], rec_rest[:], parts[:, REC + H:REC + 2 * H],
                                             ALU.subtract)
                if n is not None or m is not None:
                    last.then_inc(parts_ready, 1)
                n = tile_now(t, 3)
                if n is not None:
                    dve.wait_ge(spread_mm, n + 1)
                    dve.wait_ge(raw_ready, n + 1)
                    if not static(n) or n >= 1:
                        dve.wait_ge(y_mm, n)
                    dve.tensor_tensor(heads_outT[:], heads_raw[:], pv[:, 1], ALU.mult).then_inc(o_ready, 1)
                if u % GT == 0:
                    g = group_at(g0, 2)
                    if g is not None:
                        layer_stats(g, (u // GT) % 2)
                if u % GT == 1:
                    g = group_at(g0, 2)
                    if g is not None:
                        layer_norm(g)
                if u % GT == 2:
                    g = group_at(g0, 1)
                    if g is not None:
                        q_odd(g, (u // GT + 1) % 2)
                if u % GT == 3:
                    g = group_at(g0, 1)
                    if g is not None:
                        v_odd(g, (u // GT + 1) % 2)

            layer_stats(0, 0)
            layer_norm(0)
            layer_stats(1, 1)
            q_odd(0, 0)
            v_odd(0, 0)
            layer_norm(1)
            loop_steps(dve, 2 * GT, TILES // (2 * GT) - 2, LAST, step)

        @block.gpsimd
        def _(pool):
            def deviation(g):
                wait_alone(pool, stats_done, g + 1)
                inverse_deviation(pool, stats[:], c.minus_half[:], rstd[:], rstd_step, g)

            def add_bias(g):
                wait_alone(pool, xn_ready, g + 1)
                pool.tensor_tensor(X[:, bass.ts(g, GT), :], X[:, bass.ts(g, GT), :],
                                   c.out_bias0[:].unsqueeze(1).broadcast_to([P, GT, D]), ALU.add).then_inc(bias_added, 1)

            def spread_k(g, par):
                wait_alone(pool, prep_ev, PREP * g + 3)
                if not static(g) or g >= 2:
                    wait_alone(pool, scores_mm, GT * (g - 1))
                for j in range(4):
                    last = pool.tensor_scalar(k_heads[par][:, :, :, j, :].rearrange("p t h k -> p h t k"), kT[:],
                                              c.head_of_group[:, j:j + 1], None, ALU.mult)
                last.then_inc(k_heads_ready, 1)

            def step(t, u, g0):
                if u % GT == 0:
                    g = group_at(g0, 2)
                    if g is not None:
                        deviation(g)
                if u % GT == 1:
                    g = group_at(g0, 1)
                    if g is not None:
                        spread_k(g, (u // GT + 1) % 2)
                    g = group_at(g0, 2)
                    if g is not None:
                        add_bias(g)

            deviation(0)
            add_bias(0)
            deviation(1)
            spread_k(0, 0)
            add_bias(1)
            loop_steps(pool, 2 * GT, TILES // (2 * GT) - 2, LAST, step)

        @block.scalar
        def _(act):
            def evacuate(g, par, k):
                act.wait_ge(prep_mm, PREP * g + k + 1)
                if k == 0:
                    act.copy(xnT[:], prep[:]).then_inc(prep_ev, 1)
                elif k == 1:
                    act.copy(ctxT[:], prep[0:DC, :]).then_inc(prep_ev, 1)
                elif k == 2:
                    if not static(g) or g >= 1:
                        act.wait_ge(k_heads_ready, g)
                    for h in range(2):
                        last = act.activation(kT[:, h], prep[:, bass.ts(h, GW // 2)], ACT.Identity,
                                              bias=c.bk0[:, h:h + 1])
                    last.then_inc(prep_ev, 1)
                elif k == 3:
                    if not static(g) or g >= 2:
                        act.wait_ge(scores_mm, GT * (g - 1))
                    for h in range(2):
                        for s in range(2):
                            rows_in = slice(32 * s, 32 * s + 32)
                            last = act.activation(c.q_blocks[par][rows_in, :, 2 * h + s, 0, :],
                                                  prep[rows_in, bass.ts(h, GW // 2)].rearrange("p (t q) -> p t q", q=S),
                                                  ACT.Identity, bias=c.bq0[rows_in, h:h + 1])
                    last.then_inc(prep_ev, 1)
                else:
                    if not static(g) or g >= 2:
                        act.wait_ge(pv_mm, GT * (g - 1))
                    act.copy(c.v_heads[par][0:S, :, :, 0:DH].rearrange("p b u w -> p (b u) w"),
                             prep[0:S, :].rearrange("p (b u w) -> p (b u) w", b=GB, u=HU)).then_inc(prep_ev, 1)

            def step(t, u, g0):
                n = tile_now(t, 1)
                if n is not None:
                    act.wait_ge(sub_mm, n + 1)
                    if not static(n) or n >= 2:
                        act.wait_ge(pT_mm, 2 * n - 2)
                    act.activation(probs[(u + 1) % 2][:], scores[(u + 1) % 2][:].rearrange("p a n -> p (a n)"), ACT.Exp,
                                   scale=SCALE0).then_inc(exp_done, 1)
                def keep_transposed(n, half):
                    act.wait_ge(pT_mm, 2 * n + 1 + half)
                    if half == 0 and (not static(n) or n >= 2):
                        act.wait_ge(pv_mm, n - 1)
                    act.copy(probsT[u % 2][:, half * HU // 2:(half + 1) * HU // 2, :].rearrange("p u q -> p (u q)"),
                             probsT_bank[:]).then_inc(pT_ev, 1)

                if tile_now(t, 2) is not None:
                    keep_transposed(t - 2, 0)
                n = tile_now(t, 3)
                if n is not None:
                    act.wait_ge(pv_mm, n + 1)
                    if not static(n) or n >= 1:
                        act.wait_ge(o_ready, n)
                    act.copy(heads_raw[:].rearrange("p t q -> p (t q)"), pv[:, 0].rearrange("p t q -> p (t q)")).then_inc(raw_ready, 1)
                if tile_now(t, 2) is not None:
                    keep_transposed(t - 2, 1)
                g = group_at(g0, 1)
                if g is not None:
                    for k in PREP_AT[u % GT]:
                        evacuate(g, (u // GT + 1) % 2, k)
                if not static(t) or t < TILES + 2:
                    act.wait_ge(rows_mm, t + 1)
                    if not static(t) or t >= 1:
                        if tile_now(t, 1) is not None:
                            act.wait_ge(sub_mm, t)
                        if tile_now(t, 3) is not None:
                            act.wait_ge(spread_mm, t - 2)
                    act.copy(rows[:], rows_ps).then_inc(rows_ready, 1)

            for k in range(PREP):
                evacuate(0, 0, k)
            loop_steps(act, 2 * GT, TILES // (2 * GT) - 2, LAST, step)

        @block.tensor
        def _(pe):
            def prepare(g, par, k):
                if k == 0:
                    if not static(g) or g >= 1:
                        pe.wait_ge(prep_ev, PREP * g)
                        pe.wait_ge(v_odd_ev, g)
                    pe.wait_ge(xn_ready, g + 1)
                    for j in range(GT):
                        last = pe.transpose(prep[:, bass.ts(j, P)], xn[:, j, :], c.ident[:])
                else:
                    pe.wait_ge(prep_ev, PREP * g + k)
                if k == 1:
                    pe.wait_ge(loaded[par], 32 * ((g - par) // 2) + 32)
                    for j in range(GT):
                        last = pe.transpose(prep[0:DC, bass.ts(j, P)], ctx_in[par][:, j, :], c.ident[:])
                if k in (2, 3):
                    w, src = ((c.wk0, ctxT), (c.wq0, xnT))[k - 2]
                    for h in range(2):
                        for odd in range(2):
                            last = pe.matmul(prep[S * odd:S * odd + S, bass.ts(h, GW // 2)], w[:, bass.ts(h, D // 2)],
                                             src[:].rearrange("p (t b q) -> p b t q", b=2, q=S)[:, odd],
                                             start=True, stop=True)
                if k == 4:
                    pe.wait_ge(q_odd_ev, g + 1)
                    for b in range(GB):
                        for odd in range(2):
                            last = pe.matmul(prep[S * odd:S * odd + S, bass.ts(b, D // 2)], ctxT[:, bass.ts(b, S)],
                                             c.wv0[:].rearrange("p (u h w) -> p h u w", h=2, w=DH)[:, odd],
                                             start=True, stop=True)
                last.then_inc(prep_mm, 1)

            def step(t, u, g0):
                n = tile_now(t, 0)
                if n is not None:
                    if u % GT == 0:
                        pe.wait_ge(prep_ev, PREP * g0 + 4)
                        pe.wait_ge(q_odd_ev, g0 + 1)
                        pe.wait_ge(k_heads_ready, g0 + 1)
                    if not static(n) or n >= 2:
                        pe.wait_ge(exp_done, n - 1)
                    par, tile = (u // GT) % 2, u % GT
                    for k in range(4):
                        last = pe.matmul(scores[u % 2][:, k // 2, bass.ts(k % 2, 4 * S)],
                                         c.q_blocks[par][:, tile, k].rearrange("p b q -> p (b q)"),
                                         k_heads[par][:, tile, k // 2].rearrange("p j k -> p (j k)"),
                                         start=(k % 2 == 0), stop=True, skip_group_check=True)
                    last.then_inc(scores_mm, 1)
                n = tile_now(t, 1)
                if n is not None:
                    pe.wait_ge(rows_ready, n + 1)
                    for half in range(2):
                        last = pe.matmul(scores[(u + 1) % 2][:, half, :], rows[0:2 * H, :], c.head_cols[:, bass.ts(half, 512)],
                                         start=False, stop=True, skip_group_check=True)
                    last.then_inc(sub_mm, 1)
                n = tile_now(t, 4)
                if n is not None:
                    pe.wait_ge(o_ready, n + 1)
                    pe.wait_ge(rows_ready, min(t, TILES + 2) if static(t) else t)
                    if not static(n) or n >= 1:
                        pe.wait_ge(x_updated, n)
                    for k in range(SETS):
                        last = pe.matmul(y, heads_outT[:, k, :], c.wo0_strips[:, k, :], start=(k == 0),
                                         stop=(k == SETS - 1))
                    last.then_inc(y_mm, 1)
                def transpose_probs(half):
                    for k in range(HU // 2):
                        last = pe.transpose(probsT_bank[:, bass.ts(k, P)],
                                            probs[u % 2][:, bass.ts(half * HU // 2 + k, P)], c.ident[:])
                    last.then_inc(pT_mm, 1)

                n = tile_now(t, 2)
                if n is not None:
                    pe.wait_ge(exp_done, n + 1)
                    if not static(n) or n >= 1:
                        pe.wait_ge(pT_ev, 2 * n)
                    transpose_probs(0)
                n = tile_now(t, 3)
                if n is not None:
                    pe.wait_ge(rows_ready, n + 3)
                    if not static(n) or n >= 1:
                        pe.wait_ge(o_ready, n)
                    for k in range(SETS):
                        last = pe.matmul(pv[:, 1, k, :], c.strip_rows[REC:REC + 3 * H, k, :], rows[REC:REC + 3 * H, :],
                                         start=True, stop=True)
                    last.then_inc(spread_mm, 1)
                    pe.wait_ge(pT_ev, 2 * n + 2)
                    v_par = ((u + 5) % 8 // GT) % 2
                    if (u + 5) % GT == 0:
                        g = g0 + (u % GT - 3) // GT
                        pe.wait_ge(prep_ev, PREP * g + 5)
                        pe.wait_ge(v_odd_ev, g + 1)
                    for k in range(HU):
                        strip = slice(STRIP * (k % 4), STRIP * (k % 4) + STRIP)
                        for b in range(2):
                            batch = 2 * ((u + 5) % GT) + b
                            last = pe.matmul(pv[strip, 0, k // 4, bass.ts(b, S)], c.v_heads[v_par][:, batch, k, :],
                                             probsT[(u + 1) % 2][:, k, bass.ts(b, S)], start=True, stop=True)
                    last.then_inc(pv_mm, 1)
                n = tile_now(t, 2)
                if n is not None:
                    pe.wait_ge(pT_ev, 2 * n + 1)
                    transpose_probs(1)
                g = group_at(g0, 1)
                if g is not None:
                    for k in PREP_AT[u % GT]:
                        prepare(g, (u // GT + 1) % 2, k)
                if not static(t) or t < TILES + 2:
                    pe.wait_ge(parts_ready, t + 1)
                    if not static(t) or t >= 1:
                        pe.wait_ge(rows_ready, t)
                    if tile_now(t, 4) is not None:
                        pe.wait_ge(x_updated, t - 3)
                    pe.transpose(rows_ps, parts[:], c.ident_bf[:]).then_inc(rows_mm, 1)

            for k in range(PREP):
                prepare(0, 0, k)
            loop_steps(pe, 2 * GT, TILES // (2 * GT) - 2, LAST, step)


def group_steps(eng, lag, step):
    first = -(-lag // 2)
    for g in range(2 * first):
        step(g, g % 2)
    with eng.Fori(first, G // 2 - 1) as i:
        step(i * 2, 0)
        step(i * 2 + 1, 1)
    for g in range(G - 2, G + lag):
        step(g, g % 2)


def group_now(g, lag):
    return None if static(g) and not 0 <= g - lag < G else g - lag


class LayerNorm:

    def __init__(self, name, sb, sem, c, X):
        self.c, self.X = c, X
        self.stats6 = sb(f"{name}_stats6", [P, GT, 6], F32)
        self.stats = sb(f"{name}_stats", [P, GT, 2], F32)
        self.rstd = sb(f"{name}_rstd", [P, GT], F32)
        self.xn = sb(f"{name}_xn", [P, GT, D], F32)
        self.bn_done, self.stats_done = sem(f"{name}_bn_done"), sem(f"{name}_stats_done")
        self.rstd_step, self.xn_ready = sem(f"{name}_rstd_step"), sem(f"{name}_xn_ready")

    def statistics(self, dve, g):
        if not static(g) or g >= 1:
            wait_alone(dve, self.xn_ready, g)
        for j in range(GT):
            last = dve.bn_stats(self.stats6[:, j, :], self.X[:, g * GT + j, :])
        last.then_inc(self.bn_done, 1)
        wait_alone(dve, self.bn_done, g + 1)
        for j in range(GT):
            last = dve.bn_aggr(self.stats[:, j, :], self.stats6[:, j, :])
        last.then_inc(self.stats_done, 1)

    def deviation(self, pool, g):
        wait_alone(pool, self.stats_done, g + 1)
        inverse_deviation(pool, self.stats[:], self.c.minus_half[:], self.rstd[:], self.rstd_step, g)

    def rows(self, dve, g, transposed):
        dve.wait_ge(self.rstd_step, 2 * g + 2)
        if not static(g) or g >= 1:
            dve.wait_ge(transposed, g)
        for j in range(GT):
            last = dve.tensor_scalar(self.xn[:, j, :], self.X[:, g * GT + j, :], self.stats[:, j, 0:1],
                                     self.rstd[:, j:j + 1], ALU.subtract, ALU.mult)
        last.then_inc(self.xn_ready, 1)


class TopTwo:

    OPS = 16

    def __init__(self, name, sb, sem, c, experts):
        self.e, self.c = experts, c
        self.logits = sb(f"{name}_logits", [P, GT, experts], F32)
        self.work = sb(f"{name}_work", [P, GT, experts], F32)
        self.rest = sb(f"{name}_rest", [P, GT, experts], F32)
        self.first = sb(f"{name}_first", [P, GT, experts], F32)
        self.second = sb(f"{name}_second", [P, GT, experts], F32)
        self.m1, self.m2 = sb(f"{name}_m1", [P, GT], F32), sb(f"{name}_m2", [P, GT], F32)
        self.rank = sb(f"{name}_rank", [P, GT], F32)
        self.gap = sb(f"{name}_gap", [P, GT], F32)
        self.tanh = sb(f"{name}_tanh", [P, GT], F32)
        self.p1, self.p2 = sb(f"{name}_p1", [P, GT], F32), sb(f"{name}_p2", [P, GT], F32)
        self.weights = sb(f"{name}_weights", [P, GT, experts], F32)
        self.op_done = sem(f"{name}_op_done")
        self.gap_ready, self.tanh_ready = sem(f"{name}_gap_ready"), sem(f"{name}_tanh_ready")

    def wide(self, column):
        return column[:].unsqueeze(2).broadcast_to([P, GT, self.e])

    def choose(self, dve, g, count):
        early = self.c.early[:, E1 - self.e:E1].unsqueeze(1).broadcast_to([P, GT, self.e])

        def then(ins):
            ins.then_inc(self.op_done, 1)
            count[0] += 1
            dve.wait_ge(self.op_done, self.OPS * g + count[0])

        def one_hot(out, values, m):
            then(dve.tensor_reduce(m[:], values[:], AX_X, ALU.max))
            then(dve.tensor_tensor(self.work[:], values[:], self.wide(m), ALU.is_ge))
            then(dve.tensor_tensor(self.work[:], self.work[:], early, ALU.mult))
            then(dve.tensor_reduce(self.rank[:], self.work[:], AX_X, ALU.max))
            then(dve.tensor_tensor(out[:], self.work[:], self.wide(self.rank), ALU.is_equal))

        one_hot(self.first, self.logits, self.m1)
        then(dve.scalar_tensor_tensor(out=self.rest[:], in0=self.first[:], scalar=-FAR, in1=self.logits[:],
                                      op0=ALU.mult, op1=ALU.add))
        one_hot(self.second, self.rest, self.m2)
        dve.tensor_tensor(self.gap[:], self.m1[:], self.m2[:], ALU.subtract).then_inc(self.gap_ready, 1)

    def gap_tanh(self, act, g):
        act.wait_ge(self.gap_ready, g + 1)
        act.activation(self.tanh[:], self.gap[:], ACT.Tanh, scale=0.5).then_inc(self.tanh_ready, 1)

    def shares(self, dve, g):
        dve.wait_ge(self.tanh_ready, g + 1)
        dve.tensor_scalar(self.p1[:], self.tanh[:], 0.5, 0.5, ALU.mult, ALU.add).then_inc(self.op_done, 1)
        dve.tensor_scalar(self.p2[:], self.tanh[:], -0.5, 0.5, ALU.mult, ALU.add).then_inc(self.op_done, 1)

    def weigh(self, dve, g):
        dve.wait_ge(self.op_done, self.OPS * g + 13)
        dve.tensor_tensor(self.first[:], self.first[:], self.wide(self.p1), ALU.mult).then_inc(self.op_done, 1)
        dve.tensor_tensor(self.second[:], self.second[:], self.wide(self.p2), ALU.mult).then_inc(self.op_done, 1)
        dve.wait_ge(self.op_done, self.OPS * g + 15)
        dve.tensor_tensor(self.weights[:], self.first[:], self.second[:], ALU.add).then_inc(self.op_done, 1)


def mixture_of_layer0(nc, sb, psum, sem, c, X):
    ln = LayerNorm("b", sb, sem, c, X)
    top = TopTwo("b", sb, sem, c, E0)
    xnT = sb("b_xnT", [D, GW], F32)
    q = sb("b_q", [P, GT, E0], F32)
    q_anchor = sb("b_q_anchor", [P, GT, E0, E0], F32)
    dot = sb("b_dot", [P, GT, E0], F32)
    w_rest = sb("b_w_rest", [P, GT, E0], F32)
    w_parts = sb("b_w_parts", [P, GT, 3, E0], BF16)
    w_rows = sb("b_w_rows", [3 * E0, GW], BF16)
    hidden = [sb(f"b_hidden{i}", [P, C0, GW], F32) for i in range(2)]
    weighted = [sb(f"b_weighted{i}", [P, C0, GW], F32) for i in range(2)]

    tr, z, w_bank, y = (psum(f"b_{n}_bank", [P, 512], F32) for n in ("tr", "z", "w", "y"))
    h_bank = [psum(f"b_h{i}", [P, 512], F32) for i in range(2)]
    spread = [psum(f"b_spread{i}", [P, 512], F32) for i in range(2)]
    w_rows_ps = w_bank[0:3 * E0, 0:GW // 2].bitcast(BF16)

    xn_transposed, xT_ready = sem("b_xn_transposed"), sem("b_xT_ready")
    z_mm, q_ready, dot_step, parts_step = sem("b_z_mm"), sem("b_q_ready"), sem("b_dot_step"), sem("b_parts_step")
    w_mm, w_ready, h_mm, gelu_done = sem("b_w_mm"), sem("b_w_ready"), sem("b_h_mm"), sem("b_gelu_done")
    spread_mm, weighted_ready, y_mm, x_updated = sem("b_spread_mm"), sem("b_weighted"), sem("b_y_mm"), sem("b_x_updated")
    LAG = 3

    with nc.Block() as block:
        @block.gpsimd
        def _(pool):
            def step(g, par):
                n = group_now(g, -2)
                if n is not None:
                    ln.deviation(pool, n)

            ln.deviation(pool, 0)
            ln.deviation(pool, 1)
            group_steps(pool, LAG, step)

        @block.vector
        def _(dve):
            def route(n):
                dve.wait_ge(q_ready, n + 1)
                dve.tensor_tensor(q_anchor[:], q[:].unsqueeze(2).broadcast_to([P, GT, E0, E0]),
                                  c.anchors[:].unsqueeze(1).broadcast_to([P, GT, E0, E0]), ALU.mult).then_inc(dot_step, 1)
                dve.wait_ge(dot_step, 3 * n + 1)
                dve.reduce_sum(dot[:], q_anchor[:], AX_X).then_inc(dot_step, 1)
                dve.wait_ge(dot_step, 3 * n + 2)
                dve.tensor_scalar(top.logits[:], dot[:], float(E0), c.half_over_temp[:, 1:2], ALU.subtract,
                                  ALU.mult).then_inc(dot_step, 1)
                dve.wait_ge(dot_step, 3 * n + 3)
                top.choose(dve, n, [0])

            def split(n):
                dve.wait_ge(top.op_done, top.OPS * n + 16)
                if not static(n) or n >= 1:
                    dve.wait_ge(w_mm, n)
                dve.tensor_copy(w_parts[:, :, 0, :], top.weights[:]).then_inc(parts_step, 1)
                dve.wait_ge(parts_step, 4 * n + 1)
                dve.tensor_tensor(w_rest[:], top.weights[:], w_parts[:, :, 0, :], ALU.subtract).then_inc(parts_step, 1)
                dve.wait_ge(parts_step, 4 * n + 2)
                dve.tensor_copy(w_parts[:, :, 1, :], w_rest[:]).then_inc(parts_step, 1)
                dve.wait_ge(parts_step, 4 * n + 3)
                dve.tensor_tensor(w_parts[:, :, 2, :], w_rest[:], w_parts[:, :, 1, :],
                                  ALU.subtract).then_inc(parts_step, 1)

            def step(g, par):
                n = group_now(g, -1)
                if n is not None:
                    ln.rows(dve, n, xn_transposed)
                n = group_now(g, 1)
                if n is not None:
                    route(n)
                n = group_now(g, 2)
                if n is not None:
                    for k in range(C0):
                        dve.wait_ge(spread_mm, C0 * n + k + 1)
                        dve.wait_ge(gelu_done, C0 * n + k + 1)
                        if k == 0 and (not static(n) or n >= 2):
                            dve.wait_ge(y_mm, n - 1)
                        dve.tensor_tensor(weighted[par][:, k, :], hidden[par][:, k, :], spread[(C0 * par + k) % 2][:],
                                          ALU.mult).then_inc(weighted_ready, 1)
                n = group_now(g, 1)
                if n is not None:
                    top.shares(dve, n)
                    top.weigh(dve, n)
                    split(n)
                n = group_now(g, -2)
                if n is not None:
                    ln.statistics(dve, n)
                n = group_now(g, 3)
                if n is not None:
                    dve.wait_ge(y_mm, n + 1)
                    dve.tensor_tensor(X[:, bass.ts(n, GT), :], y[:].rearrange("p (t d) -> p t d", t=GT),
                                      X[:, bass.ts(n, GT), :], ALU.add).then_inc(x_updated, 1)

            ln.statistics(dve, 0)
            ln.rows(dve, 0, xn_transposed)
            ln.statistics(dve, 1)
            group_steps(dve, LAG, step)

        @block.scalar
        def _(act):
            def step(g, par):
                n = group_now(g, 2)
                if n is not None:
                    act.wait_ge(w_mm, n + 1)
                    if not static(n) or n >= 1:
                        act.wait_ge(spread_mm, C0 * n)
                    act.copy(w_rows[:], w_rows_ps).then_inc(w_ready, 1)
                n = group_now(g, 1)
                if n is not None:
                    act.wait_ge(z_mm, n + 1)
                    if not static(n) or n >= 1:
                        act.wait_ge(dot_step, 3 * n)
                    act.activation(q[:].rearrange("p t e -> p (t e)"), z[:, 0:GT * E0], ACT.Tanh,
                                   scale=1.0 / QUANT_TEMP).then_inc(q_ready, 1)
                    for k in range(C0):
                        act.wait_ge(h_mm, C0 * n + k + 1)
                        if k == 0 and (not static(n) or n >= 2):
                            act.wait_ge(weighted_ready, C0 * (n - 1))
                        act.activation(hidden[1 - par][:, k, :], h_bank[(C0 * (1 - par) + k) % 2][:],
                                       ACT.Gelu_apprx_tanh).then_inc(gelu_done, 1)
                    top.gap_tanh(act, n)
                n = group_now(g, 0)
                if n is not None:
                    act.wait_ge(xn_transposed, n + 1)
                    if not static(n) or n >= 1:
                        act.wait_ge(h_mm, C0 * n)
                    act.copy(xnT[:], tr[:]).then_inc(xT_ready, 1)

            group_steps(act, LAG, step)

        @block.tensor
        def _(pe):
            def spread_weights(n, par, k):
                if C0 * par + k >= 2 or not static(n) or n >= 2:
                    pe.wait_ge(weighted_ready, C0 * n + k - 1)
                pe.matmul(spread[(C0 * par + k) % 2][:], c.expert_cols[:, k, :], w_rows[:],
                          start=True, stop=True).then_inc(spread_mm, 1)

            def step(g, par):
                n = group_now(g, 0)
                if n is not None:
                    pe.wait_ge(ln.xn_ready, n + 1)
                    if not static(n) or n >= 1:
                        pe.wait_ge(xT_ready, n)
                    for j in range(GT):
                        last = pe.transpose(tr[:, bass.ts(j, P)], ln.xn[:, j, :], c.ident[:])
                    last.then_inc(xn_transposed, 1)
                n = group_now(g, 2)
                if n is not None:
                    pe.wait_ge(parts_step, 4 * n + 4)
                    if not static(n) or n >= 1:
                        pe.wait_ge(w_ready, n)
                    for j in range(GT):
                        last = pe.transpose(w_rows_ps[:, bass.ts(j, P)], w_parts[:, j].rearrange("p a e -> p (a e)"),
                                            c.ident_bf[:])
                    last.then_inc(w_mm, 1)
                n = group_now(g, 1)
                if n is not None:
                    pe.wait_ge(xT_ready, n + 1)
                    if not static(n) or n >= 1:
                        pe.wait_ge(q_ready, n)
                    for j in range(GT):
                        last = pe.matmul(z[:, bass.ts(j, E0)], xnT[:, bass.ts(j, P)], c.w_route0[:], start=True, stop=True)
                    last.then_inc(z_mm, 1)
                    for k in range(C0):
                        if C0 * (1 - par) + k >= 2 or not static(n) or n >= 2:
                            pe.wait_ge(gelu_done, C0 * n + k - 1)
                        pe.matmul(h_bank[(C0 * (1 - par) + k) % 2][:], c.w1_0[:, 2 * k:2 * k + 2, :].rearrange("d e h -> d (e h)"),
                                  xnT[:], start=True, stop=True).then_inc(h_mm, 1)
                n = group_now(g, 2)
                if n is not None:
                    pe.wait_ge(w_ready, n + 1)
                    spread_weights(n, par, 0)
                    spread_weights(n, par, 1)
                m = group_now(g, 3)
                if m is not None:
                    pe.wait_ge(weighted_ready, C0 * m + C0)
                    if not static(m) or m >= 1:
                        pe.wait_ge(x_updated, m)
                    for j in range(GT):
                        for k in range(C0):
                            last = pe.matmul(y[:, bass.ts(j, P)], weighted[1 - par][:, k, bass.ts(j, P)], c.w2_0[:, k, :],
                                             start=(k == 0), stop=(k == C0 - 1))
                    last.then_inc(y_mm, 1)
                if n is not None:
                    spread_weights(n, par, 2)

            group_steps(pe, LAG, step)


def attention_of_layer1(nc, sb, psum, sem, c, a, X):
    ln = LayerNorm("c", sb, sem, c, X)
    ctx_in = [sb(f"c_ctx{i}", [P, GT, DC], F32) for i in range(2)]
    xnT = sb("c_xnT", [D, GW], F32)
    ctxT = sb("c_ctxT", [DC, GW], F32)
    qT = sb("c_qT", [D, GW], F32)
    kT = sb("c_kT", [D, GW], F32)
    neg_max = sb("c_neg_max", [P, GT], F32)
    shifted = sb("c_shifted", [P, GT, S], F32)
    probs = c.probs1
    probsT = sb("c_probsT", [P, GT, P], F32)
    values = c.values1
    rec = sb("c_rec", [P, GT], F32)

    tr, q_bank, k_bank, v_bank, s_bank, pT_bank = (psum(f"c_{n}_bank", [P, 512], F32) for n in ("tr", "q", "k", "v", "s", "pT"))
    out_bank = psum("c_out_bank", [P, 2, 512], F32)
    outs = [out_bank[:, j // 2, (D + 1) * (j % 2):(D + 1) * (j % 2 + 1)] for j in range(GT)]

    loaded = [sem(f"c_loaded{i}") for i in range(2)]
    xn_transposed, xT_ready = sem("c_xn_transposed"), sem("c_xT_ready")
    ctx_transposed, ctxT_ready = sem("c_ctx_transposed"), sem("c_ctxT_ready")
    q_mm, k_mm, v_mm = sem("c_q_mm"), sem("c_k_mm"), sem("c_v_mm")
    q_ready, k_ready, v_ready = sem("c_q_ready"), sem("c_k_ready"), sem("c_v_ready")
    s_mm, max_done, shifted_ready, exp_done = sem("c_s_mm"), sem("c_max_done"), sem("c_shifted"), sem("c_exp_done")
    pT_mm, pT_ready, out_mm = sem("c_pT_mm"), sem("c_pT_ready"), sem("c_out_mm")
    bias_added, rec_done, x_updated = sem("c_bias_added"), sem("c_rec_done"), sem("c_x_updated")
    LAG = 2

    with nc.Block() as block:
        @block.sync
        def _(sp):
            def load(g, par):
                if not static(g) or g >= 2:
                    sp.wait_ge(ctx_transposed, g - 1)
                sp.dma_start(ctx_in[par][:],
                             a["ctx_768"].rearrange("(t b) s d -> (b s) t d", b=2)[:, bass.ts(g, GT), :]).then_inc(loaded[par], 16)

            load(0, 0)
            load(1, 1)
            with sp.Fori(1, G // 2) as i:
                load(i * 2, 0)
                load(i * 2 + 1, 1)

        @block.gpsimd
        def _(pool):
            def add_bias(n):
                wait_alone(pool, ln.xn_ready, n + 1)
                pool.tensor_tensor(X[:, bass.ts(n, GT), :], X[:, bass.ts(n, GT), :],
                                   c.out_bias1[:].unsqueeze(1).broadcast_to([P, GT, D]), ALU.add).then_inc(bias_added, 1)

            def step(g, par):
                n = group_now(g, -1)
                if n is not None:
                    add_bias(n)
                n = group_now(g, -2)
                if n is not None:
                    ln.deviation(pool, n)

            ln.deviation(pool, 0)
            add_bias(0)
            ln.deviation(pool, 1)
            group_steps(pool, LAG, step)

        @block.vector
        def _(dve):
            def step(g, par):
                n = group_now(g, 2)
                if n is not None:
                    dve.wait_ge(s_mm, n + 1)
                    dve.tensor_reduce(neg_max[:], s_bank[:, 0:GT * S].rearrange("p (t k) -> p t k", k=S), AX_X, ALU.max,
                                      negate=True).then_inc(max_done, 1)
                    dve.wait_ge(max_done, n + 1)
                    if not static(n) or n >= 1:
                        dve.wait_ge(exp_done, n)
                    dve.tensor_tensor(shifted[:], s_bank[:, 0:GT * S].rearrange("p (t k) -> p t k", k=S),
                                      neg_max[:].unsqueeze(2).broadcast_to([P, GT, S]), ALU.add).then_inc(shifted_ready, 1)
                n = group_now(g, -1)
                if n is not None:
                    ln.rows(dve, n, xn_transposed)
                n = group_now(g, 1)
                if n is not None:
                    dve.wait_ge(v_mm, n + 1)
                    if not static(n) or n >= 2:
                        dve.wait_ge(out_mm, n - 1)
                    dve.tensor_copy(values[1 - par][:, :, 0:D],
                                    v_bank[:].rearrange("p (t d) -> p t d", t=GT)).then_inc(v_ready, 1)
                n = group_now(g, -2)
                if n is not None:
                    ln.statistics(dve, n)
                n = group_now(g, 2)
                if n is not None:
                    dve.wait_ge(out_mm, n + 1)
                    dve.reciprocal(rec[:].rearrange("p (a b) -> p a b", a=2),
                                   out_bank[:, :, D:2 * (D + 1):D + 1]).then_inc(rec_done, 1)
                    dve.wait_ge(rec_done, n + 1)
                    dve.wait_ge(bias_added, n + 1)
                    for j in range(GT):
                        last = dve.scalar_tensor_tensor(out=X[:, n * GT + j, :], in0=outs[j][:, 0:D], scalar=rec[:, j:j + 1],
                                                        in1=X[:, n * GT + j, :], op0=ALU.mult, op1=ALU.add)
                    last.then_inc(x_updated, 1)

            ln.statistics(dve, 0)
            ln.rows(dve, 0, xn_transposed)
            ln.statistics(dve, 1)
            group_steps(dve, LAG, step)

        @block.scalar
        def _(act):
            def step(g, par):
                n = group_now(g, 2)
                if n is not None:
                    act.wait_ge(shifted_ready, n + 1)
                    if not static(n) or n >= 1:
                        act.wait_ge(pT_mm, n)
                    for b in range(2):
                        half = slice(S * b, S * b + S)
                        last = act.activation(probs[half, :, half], shifted[half], ACT.Exp, scale=SCALE1)
                    last.then_inc(exp_done, 1)
                m = group_now(g, 1)
                if m is not None:
                    act.wait_ge(q_mm, m + 1)
                    if not static(m) or m >= 1:
                        act.wait_ge(s_mm, m)
                    act.activation(qT[:], q_bank[:], ACT.Identity, bias=c.bq1[:, 0:1]).then_inc(q_ready, 1)
                w = group_now(g, 0)
                if w is not None:
                    act.wait_ge(xn_transposed, w + 1)
                    if not static(w) or w >= 1:
                        act.wait_ge(q_mm, w)
                    act.copy(xnT[:], tr[:]).then_inc(xT_ready, 1)
                if m is not None:
                    act.wait_ge(k_mm, m + 1)
                    act.activation(kT[:], k_bank[:], ACT.Identity, bias=c.bk1[:, 0:1]).then_inc(k_ready, 1)
                if n is not None:
                    act.wait_ge(pT_mm, n + 1)
                    if not static(n) or n >= 1:
                        act.wait_ge(out_mm, n)
                    act.copy(probsT[:].rearrange("p t q -> p (t q)"), pT_bank[:]).then_inc(pT_ready, 1)
                if w is not None:
                    act.wait_ge(ctx_transposed, w + 1)
                    if not static(w) or w >= 1:
                        act.wait_ge(v_mm, w)
                    act.copy(ctxT[:], tr[0:DC, :]).then_inc(ctxT_ready, 1)

            group_steps(act, LAG, step)

        @block.tensor
        def _(pe):
            def step(g, par):
                n = group_now(g, 2)
                if n is not None:
                    pe.wait_ge(q_ready, n + 1)
                    pe.wait_ge(k_ready, n + 1)
                    if not static(n) or n >= 1:
                        pe.wait_ge(shifted_ready, n)
                    for j in range(GT):
                        for b in range(2):
                            cols = bass.ts(2 * j + b, S)
                            last = pe.matmul(s_bank[S * b:S * b + S, bass.ts(j, S)], qT[:, cols], kT[:, cols],
                                             start=True, stop=True)
                    last.then_inc(s_mm, 1)
                w = group_now(g, 0)
                if w is not None:
                    pe.wait_ge(ln.xn_ready, w + 1)
                    if not static(w) or w >= 1:
                        pe.wait_ge(ctxT_ready, w)
                    for j in range(GT):
                        last = pe.transpose(tr[:, bass.ts(j, P)], ln.xn[:, j, :], c.ident[:])
                    last.then_inc(xn_transposed, 1)
                m = group_now(g, 1)
                if m is not None:
                    pe.wait_ge(xT_ready, m + 1)
                    if not static(m) or m >= 1:
                        pe.wait_ge(q_ready, m)
                        pe.wait_ge(k_ready, m)
                        pe.wait_ge(v_ready, m)
                    pe.matmul(q_bank[:], c.wq1[:], xnT[:], start=True, stop=True).then_inc(q_mm, 1)
                    pe.wait_ge(ctxT_ready, m + 1)
                    pe.matmul(k_bank[:], c.wk1[:], ctxT[:], start=True, stop=True).then_inc(k_mm, 1)
                    for j in range(GT):
                        last = pe.matmul(v_bank[:, bass.ts(j, P)], ctxT[:, bass.ts(j, P)], c.wv1[:], start=True, stop=True)
                    last.then_inc(v_mm, 1)
                if n is not None:
                    pe.wait_ge(exp_done, n + 1)
                    if not static(n) or n >= 1:
                        pe.wait_ge(pT_ready, n)
                    for j in range(GT):
                        last = pe.transpose(pT_bank[:, bass.ts(j, P)], probs[:, j, :], c.ident[:])
                    last.then_inc(pT_mm, 1)
                if w is not None:
                    pe.wait_ge(xT_ready, w + 1)
                    pe.wait_ge(loaded[par], 16 * ((w - par) // 2) + 16)
                    for j in range(GT):
                        last = pe.transpose(tr[0:DC, bass.ts(j, P)], ctx_in[par][:, j, :], c.ident[:])
                    last.then_inc(ctx_transposed, 1)
                if n is not None:
                    pe.wait_ge(pT_ready, n + 1)
                    pe.wait_ge(v_ready, n + 1)
                    if not static(n) or n >= 1:
                        pe.wait_ge(x_updated, n)
                    for j in range(GT):
                        last = pe.matmul(outs[j], probsT[:, j, :], values[par][:, j, :], start=True, stop=True)
                    last.then_inc(out_mm, 1)

            group_steps(pe, LAG, step)


def mixture_of_layer1(nc, sb, psum, sem, c, X):
    ln = LayerNorm("d", sb, sem, c, X)
    top = TopTwo("d", sb, sem, c, E1)
    KH = HID1 // P
    xnT = [sb(f"d_xnT{i}", [D, GW], F32) for i in range(2)]
    weights = [sb(f"d_weights{i}", [P, GT, E1], F32) for i in range(2)]
    silu = [sb(f"d_silu{i}", [P, KH, GW], F32) for i in range(2)]
    hidden = [sb(f"d_hidden{i}", [P, KH, GW], F32) for i in range(2)]

    tr, z = psum("d_tr", [P, 512], F32), psum("d_z", [P, 512], F32)
    u_bank, v_bank = ([psum(f"d_{n}{k}", [P, 512], F32) for k in range(KH)] for n in "uv")
    y = [psum(f"d_y{i}", [P, 512], F32) for i in range(2)]

    xn_transposed, xT_ready, z_mm, z_read, weights_ready = (sem(f"d_{n}") for n in ("xn_transposed", "xT_ready", "z_mm", "z_read", "weights"))
    u_mm, v_mm, silu_done, h_ready, y_mm, added = (sem(f"d_{n}") for n in ("u_mm", "v_mm", "silu_done", "h_ready", "y_mm", "added"))
    LAG = 1
    PREP_E = 3

    with nc.Block() as block:
        @block.gpsimd
        def _(pool):
            def step(g, par):
                n = group_now(g, -2)
                if n is not None:
                    ln.deviation(pool, n)

            ln.deviation(pool, 0)
            ln.deviation(pool, 1)
            group_steps(pool, LAG, step)

        @block.vector
        def _(dve):
            def add(n, par, e):
                x = E1 * n + e
                dve.wait_ge(y_mm, x + 1)
                if e == 0:
                    dve.wait_ge(weights_ready, n + 1)
                if not static(x) or x >= 1:
                    dve.wait_ge(added, x)
                for j in range(GT):
                    last = dve.scalar_tensor_tensor(out=X[:, n * GT + j, :], in0=y[e % 2][:, bass.ts(j, P)],
                                                    scalar=weights[par][:, j, e:e + 1], in1=X[:, n * GT + j, :],
                                                    op0=ALU.mult, op1=ALU.add)
                last.then_inc(added, 1)

            def step(g, par):
                m, n = group_now(g, 0), group_now(g, 1)
                for e in range(E1):
                    if n is not None:
                        x = E1 * n + e
                        if e >= 2 or not static(n) or n >= 1:
                            dve.wait_ge(y_mm, x - 1)
                        for k in range(KH):
                            dve.wait_ge(v_mm, KH * x + k + 1)
                            dve.wait_ge(silu_done, KH * x + k + 1)
                            dve.tensor_tensor(hidden[e % 2][:, k], silu[e % 2][:, k], v_bank[k][:],
                                              ALU.mult).then_inc(h_ready, 1)
                        if e >= 1:
                            add(n, 1 - par, e - 1)
                    if e == PREP_E and m is not None:
                        dve.wait_ge(z_mm, m + 1)
                        dve.tensor_copy(top.logits[:].rearrange("p t e -> p (t e)"), z[:, 0:GT * E1]).then_inc(z_read, 1)
                        dve.wait_ge(z_read, m + 1)
                        top.choose(dve, m, [0])
                    if e == PREP_E + 1:
                        if m is not None:
                            top.shares(dve, m)
                            top.weigh(dve, m)
                            dve.wait_ge(top.op_done, top.OPS * m + 16)
                            dve.tensor_copy(weights[par][:], top.weights[:]).then_inc(weights_ready, 1)
                        w = group_now(g, -1)
                        if w is not None:
                            ln.rows(dve, w, xn_transposed)
                        w = group_now(g, -2)
                        if w is not None:
                            ln.statistics(dve, w)
                if n is not None:
                    add(n, 1 - par, E1 - 1)

            ln.statistics(dve, 0)
            ln.rows(dve, 0, xn_transposed)
            ln.statistics(dve, 1)
            group_steps(dve, LAG, step)

        @block.scalar
        def _(act):
            def step(g, par):
                m, n = group_now(g, 0), group_now(g, 1)
                for e in range(E1):
                    if e == PREP_E and m is not None:
                        act.wait_ge(xn_transposed, m + 1)
                        if not static(m) or m >= 2:
                            act.wait_ge(v_mm, E1 * KH * (m - 1))
                        act.copy(xnT[par][:], tr[:]).then_inc(xT_ready, 1)
                    if n is not None:
                        x = E1 * n + e
                        for k in range(KH):
                            act.wait_ge(u_mm, KH * x + k + 1)
                            if k == 0 and (e >= 2 or not static(n) or n >= 1):
                                act.wait_ge(h_ready, KH * (x - 1))
                            act.activation(silu[e % 2][:, k], u_bank[k][:], ACT.Silu).then_inc(silu_done, 1)
                    if e == PREP_E and m is not None:
                        top.gap_tanh(act, m)

            group_steps(act, LAG, step)

        @block.tensor
        def _(pe):
            def outputs(n, par, e):
                x = E1 * n + e
                pe.wait_ge(h_ready, KH * x + KH)
                if e >= 2 or not static(n) or n >= 1:
                    pe.wait_ge(added, x - 1)
                for j in range(GT):
                    for k in range(KH):
                        last = pe.matmul(y[e % 2][:, bass.ts(j, P)], hidden[e % 2][:, k, bass.ts(j, P)], c.w3[:, e, k],
                                         start=(k == 0), stop=(k == KH - 1))
                last.then_inc(y_mm, 1)

            def step(g, par):
                m, n = group_now(g, 0), group_now(g, 1)
                for e in range(E1):
                    if n is not None:
                        x = E1 * n + e
                        if e == 0:
                            pe.wait_ge(xT_ready, n + 1)
                        for i, (bank, mm, done) in enumerate(((u_bank, u_mm, silu_done), (v_bank, v_mm, h_ready))):
                            for k in range(KH):
                                if e >= 1 or not static(n) or n >= 1:
                                    pe.wait_ge(done, KH * (x - 1) + k + 1)
                                pe.matmul(bank[k][:], c.w12[:, e, i, bass.ts(k, P)], xnT[1 - par][:], start=True,
                                          stop=True).then_inc(mm, 1)
                        if e >= 1:
                            outputs(n, 1 - par, e - 1)
                    if e == PREP_E - 1 and m is not None:
                        pe.wait_ge(ln.xn_ready, m + 1)
                        if not static(m) or m >= 1:
                            pe.wait_ge(xT_ready, m)
                        for j in range(GT):
                            last = pe.transpose(tr[:, bass.ts(j, P)], ln.xn[:, j, :], c.ident[:])
                        last.then_inc(xn_transposed, 1)
                    if e == PREP_E and m is not None:
                        pe.wait_ge(xT_ready, m + 1)
                        if not static(m) or m >= 1:
                            pe.wait_ge(z_read, m)
                        for j in range(GT):
                            last = pe.matmul(z[:, bass.ts(j, E1)], xnT[par][:, bass.ts(j, P)], c.w_route1[:], start=True,
                                             stop=True)
                        last.then_inc(z_mm, 1)
                if n is not None:
                    outputs(n, 1 - par, E1 - 1)

            group_steps(pe, LAG, step)


def load_x(nc, sem, a, X):
    x_loaded = sem("x_loaded")
    with nc.Block() as block:
        @block.sync
        def _(sp):
            sp.dma_start(X[:], a["x"].rearrange("(t b) s d -> (b s) t d", b=2)).then_inc(x_loaded, 16)
            sp.wait_ge(x_loaded, 16)


def store_result(nc, sb, sem, X, out):
    stored = sem("stored")
    with nc.Block() as block:
        @block.sync
        def _(sp):
            sp.dma_start(out.rearrange("(t b) s d -> (b s) t d", b=2), X[:]).then_inc(stored, 16)
            sp.wait_ge(stored, 16)


def build(nc, a, out, phases="ABCD"):
    with ExitStack() as ctx:
        def sb(name, shape, dt):
            return ctx.enter_context(nc.sbuf_tensor(name, shape, dt))

        def sem(name):
            return ctx.enter_context(nc.semaphore(name))

        X = sb("X", [P, TILES, D], F32)
        c = Shared()
        with ExitStack() as pctx:
            load_constants(nc, sb, lambda n, s, d: pctx.enter_context(nc.psum_tensor(n, s, d)), sem, c, a)
        if "A" not in phases:
            load_x(nc, sem, a, X)
        for name, phase, args in (("A", attention_of_layer0, (c, a, X)), ("B", mixture_of_layer0, (c, X)),
                                  ("C", attention_of_layer1, (c, a, X)), ("D", mixture_of_layer1, (c, X))):
            if name in phases:
                with ExitStack() as own:
                    phase(nc, lambda n, s, d: own.enter_context(nc.sbuf_tensor(n, s, d)),
                          lambda n, s, d: own.enter_context(nc.psum_tensor(n, s, d)),
                          lambda n: own.enter_context(nc.semaphore(n)), *args)
        store_result(nc, sb, sem, X, out)


_INS = ["x", "ctx_768", "g_xattn", "g_ffn", "L0_xattn_wq", "L0_xattn_bq", "L0_xattn_wk", "L0_xattn_bk", "L0_xattn_wv",
        "L0_xattn_bv", "L0_xattn_wo", "L0_xattn_bo", "L0_ffn_proj_w", "L0_ffn_anchors", "L0_ffn_routing_temp",
        "L0_ffn_w1", "L0_ffn_w2", "L1_xattn_Wq", "L1_xattn_bq", "L1_xattn_Wk", "L1_xattn_bk", "L1_xattn_Wv",
        "L1_xattn_bv", "L1_ffn_Wg", "L1_ffn_W1", "L1_ffn_W2", "L1_ffn_W3"]


def shape_constants():
    import numpy as np
    part = np.arange(P)
    head_of_group = ((part[:, None] % 32) // DH == np.arange(4)[None, :]).astype(np.float32)
    head_cols = np.tile(np.repeat(np.eye(H, dtype=np.float32), S, axis=1), (2, 1))
    strip_rows = np.zeros((H, SETS, 4, STRIP), np.float32)
    for h in range(H):
        strip_rows[h, h // 8, h // 2 % 4, DH * (h % 2):DH * (h % 2) + DH] = 1.0
    strip_rows = np.tile(strip_rows.reshape(H, SETS * P), (3, 1))
    expert_cols = np.tile(np.repeat(np.eye(E0, dtype=np.float32), HID0, axis=1), (3, 1))
    return {"const_ident": np.eye(P, dtype=np.float32), "const_head_of_group": head_of_group,
            "const_head_cols": head_cols, "const_expert_cols": expert_cols, "const_strip_rows": strip_rows,
            "const_early": np.arange(E1, 0, -1).astype(np.float32)}


def kernel(**inputs):
    import numpy as np
    import concourse.bacc as bacc
    from concourse.bass_utils import run_bass_kernel_spmd

    nc = bacc.Bacc("TRN2", target_bir_lowering=False, num_devices=1)
    arrays = {n: np.ascontiguousarray(inputs[n]) for n in _INS}
    arrays["L0_ffn_routing_temp"] = arrays["L0_ffn_routing_temp"].reshape(1)
    arrays.update(shape_constants())
    aps = {n: nc.dram_tensor(f"in_{n}", v.shape, mybir.dt.from_np(v.dtype), kind="ExternalInput").ap()
           for n, v in arrays.items()}
    out = nc.dram_tensor("out_x", (B, S, D), F32, kind="ExternalOutput").ap()
    build(nc, aps, out)
    r = run_bass_kernel_spmd(nc, [{f"in_{n}": v for n, v in arrays.items()}], core_ids=[0])
    return r.results[0]["out_x"]
```

```python
from contextlib import ExitStack

import concourse.bass as bass
from concourse import mybir

ALU = mybir.AluOpType
ACT = mybir.ActivationFunctionType
F32 = mybir.dt.float32
BF16 = mybir.dt.bfloat16
I32 = mybir.dt.int32
U32 = mybir.dt.uint32
AX_X = mybir.AxisListType.X

P = 128
B, S, D = 128, 64, 128
DC = 96
TILES = B * S // P
GT = 4
G = TILES // GT
GB = GT * P // S
GW = GT * P
H, DH = 16, 8
HU = H // 2
SETS = 2
REC = 64
STRIP = 32
E0, HID0 = 6, 64
C0 = E0 * HID0 // P
E1, HID1 = 8, 256
TP = 2 * P
ROW = D + 2
REGION = B * S + TP
MAX_TILES = B * S // TP
DTILES = 2 * B * S // TP + E1 - 1
DUMMY_TILES = E1 - 1
EPS = 1e-5
SCALE0 = float(DH) ** -0.5
SCALE1 = float(D) ** -0.5
QUANT_TEMP = 0.3
FAR = 1e30


def static(t):
    return isinstance(t, int)


def loop_steps(eng, first_static, looped, last, step):
    period = 2 * GT
    for t in range(first_static):
        step(t, t % period, t // GT)
    with eng.Fori(first_static // period, first_static // period + looped) as i:
        for u in range(period):
            step(i * period + u, u, i * 2 + u // GT)
    for t in range(first_static + looped * period, last):
        step(t, t % period, t // GT)


def wait_alone(eng, semaphore, value):
    eng.wait_ge(semaphore, value)
    eng.nop(nofuse=True)


def inverse_deviation(pool, stats, minus_half, rstd, rstd_step, g):
    pool.tensor_scalar(rstd, stats[:, :, 1], EPS, None, ALU.add).then_inc(rstd_step, 1)
    wait_alone(pool, rstd_step, 2 * g + 1)
    pool.tensor_tensor(rstd, rstd, minus_half, ALU.pow).then_inc(rstd_step, 1)


class Shared:
    pass


def load_constants(nc, sb, psum, sem, c, a, dispatch):
    c.first_row = sb("first_row", [P, E1], F32)
    c.earlier_f = sb("earlier_f", [P, P], F32)
    c.earlier = sb("earlier", [P, P], BF16)
    c.ones_bf = sb("ones_bf", [P, P], BF16)
    c.fill_tokens = sb("fill_tokens", [P, E1 + DUMMY_TILES, 2], F32)
    c.tile_sizes = sb("tile_sizes", [1, MAX_TILES], F32)
    c.up_to = sb("up_to", [1, E1, E1], F32)
    c.tile_number = sb("tile_number", [1, DTILES], F32)
    c.minus_half = sb("minus_half", [P, GT], F32)
    c.ident = sb("ident", [P, P], F32)
    c.ident_bf = sb("ident_bf", [P, P], BF16)
    c.head_of_group = sb("head_of_group", [P, 4], F32)
    c.head_cols_f = sb("head_cols_f", [2 * H, H * S], F32)
    c.head_cols = sb("head_cols", [2 * H, H * S], BF16)
    c.expert_cols_f = sb("expert_cols_f", [3 * E0, C0, P], F32)
    c.expert_cols = sb("expert_cols", [3 * E0, C0, P], BF16)
    c.expert_number = sb("expert_number", [P, E1], F32)
    c.gates_in = sb("gates_in", [P, 4], F32)
    c.gates = sb("gates", [P, 4], F32)
    c.wq0 = sb("wq0", [D, D], F32)
    c.wk0 = sb("wk0", [DC, D], F32)
    c.wv0 = sb("wv0", [DC, D], F32)
    c.wo0_in = sb("wo0_in", [D, D], F32)
    c.wo0 = sb("wo0", [D, D], F32)
    c.bq0 = sb("bq0", [P, 2], F32)
    c.bk0 = sb("bk0", [P, 2], F32)
    c.wo0_strips_in = sb("wo0_strips_in", [P, SETS, D], F32)
    c.wo0_strips = sb("wo0_strips", [P, SETS, D], F32)
    c.bv0 = sb("bv0", [D, 1], F32)
    c.bv0_wide = sb("bv0_wide", [D, P], F32)
    c.bo0_rows = sb("bo0_rows", [P, D], F32)
    c.bo0_gated = sb("bo0_gated", [P, D], F32)
    c.out_bias0 = sb("out_bias0", [P, D], F32)
    c.w_route0_in = sb("w_route0_in", [E0, D], F32)
    c.w_route0 = sb("w_route0", [D, E0], F32)
    c.anchors = sb("anchors", [P, E0, E0], F32)
    c.temp_in = sb("temp_in", [P, 1], F32)
    c.temp = sb("temp", [P, 1], F32)
    c.half_over_temp = sb("half_over_temp", [P, 2], F32)
    c.w1_0 = sb("w1_0", [D, E0, HID0], F32)
    c.w2_0_in = sb("w2_0_in", [P, C0, D], F32)
    c.w2_0 = sb("w2_0", [P, C0, D], F32)
    c.wq1 = sb("wq1", [D, D], F32)
    c.wk1 = sb("wk1", [DC, D], F32)
    c.wv1_in = sb("wv1_in", [DC, D], F32)
    c.wv1 = sb("wv1", [DC, D], F32)
    c.bq1 = sb("bq1", [D, 1], F32)
    c.bk1 = sb("bk1", [D, 1], F32)
    c.bv1_rows = sb("bv1_rows", [P, D], F32)
    c.out_bias1 = sb("out_bias1", [P, D], F32)
    c.w_route1 = sb("w_route1", [D, E1], F32)
    c.w12 = sb("w12", [D, E1, 2, HID1], F32)
    c.w3_in = sb("w3_in", [P, E1, HID1 // P, D], F32)
    c.w3 = sb("w3", [P, E1, HID1 // P, D], F32)
    c.v_heads = [sb(f"v_heads{i}", [P, GB, HU, STRIP], F32) for i in range(2)]
    c.q_blocks = [sb(f"q_blocks{i}", [P, GT, 4, 2, S], F32) for i in range(2)]
    c.parts = sb("parts", [P, REC + 3 * H], BF16)
    c.strip_rows_f = sb("strip_rows_f", [P, SETS, P], F32)
    c.strip_rows = sb("strip_rows", [P, SETS, P], BF16)
    c.probs1 = sb("probs1", [P, GT, P], F32)
    c.values1 = [sb(f"values1_{i}", [P, GT, D + 1], F32) for i in range(2)]

    bank = psum("constants_bank", [P, 512], F32)
    loads = sem("loads")
    tanh_done = sem("tanh_done")
    zeroed, fill_zeroed = sem("zeroed"), sem("fill_zeroed")
    gated = sem("gated")
    bias_mm = sem("bias_mm")
    bv_wide_done = sem("bv_wide_done")
    temp_step = sem("temp_step")

    def column(row):
        return row.rearrange("(p a) -> p a", a=1)

    def spread(ap, n):
        return ap.rearrange("(a n) -> a n", a=1).broadcast_to([P, n])

    plan = [
        (c.first_row[:], spread(a["const_first_row"], E1)), (c.earlier_f[:], a["const_earlier"]),
        (c.fill_tokens[:], a["const_fill_tokens"]), (dispatch.tokens[:], a["const_tokens"]),
        (c.tile_sizes[:], a["const_tile_sizes"]), (c.up_to[:], a["const_up_to"]), (c.tile_number[:], a["const_tile_number"]),
        (c.ident[:], a["const_ident"]), (c.head_of_group[:], a["const_head_of_group"]),
        (c.head_cols_f[:], a["const_head_cols"]),
        (c.strip_rows_f[REC:REC + 3 * H, :, :], a["const_strip_rows"].rearrange("h (t r) -> h t r", t=SETS)),
        (c.expert_cols_f[:], a["const_expert_cols"].rearrange("p (c n) -> p c n", c=C0)),
        (c.expert_number[:], spread(a["const_expert_number"], E1)),
        (c.gates_in[:, 0:2], spread(a["g_xattn"], 2)), (c.gates_in[:, 2:4], spread(a["g_ffn"], 2)),
        (c.wq0[:], a["L0_xattn_wq"]), (c.wk0[:], a["L0_xattn_wk"]), (c.wv0[:], a["L0_xattn_wv"]),
        (c.wo0_in[:], a["L0_xattn_wo"]),
        *[(dst[half:half + D // 2, :], a[name].rearrange("(h r) -> r h", h=2))
          for dst, name in ((c.bq0, "L0_xattn_bq"), (c.bk0, "L0_xattn_bk")) for half in (0, D // 2)],
        *[(c.wo0_strips_in[STRIP * k:STRIP * k + 2 * DH, :, :],
           a["L0_xattn_wo"].rearrange("(t k r) d -> k r t d", t=SETS, k=4)[k]) for k in range(4)],
        (c.bv0[:], column(a["L0_xattn_bv"])), (c.bo0_rows[:], spread(a["L0_xattn_bo"], D)),
        (c.w_route0_in[:], a["L0_ffn_proj_w"]),
        (c.anchors[:].rearrange("p e d -> p (e d)"), spread(a["L0_ffn_anchors"].rearrange("e d -> (e d)"), E0 * E0)),
        (c.temp_in[:], spread(a["L0_ffn_routing_temp"], 1)),
        (c.w1_0[:], a["L0_ffn_w1"].rearrange("e d h -> d e h")),
        (c.w2_0_in[:], a["L0_ffn_w2"].rearrange("(c a) h d -> (a h) c d", c=C0)),
        (c.wq1[:], a["L1_xattn_Wq"]), (c.wk1[:], a["L1_xattn_Wk"]), (c.wv1_in[:], a["L1_xattn_Wv"]),
        (c.bq1[:], column(a["L1_xattn_bq"])), (c.bk1[:], column(a["L1_xattn_bk"])),
        (c.bv1_rows[:], spread(a["L1_xattn_bv"], D)),
        (c.w_route1[:], a["L1_ffn_Wg"]),
        (c.w12[:, :, 0, :], a["L1_ffn_W1"].rearrange("e d h -> d e h")),
        (c.w12[:, :, 1, :], a["L1_ffn_W2"].rearrange("e d h -> d e h")),
        (c.w3_in[:], a["L1_ffn_W3"].rearrange("e (b h) d -> h e b d", h=P)),
    ]

    with nc.Block() as block:
        @block.sync
        def _(sp):
            sp.wait_ge(zeroed, 1)
            for n, (dst, src) in enumerate(plan):
                sp.dma_start(dst, src, allow_slow_non_contiguous=True).then_inc(loads, 16)
            sp.wait_ge(loads, 16 * len(plan))

        @block.gpsimd
        def _(pool):
            pool.memset(c.wo0_strips_in[:], 0.0).then_inc(zeroed, 1)
            pool.memset(c.parts[:], 0.0)
            for v in c.v_heads:
                pool.memset(v[:], 0.0)
            for q in c.q_blocks:
                pool.memset(q[:], 0.0)
            pool.memset(c.probs1[:].rearrange("p t k -> p (t k)"), 0.0)
            pool.memset(c.minus_half[:], -0.5)
            pool.memset(c.ones_bf[:], 1.0)
            pool.memset(dispatch.fill[:].rearrange("p a h r -> p (a h r)"), 0.0).then_inc(fill_zeroed, 1)
            for v in c.values1:
                pool.memset(v[:, :, D:D + 1], 1.0)

        @block.scalar
        def _(act):
            act.wait_ge(loads, 16 * len(plan))
            act.activation(c.gates[:], c.gates_in[:], ACT.Tanh).then_inc(tanh_done, 1)

        @block.vector
        def _(dve):
            dve.wait_ge(loads, 16 * len(plan))
            dve.tensor_copy(c.bv0_wide[:], c.bv0[:, 0:1].broadcast_to([D, P])).then_inc(bv_wide_done, 1)
            dve.tensor_copy(c.head_cols[:], c.head_cols_f[:])
            dve.tensor_copy(c.earlier[:], c.earlier_f[:])
            dve.wait_ge(fill_zeroed, 1)
            dve.tensor_copy(dispatch.fill[:, :, :, D], c.fill_tokens[:])
            dve.tensor_copy(c.strip_rows[REC:REC + 3 * H, :, :], c.strip_rows_f[REC:REC + 3 * H, :, :])
            dve.tensor_copy(c.expert_cols[:], c.expert_cols_f[:])
            dve.tensor_copy(c.ident_bf[:], c.ident[:])
            dve.tensor_scalar(c.temp[:], c.temp_in[:], 0.1, None, ALU.max).then_inc(temp_step, 1)
            dve.wait_ge(temp_step, 1)
            dve.reciprocal(c.half_over_temp[:, 0:1], c.temp[:]).then_inc(temp_step, 1)
            dve.wait_ge(temp_step, 2)
            dve.tensor_scalar(c.half_over_temp[:, 1:2], c.half_over_temp[:, 0:1], 0.5, None, ALU.mult)
            dve.wait_ge(tanh_done, 1)
            dve.tensor_scalar(c.wo0[:], c.wo0_in[:], c.gates[:, 0:1], None, ALU.mult).then_inc(gated, 1)
            dve.tensor_scalar(c.wo0_strips[:].rearrange("p t d -> p (t d)"),
                              c.wo0_strips_in[:].rearrange("p t d -> p (t d)"), c.gates[:, 0:1], None, ALU.mult)
            dve.tensor_scalar(c.bo0_gated[:], c.bo0_rows[:], c.gates[:, 0:1], None, ALU.mult).then_inc(gated, 1)
            dve.tensor_scalar(c.w2_0[:].rearrange("p c d -> p (c d)"), c.w2_0_in[:].rearrange("p c d -> p (c d)"),
                              c.gates[:, 2:3], None, ALU.mult)
            dve.tensor_scalar(c.w3[:].rearrange("p e b d -> p (e b d)"), c.w3_in[:].rearrange("p e b d -> p (e b d)"),
                              c.gates[:, 3:4], None, ALU.mult)
            dve.tensor_scalar(c.wv1[:], c.wv1_in[:], c.gates[0:DC, 1:2], None, ALU.mult)
            dve.tensor_scalar(c.out_bias1[:], c.bv1_rows[:], c.gates[:, 1:2], None, ALU.mult)
            dve.wait_ge(bias_mm, 2)
            dve.tensor_copy(c.w_route0[:], bank[:, 256:256 + E0])
            dve.wait_ge(gated, 2)
            dve.tensor_tensor(c.out_bias0[:], bank[:, 0:D], c.bo0_gated[:], ALU.add)

        @block.tensor
        def _(pe):
            pe.wait_ge(loads, 16 * len(plan))
            pe.transpose(bank[:, 256:256 + E0], c.w_route0_in[:], c.ident[0:E0, 0:E0]).then_inc(bias_mm, 1)
            pe.wait_ge(bv_wide_done, 1)
            pe.wait_ge(gated, 1)
            pe.matmul(bank[:, 0:D], c.bv0_wide[:], c.wo0[:], start=True, stop=True).then_inc(bias_mm, 1)


def attention_of_layer0(nc, sb, psum, sem, c, a, X):
    stats6 = sb("a_stats6", [P, GT, 6], F32)
    stats = sb("a_stats", [P, GT, 2], F32)
    rstd = sb("a_rstd", [P, GT], F32)
    xn = sb("a_xn", [P, GT, D], F32)
    xnT = sb("a_xnT", [D, GW], F32)
    ctx_in = [sb(f"a_ctx{i}", [P, GT, DC], F32) for i in range(2)]
    ctxT = sb("a_ctxT", [DC, GW], F32)
    kT = sb("a_kT", [P, 2, GT, S], F32)
    k_heads = [sb(f"a_k_heads{i}", [P, GT, 2, 4, S], F32) for i in range(2)]
    neg_max = sb("a_neg_max", [P, H], F32)
    parts = c.parts
    rows = sb("a_rows", [REC + 3 * H, P], BF16)
    probs = [sb(f"a_probs{i}", [P, H * S], F32) for i in range(2)]
    probsT = [sb(f"a_probsT{i}", [P, HU, P], F32) for i in range(2)]
    denom = sb("a_denom", [P, H], F32)
    rec = sb("a_rec", [P, H], F32)
    rec_rest = sb("a_rec_rest", [P, H], F32)
    heads_raw = sb("a_heads_raw", [P, SETS, P], F32)
    heads_outT = sb("a_heads_outT", [P, SETS, P], F32)

    scores = [psum(f"a_scores{i}", [P, 2, 512], F32) for i in range(2)]
    probsT_bank = psum("a_probsT_bank", [P, 512], F32)
    prep = psum("a_prep", [P, 512], F32)
    small = psum("a_small", [P, 512], F32)
    pv = psum("a_pv", [P, 2, SETS, P], F32)
    y = small[:, 0:D]
    rows_ps = small[0:REC + 3 * H, D:D + P // 2].bitcast(BF16)

    loaded = [sem(f"a_loaded{i}") for i in range(2)]
    bn_done, stats_done = sem("a_bn_done"), sem("a_stats_done")
    rstd_step, xn_ready, bias_added = sem("a_rstd_step"), sem("a_xn_ready"), sem("a_bias_added")
    prep_mm, prep_ev, v_odd_ev = sem("a_prep_mm"), sem("a_prep_ev"), sem("a_v_odd_ev")
    q_odd_ev, k_heads_ready = sem("a_q_odd_ev"), sem("a_k_heads")
    scores_mm, max_done, part1_done, parts_ready = sem("a_scores_mm"), sem("a_max"), sem("a_part1"), sem("a_parts")
    sum_done, rec_done, rec1_done = sem("a_sum"), sem("a_rec_done"), sem("a_rec1")
    rest_done, rec2_done, raw_ready = sem("a_rest"), sem("a_rec2"), sem("a_raw_ready")
    rows_mm, rows_ready, sub_mm, exp_done = sem("a_rows_mm"), sem("a_rows_ready"), sem("a_sub_mm"), sem("a_exp")
    pT_mm, pT_ev = sem("a_pT_mm"), sem("a_pT_ev")
    pv_mm, spread_mm, o_ready = sem("a_pv_mm"), sem("a_spread_mm"), sem("a_o_ready")
    y_mm, x_updated = sem("a_y_mm"), sem("a_x_updated")
    PREP = 5
    PREP_AT = ((0, 1), (2,), (3,), (4,))
    LAST = TILES + 4

    def tile_now(t, lag):
        return None if static(t) and not 0 <= t - lag < TILES else t - lag

    def group_at(g0, more):
        return None if static(g0) and g0 + more >= G else g0 + more

    with nc.Block() as block:
        @block.sync
        def _(sp):
            def load(g, par):
                if not static(g) or g >= 2:
                    sp.wait_ge(prep_mm, PREP * (g - 2) + 2)
                sp.dma_start(X[:, bass.ts(g, GT), :],
                             a["x"].rearrange("(t b) s d -> (b s) t d", b=2)[:, bass.ts(g, GT), :]).then_inc(loaded[par], 16)
                sp.dma_start(ctx_in[par][:],
                             a["ctx_768"].rearrange("(t b) s d -> (b s) t d", b=2)[:, bass.ts(g, GT), :]).then_inc(loaded[par], 16)

            load(0, 0)
            load(1, 1)
            with sp.Fori(1, G // 2) as i:
                load(i * 2, 0)
                load(i * 2 + 1, 1)

        @block.vector
        def _(dve):
            def layer_stats(g, par):
                dve.wait_ge(loaded[par], 32 * ((g - par) // 2) + 32)
                if not static(g) or g >= 1:
                    dve.wait_ge(xn_ready, g)
                for j in range(GT):
                    last = dve.bn_stats(stats6[:, j, :], X[:, g * GT + j, :])
                last.then_inc(bn_done, 1)
                wait_alone(dve, bn_done, g + 1)
                for j in range(GT):
                    last = dve.bn_aggr(stats[:, j, :], stats6[:, j, :])
                last.then_inc(stats_done, 1)

            def layer_norm(g):
                dve.wait_ge(rstd_step, 2 * g + 2)
                if not static(g) or g >= 1:
                    dve.wait_ge(prep_mm, PREP * (g - 1) + 1)
                for j in range(GT):
                    last = dve.tensor_scalar(xn[:, j, :], X[:, g * GT + j, :], stats[:, j, 0:1], rstd[:, j:j + 1],
                                             ALU.subtract, ALU.mult)
                last.then_inc(xn_ready, 1)

            def q_odd(g, par):
                dve.wait_ge(prep_mm, PREP * g + 4)
                if not static(g) or g >= 2:
                    dve.wait_ge(scores_mm, GT * (g - 1))
                for h in range(2):
                    for s in range(2):
                        rows_in = slice(64 + 32 * s, 96 + 32 * s)
                        last = dve.tensor_scalar(c.q_blocks[par][rows_in, :, 2 * h + s, 1, :],
                                                 prep[rows_in, bass.ts(h, GW // 2)].rearrange("p (t q) -> p t q", q=S),
                                                 c.bq0[rows_in, h:h + 1], None, ALU.add)
                last.then_inc(q_odd_ev, 1)

            def v_odd(g, par):
                dve.wait_ge(prep_mm, PREP * g + 5)
                if not static(g) or g >= 2:
                    dve.wait_ge(pv_mm, GT * (g - 1))
                dve.tensor_copy(c.v_heads[par][S:P, :, :, DH:2 * DH].rearrange("p b u w -> p (b u) w"),
                                prep[S:P, :].rearrange("p (b u w) -> p (b u) w", b=GB, u=HU)).then_inc(v_odd_ev, 1)

            def step(t, u, g0):
                n, m = tile_now(t, 0), tile_now(t, 2)
                if n is not None:
                    dve.wait_ge(scores_mm, n + 1)
                    dve.tensor_reduce(neg_max[:], scores[u % 2][:].rearrange("p a (h k) -> p (a h) k", k=S), AX_X,
                                      ALU.max, negate=True).then_inc(max_done, 1)
                w = tile_now(t, 4)
                if w is not None:
                    if u % GT == 0:
                        dve.wait_ge(bias_added, g0)
                    dve.wait_ge(y_mm, w + 1)
                    dve.tensor_tensor(X[:, w, :], y, X[:, w, :], ALU.add).then_inc(x_updated, 1)
                if m is not None:
                    dve.wait_ge(exp_done, m + 1)
                    dve.reduce_sum(denom[:], probs[u % 2][:].rearrange("p (h k) -> p h k", k=S), AX_X).then_inc(sum_done, 1)
                if (n is not None or m is not None) and (not static(t) or t >= 1):
                    dve.wait_ge(rows_mm, t)
                if n is not None:
                    dve.wait_ge(max_done, n + 1)
                    dve.tensor_copy(parts[:, 0:H], neg_max[:]).then_inc(part1_done, 1)
                if m is not None:
                    dve.wait_ge(sum_done, m + 1)
                    dve.reciprocal(rec[:], denom[:]).then_inc(rec_done, 1)
                if n is not None:
                    dve.wait_ge(part1_done, n + 1)
                    last = dve.tensor_tensor(parts[:, H:2 * H], neg_max[:], parts[:, 0:H], ALU.subtract)
                if m is not None:
                    dve.wait_ge(rec_done, m + 1)
                    dve.tensor_copy(parts[:, REC:REC + H], rec[:]).then_inc(rec1_done, 1)
                if m is not None:
                    dve.wait_ge(rec1_done, m + 1)
                    dve.tensor_tensor(rec_rest[:], rec[:], parts[:, REC:REC + H], ALU.subtract).then_inc(rest_done, 1)
                    dve.wait_ge(rest_done, m + 1)
                    dve.tensor_copy(parts[:, REC + H:REC + 2 * H], rec_rest[:]).then_inc(rec2_done, 1)
                    dve.wait_ge(rec2_done, m + 1)
                    last = dve.tensor_tensor(parts[:, REC + 2 * H:REC + 3 * H], rec_rest[:], parts[:, REC + H:REC + 2 * H],
                                             ALU.subtract)
                if n is not None or m is not None:
                    last.then_inc(parts_ready, 1)
                n = tile_now(t, 3)
                if n is not None:
                    dve.wait_ge(spread_mm, n + 1)
                    dve.wait_ge(raw_ready, n + 1)
                    if not static(n) or n >= 1:
                        dve.wait_ge(y_mm, n)
                    dve.tensor_tensor(heads_outT[:], heads_raw[:], pv[:, 1], ALU.mult).then_inc(o_ready, 1)
                if u % GT == 0:
                    g = group_at(g0, 2)
                    if g is not None:
                        layer_stats(g, (u // GT) % 2)
                if u % GT == 1:
                    g = group_at(g0, 2)
                    if g is not None:
                        layer_norm(g)
                if u % GT == 2:
                    g = group_at(g0, 1)
                    if g is not None:
                        q_odd(g, (u // GT + 1) % 2)
                if u % GT == 3:
                    g = group_at(g0, 1)
                    if g is not None:
                        v_odd(g, (u // GT + 1) % 2)

            layer_stats(0, 0)
            layer_norm(0)
            layer_stats(1, 1)
            q_odd(0, 0)
            v_odd(0, 0)
            layer_norm(1)
            loop_steps(dve, 2 * GT, TILES // (2 * GT) - 2, LAST, step)

        @block.gpsimd
        def _(pool):
            def deviation(g):
                wait_alone(pool, stats_done, g + 1)
                inverse_deviation(pool, stats[:], c.minus_half[:], rstd[:], rstd_step, g)

            def add_bias(g):
                wait_alone(pool, xn_ready, g + 1)
                pool.tensor_tensor(X[:, bass.ts(g, GT), :], X[:, bass.ts(g, GT), :],
                                   c.out_bias0[:].unsqueeze(1).broadcast_to([P, GT, D]), ALU.add).then_inc(bias_added, 1)

            def spread_k(g, par):
                wait_alone(pool, prep_ev, PREP * g + 3)
                if not static(g) or g >= 2:
                    wait_alone(pool, scores_mm, GT * (g - 1))
                for j in range(4):
                    last = pool.tensor_scalar(k_heads[par][:, :, :, j, :].rearrange("p t h k -> p h t k"), kT[:],
                                              c.head_of_group[:, j:j + 1], None, ALU.mult)
                last.then_inc(k_heads_ready, 1)

            def step(t, u, g0):
                if u % GT == 0:
                    g = group_at(g0, 2)
                    if g is not None:
                        deviation(g)
                if u % GT == 1:
                    g = group_at(g0, 1)
                    if g is not None:
                        spread_k(g, (u // GT + 1) % 2)
                    g = group_at(g0, 2)
                    if g is not None:
                        add_bias(g)

            deviation(0)
            add_bias(0)
            deviation(1)
            spread_k(0, 0)
            add_bias(1)
            loop_steps(pool, 2 * GT, TILES // (2 * GT) - 2, LAST, step)

        @block.scalar
        def _(act):
            def evacuate(g, par, k):
                act.wait_ge(prep_mm, PREP * g + k + 1)
                if k == 0:
                    act.copy(xnT[:], prep[:]).then_inc(prep_ev, 1)
                elif k == 1:
                    act.copy(ctxT[:], prep[0:DC, :]).then_inc(prep_ev, 1)
                elif k == 2:
                    if not static(g) or g >= 1:
                        act.wait_ge(k_heads_ready, g)
                    for h in range(2):
                        last = act.activation(kT[:, h], prep[:, bass.ts(h, GW // 2)], ACT.Identity,
                                              bias=c.bk0[:, h:h + 1])
                    last.then_inc(prep_ev, 1)
                elif k == 3:
                    if not static(g) or g >= 2:
                        act.wait_ge(scores_mm, GT * (g - 1))
                    for h in range(2):
                        for s in range(2):
                            rows_in = slice(32 * s, 32 * s + 32)
                            last = act.activation(c.q_blocks[par][rows_in, :, 2 * h + s, 0, :],
                                                  prep[rows_in, bass.ts(h, GW // 2)].rearrange("p (t q) -> p t q", q=S),
                                                  ACT.Identity, bias=c.bq0[rows_in, h:h + 1])
                    last.then_inc(prep_ev, 1)
                else:
                    if not static(g) or g >= 2:
                        act.wait_ge(pv_mm, GT * (g - 1))
                    act.copy(c.v_heads[par][0:S, :, :, 0:DH].rearrange("p b u w -> p (b u) w"),
                             prep[0:S, :].rearrange("p (b u w) -> p (b u) w", b=GB, u=HU)).then_inc(prep_ev, 1)

            def step(t, u, g0):
                n = tile_now(t, 1)
                if n is not None:
                    act.wait_ge(sub_mm, n + 1)
                    if not static(n) or n >= 2:
                        act.wait_ge(pT_mm, 2 * n - 2)
                    act.activation(probs[(u + 1) % 2][:], scores[(u + 1) % 2][:].rearrange("p a n -> p (a n)"), ACT.Exp,
                                   scale=SCALE0).then_inc(exp_done, 1)
                def keep_transposed(n, half):
                    act.wait_ge(pT_mm, 2 * n + 1 + half)
                    if half == 0 and (not static(n) or n >= 2):
                        act.wait_ge(pv_mm, n - 1)
                    act.copy(probsT[u % 2][:, half * HU // 2:(half + 1) * HU // 2, :].rearrange("p u q -> p (u q)"),
                             probsT_bank[:]).then_inc(pT_ev, 1)

                if tile_now(t, 2) is not None:
                    keep_transposed(t - 2, 0)
                n = tile_now(t, 3)
                if n is not None:
                    act.wait_ge(pv_mm, n + 1)
                    if not static(n) or n >= 1:
                        act.wait_ge(o_ready, n)
                    act.copy(heads_raw[:].rearrange("p t q -> p (t q)"), pv[:, 0].rearrange("p t q -> p (t q)")).then_inc(raw_ready, 1)
                if tile_now(t, 2) is not None:
                    keep_transposed(t - 2, 1)
                g = group_at(g0, 1)
                if g is not None:
                    for k in PREP_AT[u % GT]:
                        evacuate(g, (u // GT + 1) % 2, k)
                if not static(t) or t < TILES + 2:
                    act.wait_ge(rows_mm, t + 1)
                    if not static(t) or t >= 1:
                        if tile_now(t, 1) is not None:
                            act.wait_ge(sub_mm, t)
                        if tile_now(t, 3) is not None:
                            act.wait_ge(spread_mm, t - 2)
                    act.copy(rows[:], rows_ps).then_inc(rows_ready, 1)

            for k in range(PREP):
                evacuate(0, 0, k)
            loop_steps(act, 2 * GT, TILES // (2 * GT) - 2, LAST, step)

        @block.tensor
        def _(pe):
            def prepare(g, par, k):
                if k == 0:
                    if not static(g) or g >= 1:
                        pe.wait_ge(prep_ev, PREP * g)
                        pe.wait_ge(v_odd_ev, g)
                    pe.wait_ge(xn_ready, g + 1)
                    for j in range(GT):
                        last = pe.transpose(prep[:, bass.ts(j, P)], xn[:, j, :], c.ident[:])
                else:
                    pe.wait_ge(prep_ev, PREP * g + k)
                if k == 1:
                    pe.wait_ge(loaded[par], 32 * ((g - par) // 2) + 32)
                    for j in range(GT):
                        last = pe.transpose(prep[0:DC, bass.ts(j, P)], ctx_in[par][:, j, :], c.ident[:])
                if k in (2, 3):
                    w, src = ((c.wk0, ctxT), (c.wq0, xnT))[k - 2]
                    for h in range(2):
                        for odd in range(2):
                            last = pe.matmul(prep[S * odd:S * odd + S, bass.ts(h, GW // 2)], w[:, bass.ts(h, D // 2)],
                                             src[:].rearrange("p (t b q) -> p b t q", b=2, q=S)[:, odd],
                                             start=True, stop=True)
                if k == 4:
                    pe.wait_ge(q_odd_ev, g + 1)
                    for b in range(GB):
                        for odd in range(2):
                            last = pe.matmul(prep[S * odd:S * odd + S, bass.ts(b, D // 2)], ctxT[:, bass.ts(b, S)],
                                             c.wv0[:].rearrange("p (u h w) -> p h u w", h=2, w=DH)[:, odd],
                                             start=True, stop=True)
                last.then_inc(prep_mm, 1)

            def step(t, u, g0):
                n = tile_now(t, 0)
                if n is not None:
                    if u % GT == 0:
                        pe.wait_ge(prep_ev, PREP * g0 + 4)
                        pe.wait_ge(q_odd_ev, g0 + 1)
                        pe.wait_ge(k_heads_ready, g0 + 1)
                    if not static(n) or n >= 2:
                        pe.wait_ge(exp_done, n - 1)
                    par, tile = (u // GT) % 2, u % GT
                    for k in range(4):
                        last = pe.matmul(scores[u % 2][:, k // 2, bass.ts(k % 2, 4 * S)],
                                         c.q_blocks[par][:, tile, k].rearrange("p b q -> p (b q)"),
                                         k_heads[par][:, tile, k // 2].rearrange("p j k -> p (j k)"),
                                         start=(k % 2 == 0), stop=True, skip_group_check=True)
                    last.then_inc(scores_mm, 1)
                n = tile_now(t, 1)
                if n is not None:
                    pe.wait_ge(rows_ready, n + 1)
                    for half in range(2):
                        last = pe.matmul(scores[(u + 1) % 2][:, half, :], rows[0:2 * H, :], c.head_cols[:, bass.ts(half, 512)],
                                         start=False, stop=True, skip_group_check=True)
                    last.then_inc(sub_mm, 1)
                n = tile_now(t, 4)
                if n is not None:
                    pe.wait_ge(o_ready, n + 1)
                    pe.wait_ge(rows_ready, min(t, TILES + 2) if static(t) else t)
                    if not static(n) or n >= 1:
                        pe.wait_ge(x_updated, n)
                    for k in range(SETS):
                        last = pe.matmul(y, heads_outT[:, k, :], c.wo0_strips[:, k, :], start=(k == 0),
                                         stop=(k == SETS - 1))
                    last.then_inc(y_mm, 1)
                def transpose_probs(half):
                    for k in range(HU // 2):
                        last = pe.transpose(probsT_bank[:, bass.ts(k, P)],
                                            probs[u % 2][:, bass.ts(half * HU // 2 + k, P)], c.ident[:])
                    last.then_inc(pT_mm, 1)

                n = tile_now(t, 2)
                if n is not None:
                    pe.wait_ge(exp_done, n + 1)
                    if not static(n) or n >= 1:
                        pe.wait_ge(pT_ev, 2 * n)
                    transpose_probs(0)
                n = tile_now(t, 3)
                if n is not None:
                    pe.wait_ge(rows_ready, n + 3)
                    if not static(n) or n >= 1:
                        pe.wait_ge(o_ready, n)
                    for k in range(SETS):
                        last = pe.matmul(pv[:, 1, k, :], c.strip_rows[REC:REC + 3 * H, k, :], rows[REC:REC + 3 * H, :],
                                         start=True, stop=True)
                    last.then_inc(spread_mm, 1)
                    pe.wait_ge(pT_ev, 2 * n + 2)
                    v_par = ((u + 5) % 8 // GT) % 2
                    if (u + 5) % GT == 0:
                        g = g0 + (u % GT - 3) // GT
                        pe.wait_ge(prep_ev, PREP * g + 5)
                        pe.wait_ge(v_odd_ev, g + 1)
                    for k in range(HU):
                        strip = slice(STRIP * (k % 4), STRIP * (k % 4) + STRIP)
                        for b in range(2):
                            batch = 2 * ((u + 5) % GT) + b
                            last = pe.matmul(pv[strip, 0, k // 4, bass.ts(b, S)], c.v_heads[v_par][:, batch, k, :],
                                             probsT[(u + 1) % 2][:, k, bass.ts(b, S)], start=True, stop=True)
                    last.then_inc(pv_mm, 1)
                n = tile_now(t, 2)
                if n is not None:
                    pe.wait_ge(pT_ev, 2 * n + 1)
                    transpose_probs(1)
                g = group_at(g0, 1)
                if g is not None:
                    for k in PREP_AT[u % GT]:
                        prepare(g, (u // GT + 1) % 2, k)
                if not static(t) or t < TILES + 2:
                    pe.wait_ge(parts_ready, t + 1)
                    if not static(t) or t >= 1:
                        pe.wait_ge(rows_ready, t)
                    if tile_now(t, 4) is not None:
                        pe.wait_ge(x_updated, t - 3)
                    pe.transpose(rows_ps, parts[:], c.ident_bf[:]).then_inc(rows_mm, 1)

            for k in range(PREP):
                prepare(0, 0, k)
            loop_steps(pe, 2 * GT, TILES // (2 * GT) - 2, LAST, step)


def group_steps(eng, lag, step):
    first = -(-lag // 2)
    for g in range(2 * first):
        step(g, g % 2)
    with eng.Fori(first, G // 2 - 1) as i:
        step(i * 2, 0)
        step(i * 2 + 1, 1)
    for g in range(G - 2, G + lag):
        step(g, g % 2)


def group_now(g, lag):
    return None if static(g) and not 0 <= g - lag < G else g - lag


class LayerNorm:

    def __init__(self, name, sb, sem, c, X, own_rows=True):
        self.c, self.X = c, X
        self.stats6 = sb(f"{name}_stats6", [P, GT, 6], F32)
        self.stats = sb(f"{name}_stats", [P, GT, 2], F32)
        self.rstd = sb(f"{name}_rstd", [P, GT], F32)
        if own_rows:
            self.xn = sb(f"{name}_xn", [P, GT, D], F32)
        self.bn_done, self.stats_done = sem(f"{name}_bn_done"), sem(f"{name}_stats_done")
        self.rstd_step, self.xn_ready = sem(f"{name}_rstd_step"), sem(f"{name}_xn_ready")

    def statistics(self, dve, g):
        if not static(g) or g >= 1:
            wait_alone(dve, self.xn_ready, g)
        for j in range(GT):
            last = dve.bn_stats(self.stats6[:, j, :], self.X[:, g * GT + j, :])
        last.then_inc(self.bn_done, 1)
        wait_alone(dve, self.bn_done, g + 1)
        for j in range(GT):
            last = dve.bn_aggr(self.stats[:, j, :], self.stats6[:, j, :])
        last.then_inc(self.stats_done, 1)

    def deviation(self, pool, g):
        wait_alone(pool, self.stats_done, g + 1)
        inverse_deviation(pool, self.stats[:], self.c.minus_half[:], self.rstd[:], self.rstd_step, g)

    def rows(self, dve, g, transposed):
        dve.wait_ge(self.rstd_step, 2 * g + 2)
        if not static(g) or g >= 1:
            dve.wait_ge(transposed, g)
        self.normalise(dve, g, self.xn)

    def normalise(self, dve, g, out):
        for j in range(GT):
            last = dve.tensor_scalar(out[:, j, 0:D], self.X[:, g * GT + j, :], self.stats[:, j, 0:1],
                                     self.rstd[:, j:j + 1], ALU.subtract, ALU.mult)
        last.then_inc(self.xn_ready, 1)


class TopTwo:

    def __init__(self, name, sb, sem, c, experts, weighed):
        self.e, self.c = experts, c
        self.ops = 9 if weighed else 6
        self.logits = sb(f"{name}_logits", [P, GT, 8], F32)
        self.sorted = sb(f"{name}_sorted", [P, GT, 8], F32)
        self.index = sb(f"{name}_index", [P, GT, 8], U32)
        self.pick_index = sb(f"{name}_pick_index", [P, 2, GT], F32)
        self.picks = sb(f"{name}_picks", [P, 2, GT, experts], F32)
        self.first, self.second = self.picks[:, 0], self.picks[:, 1]
        self.gap = sb(f"{name}_gap", [P, GT], F32)
        self.tanh = sb(f"{name}_tanh", [P, GT], F32)
        if weighed:
            self.p1, self.p2 = sb(f"{name}_p1", [P, GT], F32), sb(f"{name}_p2", [P, GT], F32)
            self.weights = sb(f"{name}_weights", [P, GT, experts], F32)
        self.op_done = sem(f"{name}_op_done")
        self.gap_ready, self.tanh_ready = sem(f"{name}_gap_ready"), sem(f"{name}_tanh_ready")

    def wide(self, column):
        return column[:].unsqueeze(2).broadcast_to([P, GT, self.e])

    def set_up(self, dve):
        if self.e < 8:
            dve.memset(self.logits[:, :, self.e:], -FAR).then_inc(self.gap_ready, 1)

    def choose(self, dve, g):
        for j in range(GT):
            last = dve.max(self.sorted[:, j], self.logits[:, j])
        last.then_inc(self.op_done, 1)
        wait_alone(dve, self.op_done, self.ops * g + 1)
        for j in range(GT):
            last = dve.max_index(self.index[:, j], self.sorted[:, j], self.logits[:, j])
        last.then_inc(self.op_done, 1)
        dve.tensor_tensor(self.gap[:], self.sorted[:, :, 0], self.sorted[:, :, 1], ALU.subtract).then_inc(self.gap_ready, 1)
        dve.wait_ge(self.op_done, self.ops * g + 2)
        dve.tensor_copy(self.pick_index[:], self.index[:, :, 0:2].rearrange("p t k -> p k t")).then_inc(self.op_done, 1)
        dve.wait_ge(self.op_done, self.ops * g + 3)
        dve.tensor_tensor(self.picks[:], self.pick_index[:].unsqueeze(3).broadcast_to([P, 2, GT, self.e]),
                          self.c.expert_number[:, 0:self.e].unsqueeze(1).unsqueeze(1).broadcast_to([P, 2, GT, self.e]),
                          ALU.is_equal).then_inc(self.op_done, 1)
        dve.wait_ge(self.op_done, self.ops * g + 4)

    def gap_tanh(self, act, g):
        act.wait_ge(self.gap_ready, g + (2 if self.e < 8 else 1))
        act.activation(self.tanh[:], self.gap[:], ACT.Tanh, scale=0.5).then_inc(self.tanh_ready, 1)

    def shares(self, dve, g, p1, p2):
        dve.wait_ge(self.tanh_ready, g + 1)
        dve.tensor_scalar(p1, self.tanh[:], 0.5, 0.5, ALU.mult, ALU.add).then_inc(self.op_done, 1)
        dve.tensor_scalar(p2, self.tanh[:], -0.5, 0.5, ALU.mult, ALU.add).then_inc(self.op_done, 1)

    def weigh(self, dve, g):
        dve.wait_ge(self.op_done, self.ops * g + 6)
        dve.tensor_tensor(self.first, self.first, self.wide(self.p1), ALU.mult).then_inc(self.op_done, 1)
        dve.tensor_tensor(self.second, self.second, self.wide(self.p2), ALU.mult).then_inc(self.op_done, 1)
        dve.wait_ge(self.op_done, self.ops * g + 8)
        dve.tensor_tensor(self.weights[:], self.first, self.second, ALU.add).then_inc(self.op_done, 1)


def mixture_of_layer0(nc, sb, psum, sem, c, X):
    ln = LayerNorm("b", sb, sem, c, X)
    top = TopTwo("b", sb, sem, c, E0, True)
    xnT = sb("b_xnT", [D, GW], F32)
    q = sb("b_q", [P, GT, E0], F32)
    q_anchor = sb("b_q_anchor", [P, GT, E0, E0], F32)
    dot = sb("b_dot", [P, GT, E0], F32)
    w_rest = sb("b_w_rest", [P, GT, E0], F32)
    w_parts = sb("b_w_parts", [P, GT, 3, E0], BF16)
    w_rows = sb("b_w_rows", [3 * E0, GW], BF16)
    hidden = [sb(f"b_hidden{i}", [P, C0, GW], F32) for i in range(2)]
    weighted = [sb(f"b_weighted{i}", [P, C0, GW], F32) for i in range(2)]

    tr, z, w_bank, y = (psum(f"b_{n}_bank", [P, 512], F32) for n in ("tr", "z", "w", "y"))
    h_bank = [psum(f"b_h{i}", [P, 512], F32) for i in range(2)]
    spread = [psum(f"b_spread{i}", [P, 512], F32) for i in range(2)]
    w_rows_ps = w_bank[0:3 * E0, 0:GW // 2].bitcast(BF16)

    xn_transposed, xT_ready = sem("b_xn_transposed"), sem("b_xT_ready")
    z_mm, q_ready, dot_step, parts_step = sem("b_z_mm"), sem("b_q_ready"), sem("b_dot_step"), sem("b_parts_step")
    w_mm, w_ready, h_mm, gelu_done = sem("b_w_mm"), sem("b_w_ready"), sem("b_h_mm"), sem("b_gelu_done")
    spread_mm, weighted_ready, y_mm, x_updated = sem("b_spread_mm"), sem("b_weighted"), sem("b_y_mm"), sem("b_x_updated")
    LAG = 3

    with nc.Block() as block:
        @block.gpsimd
        def _(pool):
            def step(g, par):
                n = group_now(g, -2)
                if n is not None:
                    ln.deviation(pool, n)

            ln.deviation(pool, 0)
            ln.deviation(pool, 1)
            group_steps(pool, LAG, step)

        @block.vector
        def _(dve):
            def route(n):
                dve.wait_ge(q_ready, n + 1)
                dve.tensor_tensor(q_anchor[:], q[:].unsqueeze(2).broadcast_to([P, GT, E0, E0]),
                                  c.anchors[:].unsqueeze(1).broadcast_to([P, GT, E0, E0]), ALU.mult).then_inc(dot_step, 1)
                dve.wait_ge(dot_step, 3 * n + 1)
                dve.reduce_sum(dot[:], q_anchor[:], AX_X).then_inc(dot_step, 1)
                dve.wait_ge(dot_step, 3 * n + 2)
                dve.tensor_scalar(top.logits[:, :, 0:E0], dot[:], float(E0), c.half_over_temp[:, 1:2], ALU.subtract,
                                  ALU.mult).then_inc(dot_step, 1)
                wait_alone(dve, dot_step, 3 * n + 3)
                top.choose(dve, n)

            def split(n):
                dve.wait_ge(top.op_done, top.ops * n + top.ops)
                if not static(n) or n >= 1:
                    dve.wait_ge(w_mm, n)
                dve.tensor_copy(w_parts[:, :, 0, :], top.weights[:]).then_inc(parts_step, 1)
                dve.wait_ge(parts_step, 4 * n + 1)
                dve.tensor_tensor(w_rest[:], top.weights[:], w_parts[:, :, 0, :], ALU.subtract).then_inc(parts_step, 1)
                dve.wait_ge(parts_step, 4 * n + 2)
                dve.tensor_copy(w_parts[:, :, 1, :], w_rest[:]).then_inc(parts_step, 1)
                dve.wait_ge(parts_step, 4 * n + 3)
                dve.tensor_tensor(w_parts[:, :, 2, :], w_rest[:], w_parts[:, :, 1, :],
                                  ALU.subtract).then_inc(parts_step, 1)

            def step(g, par):
                n = group_now(g, -1)
                if n is not None:
                    ln.rows(dve, n, xn_transposed)
                n = group_now(g, 1)
                if n is not None:
                    route(n)
                n = group_now(g, 2)
                if n is not None:
                    for k in range(C0):
                        dve.wait_ge(spread_mm, C0 * n + k + 1)
                        dve.wait_ge(gelu_done, C0 * n + k + 1)
                        if k == 0 and (not static(n) or n >= 2):
                            dve.wait_ge(y_mm, n - 1)
                        dve.tensor_tensor(weighted[par][:, k, :], hidden[par][:, k, :], spread[(C0 * par + k) % 2][:],
                                          ALU.mult).then_inc(weighted_ready, 1)
                n = group_now(g, 1)
                if n is not None:
                    top.shares(dve, n, top.p1[:], top.p2[:])
                    top.weigh(dve, n)
                    split(n)
                n = group_now(g, -2)
                if n is not None:
                    ln.statistics(dve, n)
                n = group_now(g, 3)
                if n is not None:
                    dve.wait_ge(y_mm, n + 1)
                    dve.tensor_tensor(X[:, bass.ts(n, GT), :], y[:].rearrange("p (t d) -> p t d", t=GT),
                                      X[:, bass.ts(n, GT), :], ALU.add).then_inc(x_updated, 1)

            top.set_up(dve)
            ln.statistics(dve, 0)
            ln.rows(dve, 0, xn_transposed)
            ln.statistics(dve, 1)
            group_steps(dve, LAG, step)

        @block.scalar
        def _(act):
            def step(g, par):
                n = group_now(g, 2)
                if n is not None:
                    act.wait_ge(w_mm, n + 1)
                    if not static(n) or n >= 1:
                        act.wait_ge(spread_mm, C0 * n)
                    act.copy(w_rows[:], w_rows_ps).then_inc(w_ready, 1)
                n = group_now(g, 1)
                if n is not None:
                    act.wait_ge(z_mm, n + 1)
                    if not static(n) or n >= 1:
                        act.wait_ge(dot_step, 3 * n)
                    act.activation(q[:].rearrange("p t e -> p (t e)"), z[:, 0:GT * E0], ACT.Tanh,
                                   scale=1.0 / QUANT_TEMP).then_inc(q_ready, 1)
                    for k in range(C0):
                        act.wait_ge(h_mm, C0 * n + k + 1)
                        if k == 0 and (not static(n) or n >= 2):
                            act.wait_ge(weighted_ready, C0 * (n - 1))
                        act.activation(hidden[1 - par][:, k, :], h_bank[(C0 * (1 - par) + k) % 2][:],
                                       ACT.Gelu_apprx_tanh).then_inc(gelu_done, 1)
                    top.gap_tanh(act, n)
                n = group_now(g, 0)
                if n is not None:
                    act.wait_ge(xn_transposed, n + 1)
                    if not static(n) or n >= 1:
                        act.wait_ge(h_mm, C0 * n)
                    act.copy(xnT[:], tr[:]).then_inc(xT_ready, 1)

            group_steps(act, LAG, step)

        @block.tensor
        def _(pe):
            def spread_weights(n, par, k):
                if C0 * par + k >= 2 or not static(n) or n >= 2:
                    pe.wait_ge(weighted_ready, C0 * n + k - 1)
                pe.matmul(spread[(C0 * par + k) % 2][:], c.expert_cols[:, k, :], w_rows[:],
                          start=True, stop=True).then_inc(spread_mm, 1)

            def step(g, par):
                n = group_now(g, 0)
                if n is not None:
                    pe.wait_ge(ln.xn_ready, n + 1)
                    if not static(n) or n >= 1:
                        pe.wait_ge(xT_ready, n)
                    for j in range(GT):
                        last = pe.transpose(tr[:, bass.ts(j, P)], ln.xn[:, j, :], c.ident[:])
                    last.then_inc(xn_transposed, 1)
                n = group_now(g, 2)
                if n is not None:
                    pe.wait_ge(parts_step, 4 * n + 4)
                    if not static(n) or n >= 1:
                        pe.wait_ge(w_ready, n)
                    for j in range(GT):
                        last = pe.transpose(w_rows_ps[:, bass.ts(j, P)], w_parts[:, j].rearrange("p a e -> p (a e)"),
                                            c.ident_bf[:])
                    last.then_inc(w_mm, 1)
                n = group_now(g, 1)
                if n is not None:
                    pe.wait_ge(xT_ready, n + 1)
                    if not static(n) or n >= 1:
                        pe.wait_ge(q_ready, n)
                    for j in range(GT):
                        last = pe.matmul(z[:, bass.ts(j, E0)], xnT[:, bass.ts(j, P)], c.w_route0[:], start=True, stop=True)
                    last.then_inc(z_mm, 1)
                    for k in range(C0):
                        if C0 * (1 - par) + k >= 2 or not static(n) or n >= 2:
                            pe.wait_ge(gelu_done, C0 * n + k - 1)
                        pe.matmul(h_bank[(C0 * (1 - par) + k) % 2][:], c.w1_0[:, 2 * k:2 * k + 2, :].rearrange("d e h -> d (e h)"),
                                  xnT[:], start=True, stop=True).then_inc(h_mm, 1)
                n = group_now(g, 2)
                if n is not None:
                    pe.wait_ge(w_ready, n + 1)
                    spread_weights(n, par, 0)
                    spread_weights(n, par, 1)
                m = group_now(g, 3)
                if m is not None:
                    pe.wait_ge(weighted_ready, C0 * m + C0)
                    if not static(m) or m >= 1:
                        pe.wait_ge(x_updated, m)
                    for j in range(GT):
                        for k in range(C0):
                            last = pe.matmul(y[:, bass.ts(j, P)], weighted[1 - par][:, k, bass.ts(j, P)], c.w2_0[:, k, :],
                                             start=(k == 0), stop=(k == C0 - 1))
                    last.then_inc(y_mm, 1)
                if n is not None:
                    spread_weights(n, par, 2)

            group_steps(pe, LAG, step)


class Dispatch:

    def __init__(self, nc, sb, sem):
        self.rows = nc.dram_tensor("sorted_rows", (E1 * REGION + DUMMY_TILES * TP, ROW), F32).ap()
        self.next_row = sb("next_row", [P, E1], F32)
        self.fill = sb("fill", [P, E1 + DUMMY_TILES, 2, ROW], F32)
        self.tokens = sb("tokens", [P, TILES], F32)
        self.sent = [sem(f"sent{i}") for i in range(2)]
        self.x_stored = sem("x_stored")


def attention_and_routing_of_layer1(nc, sb, psum, sem, c, a, X, dispatch, out):
    ln = LayerNorm("c", sb, sem, c, X)
    ctx_in = [sb(f"c_ctx{i}", [P, GT, DC], F32) for i in range(2)]
    xnT = sb("c_xnT", [D, GW], F32)
    ctxT = sb("c_ctxT", [DC, GW], F32)
    qT = sb("c_qT", [D, GW], F32)
    kT = sb("c_kT", [D, GW], F32)
    neg_max = sb("c_neg_max", [P, GT], F32)
    shifted = sb("c_shifted", [P, GT, S], F32)
    probs = c.probs1
    probsT = sb("c_probsT", [P, GT, P], F32)
    values = c.values1
    rec = sb("c_rec", [P, GT], F32)

    tr, q_bank, k_bank, v_bank, s_bank, pT_bank = (psum(f"c_{n}_bank", [P, 512], F32) for n in ("tr", "q", "k", "v", "s", "pT"))
    out_bank = psum("c_out_bank", [P, 2, 512], F32)
    outs = [out_bank[:, j // 2, (D + 1) * (j % 2):(D + 1) * (j % 2 + 1)] for j in range(GT)]

    loaded = [sem(f"c_loaded{i}") for i in range(2)]
    xn_transposed, xT_ready = sem("c_xn_transposed"), sem("c_xT_ready")
    ctx_transposed, ctxT_ready = sem("c_ctx_transposed"), sem("c_ctxT_ready")
    q_mm, k_mm, v_mm = sem("c_q_mm"), sem("c_k_mm"), sem("c_v_mm")
    q_ready, k_ready, v_ready = sem("c_q_ready"), sem("c_k_ready"), sem("c_v_ready")
    s_mm, max_done, shifted_ready, exp_done = sem("c_s_mm"), sem("c_max_done"), sem("c_shifted"), sem("c_exp_done")
    pT_mm, pT_ready, out_mm = sem("c_pT_mm"), sem("c_pT_ready"), sem("c_out_mm")
    rec_done, x_updated = sem("c_rec_done"), sem("c_x_updated")
    ln2 = LayerNorm("r", sb, sem, c, X, own_rows=False)
    top = TopTwo("r", sb, sem, c, E1, False)
    send = [[sb(f"r_send{i}_{k}", [P, GT, ROW], F32) for k in range(2)] for i in range(2)]
    xrT = sb("r_xrT", [D, GW], F32)
    chosen = sb("r_chosen", [P, GT + 1, E1], BF16)
    place = sb("r_place", [P, GT, E1], F32)
    picked = sb("r_picked", [P, 2, GT, E1], F32)
    slot_f = sb("r_slot_f", [P, 2, GT], F32)
    slots = [sb(f"r_slots{i}", [P, 2, GT], U32) for i in range(2)]
    z = out_bank[:, 0, 2 * (D + 1):2 * (D + 1) + GT * E1]
    ranks = out_bank[:, 1, 2 * (D + 1):2 * (D + 1) + (GT + 1) * E1]
    xr_transposed, xrT_ready, second_row_ready = sem("r_xr_transposed"), sem("r_xrT_ready"), sem("r_second_row")
    z_mm, z_read, chosen_ready, ranks_mm, place_step = (sem(f"r_{n}") for n in ("z_mm", "z_read", "chosen", "ranks_mm", "place_step"))
    set_up, next_row_done = sem("r_set_up"), sem("r_next_row")
    PLACE_STEPS = 5
    LAG = 5

    with nc.Block() as block:
        @block.sync
        def _(sp):
            def load(g, par):
                if not static(g) or g >= 2:
                    sp.wait_ge(ctx_transposed, g - 1)
                sp.dma_start(ctx_in[par][:],
                             a["ctx_768"].rearrange("(t b) s d -> (b s) t d", b=2)[:, bass.ts(g, GT), :]).then_inc(loaded[par], 16)

            def store(g):
                sp.wait_ge(x_updated, g + 1)
                sp.dma_start(out[0:B * S, :].rearrange("(t p) d -> p t d", p=P)[:, bass.ts(g, GT), :],
                             X[:, bass.ts(g, GT), :]).then_inc(dispatch.x_stored, 16)

            load(0, 0)
            load(1, 1)
            with sp.Fori(1, G // 2) as i:
                load(i * 2, 0)
                load(i * 2 + 1, 1)
                store(i * 2 - 2)
                store(i * 2 - 1)
            store(G - 2)
            store(G - 1)
            for k in range(2):
                sp.wait_ge(dispatch.sent[k], 16 * 2 * GT * (G // 2))
            sp.wait_ge(dispatch.x_stored, 16 * G)

        @block.gpsimd
        def _(pool):
            def scatter(n, par, ks):
                if ks[0] == 0:
                    pool.wait_ge(second_row_ready, n + 1)
                    wait_alone(pool, place_step, PLACE_STEPS * n + PLACE_STEPS)
                for k in ks:
                    for j in range(GT):
                        pool.indirect_dma_start(dispatch.rows, bass.IndirectOffsetOnAxis(ap=slots[par][:, k, j:j + 1], axis=0),
                                                send[par][k][:, j, :], None).then_inc(dispatch.sent[par], 16)

            def step(g, par):
                n = group_now(g, 5)
                if n is not None:
                    scatter(n, 1 - par, (0, 1))
                n = group_now(g, 3)
                if n is not None:
                    ln2.deviation(pool, n)
                n = group_now(g, -2)
                if n is not None:
                    ln.deviation(pool, n)

            pool.memset(chosen[:].rearrange("p t e -> p (t e)"), 0.0).then_inc(set_up, 1)
            ln.deviation(pool, 0)
            ln.deviation(pool, 1)
            group_steps(pool, LAG, step)

        @block.vector
        def _(dve):
            def places(r, par):
                dve.wait_ge(ranks_mm, r + 1)
                dve.wait_ge(next_row_done, r + 1)
                dve.tensor_tensor(place[:], ranks[:, 0:GT * E1].rearrange("p (t e) -> p t e", e=E1),
                                  dispatch.next_row[:].unsqueeze(1).broadcast_to([P, GT, E1]), ALU.add).then_inc(place_step, 1)
                dve.wait_ge(place_step, PLACE_STEPS * r + 1)
                dve.tensor_tensor(dispatch.next_row[:], dispatch.next_row[:], ranks[:, GT * E1:(GT + 1) * E1],
                                  ALU.add).then_inc(next_row_done, 1)
                dve.tensor_tensor(picked[:], top.picks[:], place[:].unsqueeze(1).broadcast_to([P, 2, GT, E1]),
                                  ALU.mult).then_inc(place_step, 1)
                dve.wait_ge(place_step, PLACE_STEPS * r + 2)
                dve.tensor_reduce(slot_f[:], picked[:], AX_X, ALU.add).then_inc(place_step, 1)
                dve.wait_ge(place_step, PLACE_STEPS * r + 3)
                dve.tensor_copy(slots[par][:], slot_f[:]).then_inc(place_step, 1)
                dve.wait_ge(place_step, PLACE_STEPS * r + 4)
                dve.wait_ge(top.op_done, top.ops * r + top.ops)
                dve.wait_ge(next_row_done, r + 2)
                dve.sem_inc(place_step, 1)

            def step(g, par):
                n = group_now(g, 2)
                if n is not None:
                    dve.wait_ge(s_mm, n + 1)
                    dve.tensor_reduce(neg_max[:], s_bank[:, 0:GT * S].rearrange("p (t k) -> p t k", k=S), AX_X, ALU.max,
                                      negate=True).then_inc(max_done, 1)
                    dve.wait_ge(max_done, n + 1)
                    if not static(n) or n >= 1:
                        dve.wait_ge(exp_done, n)
                    dve.tensor_tensor(shifted[:], s_bank[:, 0:GT * S].rearrange("p (t k) -> p t k", k=S),
                                      neg_max[:].unsqueeze(2).broadcast_to([P, GT, S]), ALU.add).then_inc(shifted_ready, 1)
                n = group_now(g, 3)
                if n is not None:
                    dve.wait_ge(x_updated, n + 1)
                    ln2.statistics(dve, n)
                n = group_now(g, -1)
                if n is not None:
                    ln.rows(dve, n, xn_transposed)
                r = group_now(g, 4)
                if r is not None:
                    dve.wait_ge(z_mm, r + 1)
                    if not static(r) or r >= 1:
                        dve.wait_ge(place_step, PLACE_STEPS * r)
                    dve.tensor_copy(top.logits[:].rearrange("p t e -> p (t e)"), z).then_inc(z_read, 1)
                    wait_alone(dve, z_read, r + 1)
                    top.choose(dve, r)
                    if not static(r) or r >= 1:
                        dve.wait_ge(ranks_mm, r)
                    if static(r) and r == 0:
                        dve.wait_ge(set_up, 1)
                    dve.tensor_tensor(chosen[:, 0:GT, :], top.first, top.second, ALU.add).then_inc(chosen_ready, 1)
                n = group_now(g, 1)
                if n is not None:
                    dve.wait_ge(v_mm, n + 1)
                    if not static(n) or n >= 2:
                        dve.wait_ge(out_mm, n - 1)
                    dve.tensor_tensor(values[1 - par][:, :, 0:D], v_bank[:].rearrange("p (t d) -> p t d", t=GT),
                                      c.out_bias1[:].unsqueeze(1).broadcast_to([P, GT, D]), ALU.add).then_inc(v_ready, 1)
                n = group_now(g, -2)
                if n is not None:
                    ln.statistics(dve, n)
                if r is not None:
                    top.shares(dve, r, send[par][0][:, :, D + 1], send[par][1][:, :, D + 1])
                    places(r, par)
                n = group_now(g, 2)
                if n is not None:
                    dve.wait_ge(out_mm, n + 1)
                    dve.reciprocal(rec[:].rearrange("p (a b) -> p a b", a=2),
                                   out_bank[:, :, D:2 * (D + 1):D + 1]).then_inc(rec_done, 1)
                    dve.wait_ge(rec_done, n + 1)
                    for j in range(GT):
                        last = dve.scalar_tensor_tensor(out=X[:, n * GT + j, :], in0=outs[j][:, 0:D], scalar=rec[:, j:j + 1],
                                                        in1=X[:, n * GT + j, :], op0=ALU.mult, op1=ALU.add)
                    last.then_inc(x_updated, 1)
                n = group_now(g, 3)
                if n is not None:
                    dve.wait_ge(ln2.rstd_step, 2 * n + 2)
                    if not static(n) or n >= 2:
                        dve.wait_ge(dispatch.sent[1 - par], 16 * 2 * GT * ((n + par - 1) // 2))
                    for k in range(2):
                        dve.tensor_copy(send[1 - par][k][:, :, D], dispatch.tokens[:, bass.ts(n, GT)])
                    ln2.normalise(dve, n, send[1 - par][0])

            dve.tensor_copy(dispatch.next_row[:], c.first_row[:]).then_inc(next_row_done, 1)
            ln.statistics(dve, 0)
            ln.rows(dve, 0, xn_transposed)
            ln.statistics(dve, 1)
            group_steps(dve, LAG, step)

        @block.scalar
        def _(act):
            def step(g, par):
                r = group_now(g, 4)
                if r is not None:
                    act.wait_ge(ln2.xn_ready, r + 1)
                    act.copy(send[par][1][:, :, 0:D], send[par][0][:, :, 0:D]).then_inc(second_row_ready, 1)
                    act.wait_ge(xr_transposed, r + 1)
                    if not static(r) or r >= 1:
                        act.wait_ge(z_mm, r)
                    act.copy(xrT[:], tr[:]).then_inc(xrT_ready, 1)
                n = group_now(g, 2)
                if n is not None:
                    act.wait_ge(shifted_ready, n + 1)
                    if not static(n) or n >= 1:
                        act.wait_ge(pT_mm, n)
                    for b in range(2):
                        half = slice(S * b, S * b + S)
                        last = act.activation(probs[half, :, half], shifted[half], ACT.Exp, scale=SCALE1)
                    last.then_inc(exp_done, 1)
                m = group_now(g, 1)
                if m is not None:
                    act.wait_ge(q_mm, m + 1)
                    if not static(m) or m >= 1:
                        act.wait_ge(s_mm, m)
                    act.activation(qT[:], q_bank[:], ACT.Identity, bias=c.bq1[:, 0:1]).then_inc(q_ready, 1)
                w = group_now(g, 0)
                if w is not None:
                    act.wait_ge(xn_transposed, w + 1)
                    if not static(w) or w >= 1:
                        act.wait_ge(q_mm, w)
                    act.copy(xnT[:], tr[:]).then_inc(xT_ready, 1)
                if m is not None:
                    act.wait_ge(k_mm, m + 1)
                    act.activation(kT[:], k_bank[:], ACT.Identity, bias=c.bk1[:, 0:1]).then_inc(k_ready, 1)
                if r is not None:
                    top.gap_tanh(act, r)
                if n is not None:
                    act.wait_ge(pT_mm, n + 1)
                    if not static(n) or n >= 1:
                        act.wait_ge(out_mm, n)
                    act.copy(probsT[:].rearrange("p t q -> p (t q)"), pT_bank[:]).then_inc(pT_ready, 1)
                if w is not None:
                    act.wait_ge(ctx_transposed, w + 1)
                    if not static(w) or w >= 1:
                        act.wait_ge(v_mm, w)
                    act.copy(ctxT[:], tr[0:DC, :]).then_inc(ctxT_ready, 1)

            group_steps(act, LAG, step)

        @block.tensor
        def _(pe):
            def step(g, par):
                r = group_now(g, 4)
                if r is not None:
                    pe.wait_ge(ln2.xn_ready, r + 1)
                    pe.wait_ge(ctxT_ready, min(g, G) if static(g) else g)
                    if static(g) and g > G:
                        pe.wait_ge(xrT_ready, r)
                    for j in range(GT):
                        last = pe.transpose(tr[:, bass.ts(j, P)], send[par][0][:, j, 0:D], c.ident[:])
                    last.then_inc(xr_transposed, 1)
                n = group_now(g, 2)
                if n is not None:
                    pe.wait_ge(q_ready, n + 1)
                    pe.wait_ge(k_ready, n + 1)
                    if not static(n) or n >= 1:
                        pe.wait_ge(shifted_ready, n)
                    for j in range(GT):
                        for b in range(2):
                            cols = bass.ts(2 * j + b, S)
                            last = pe.matmul(s_bank[S * b:S * b + S, bass.ts(j, S)], qT[:, cols], kT[:, cols],
                                             start=True, stop=True)
                    last.then_inc(s_mm, 1)
                w = group_now(g, 0)
                if w is not None:
                    pe.wait_ge(ln.xn_ready, w + 1)
                    if r is not None:
                        pe.wait_ge(xrT_ready, r + 1)
                    elif w >= 1:
                        pe.wait_ge(ctxT_ready, w)
                    for j in range(GT):
                        last = pe.transpose(tr[:, bass.ts(j, P)], ln.xn[:, j, :], c.ident[:])
                    last.then_inc(xn_transposed, 1)
                if r is not None:
                    pe.wait_ge(xrT_ready, r + 1)
                    pe.wait_ge(x_updated, min(g - 2, G) if static(g) else g - 2)
                    if not static(r) or r >= 1:
                        pe.wait_ge(place_step, PLACE_STEPS * r)
                    for j in range(GT):
                        last = pe.matmul(z[:, bass.ts(j, E1)], xrT[:, bass.ts(j, P)], c.w_route1[:], start=True, stop=True)
                    last.then_inc(z_mm, 1)
                m = group_now(g, 1)
                if m is not None:
                    pe.wait_ge(xT_ready, m + 1)
                    if not static(m) or m >= 1:
                        pe.wait_ge(q_ready, m)
                        pe.wait_ge(k_ready, m)
                        pe.wait_ge(v_ready, m)
                    pe.matmul(q_bank[:], c.wq1[:], xnT[:], start=True, stop=True).then_inc(q_mm, 1)
                    pe.wait_ge(ctxT_ready, m + 1)
                    pe.matmul(k_bank[:], c.wk1[:], ctxT[:], start=True, stop=True).then_inc(k_mm, 1)
                    for j in range(GT):
                        last = pe.matmul(v_bank[:, bass.ts(j, P)], ctxT[:, bass.ts(j, P)], c.wv1[:], start=True, stop=True)
                    last.then_inc(v_mm, 1)
                if n is not None:
                    pe.wait_ge(exp_done, n + 1)
                    if not static(n) or n >= 1:
                        pe.wait_ge(pT_ready, n)
                    for j in range(GT):
                        last = pe.transpose(pT_bank[:, bass.ts(j, P)], probs[:, j, :], c.ident[:])
                    last.then_inc(pT_mm, 1)
                if w is not None:
                    pe.wait_ge(xT_ready, w + 1)
                    pe.wait_ge(loaded[par], 16 * ((w - par) // 2) + 16)
                    for j in range(GT):
                        last = pe.transpose(tr[0:DC, bass.ts(j, P)], ctx_in[par][:, j, :], c.ident[:])
                    last.then_inc(ctx_transposed, 1)
                if r is not None:
                    pe.wait_ge(chosen_ready, r + 1)
                    pe.matmul(ranks, c.earlier[:], chosen[:].rearrange("p t e -> p (t e)"), start=True, stop=False,
                              skip_group_check=True)
                    for j in range(GT):
                        last = pe.matmul(ranks[:, (j + 1) * E1:(GT + 1) * E1], c.ones_bf[:],
                                         chosen[:, j, :].unsqueeze(1).broadcast_to([P, GT - j, E1]), start=False,
                                         stop=(j == GT - 1), skip_group_check=True)
                    last.then_inc(ranks_mm, 1)
                if n is not None:
                    pe.wait_ge(pT_ready, n + 1)
                    pe.wait_ge(v_ready, n + 1)
                    if r is not None:
                        pe.wait_ge(place_step, PLACE_STEPS * r + PLACE_STEPS)
                    if not static(n) or n >= 1:
                        pe.wait_ge(x_updated, n)
                    for j in range(GT):
                        last = pe.matmul(outs[j], probsT[:, j, :], values[par][:, j, :], start=True, stop=True)
                    last.then_inc(out_mm, 1)

            group_steps(pe, LAG, step)




def tile_steps(eng, lag, step):
    for t in range(4):
        step(t, t)
    with eng.Fori(1, DTILES // 4) as i:
        for u in range(4):
            step(i * 4 + u, u)
    for t in range(DTILES // 4 * 4, DTILES + lag):
        step(t, t % 4)


def pair_tile(t, lag):
    return None if static(t) and not 0 <= t - lag < DTILES else t - lag


def mixture_of_layer1(nc, sb, psum, sem, c, dispatch, out):
    KH = HID1 // P
    HT = TP // P
    count = sb("d_count", [1, E1], F32)
    over = sb("d_over", [1, E1, MAX_TILES], F32)
    tiles = sb("d_tiles", [1, E1], F32)
    upto = sb("d_upto", [1, E1, E1], F32)
    ends = sb("d_ends", [1, E1], F32)
    past = sb("d_past", [1, DTILES, E1], F32)
    expert = sb("d_expert", [1, DTILES], F32)
    past_tiles = sb("d_past_tiles", [1, DTILES, E1], F32)
    start = sb("d_start", [1, DTILES], F32)
    start_i = sb("d_start_i", [1, DTILES], I32)
    half_i = sb("d_half_i", [1, DTILES], I32)
    half = sb("d_half", [1, DTILES], F32)
    first_f = sb("d_first_f", [1, DTILES], F32)
    waits_f = sb("d_waits_f", [1, 2, DTILES], F32)
    end_row = sb("d_end_row", [1, E1], I32)
    tile_expert = sb("d_tile_expert", [1, DTILES], I32)
    tile_row = sb("d_tile_row", [1, DTILES], I32)
    tile_waits = sb("d_tile_waits", [1, 2, DTILES], I32)

    rows = [sb(f"d_rows{i}", [P, HT, ROW], F32) for i in range(4)]
    xT = [sb(f"d_xT{i}", [D, TP], F32) for i in range(2)]
    w12 = [sb(f"d_w12_{i}", [D, 2 * HID1], F32) for i in range(2)]
    w3 = [sb(f"d_w3_{i}", [P, HID1 // P * D], F32) for i in range(2)]
    silu = [sb(f"d_silu{i}", [P, KH * TP], F32) for i in range(2)]
    hidden = [sb(f"d_hidden{i}", [P, KH, TP], F32) for i in range(2)]
    shares = [sb(f"d_y{i}", [P, HT, D], F32) for i in range(2)]
    token = [sb(f"d_token{i}", [P, HT], U32) for i in range(2)]

    tr, u_bank, v_bank, y = ([psum(f"d_{n}{i}", [P, 512], F32) for i in range(2)] for n in ("tr", "u", "v", "y_bank"))

    plan_step, plan_ready, filled = sem("d_plan_step"), sem("d_plan_ready"), sem("d_filled")
    loaded = [sem(f"d_loaded{i}") for i in range(4)]
    x_transposed, xT_ready, w12_ready, w3_ready = (sem(f"d_{n}") for n in ("x_transposed", "xT_ready", "w12_ready", "w3_ready"))
    u_mm, v_mm, silu_done, h_ready, y_mm, y_ready = (sem(f"d_{n}") for n in ("u_mm", "v_mm", "silu_done", "h_ready", "y_mm", "y_ready"))
    added = [sem(f"d_added{i}") for i in range(2)]
    LAG = 2

    with nc.Block() as block:
        @block.sync
        def _(sp):
            def load(t, u):
                first = sp.value_load(tile_row[0:1, bass.ds(t, 1)], min_val=0, max_val=E1 * REGION + (DUMMY_TILES - 1) * TP)
                if not static(t) or t >= 4:
                    sp.wait_ge(y_ready, t - 3)
                sp.dma_start(rows[u][:], dispatch.rows[bass.ds(first, TP), :].rearrange("(p h) d -> p h d", h=HT)
                             ).then_inc(loaded[u], 16)

            sp.dma_start(dispatch.rows[E1 * REGION:, :].rearrange("(a p h) d -> p a h d", p=P, h=HT),
                         dispatch.fill[:, E1:]).then_inc(filled, 16)
            sp.wait_ge(plan_ready, 1)
            for e in range(E1):
                end = sp.value_load(end_row[0:1, e:e + 1], min_val=e * REGION, max_val=e * REGION + B * S)
                sp.dma_start(dispatch.rows[bass.ds(end, TP), :].rearrange("(p h) d -> p h d", h=HT),
                             dispatch.fill[:, e]).then_inc(filled, 16)
            sp.wait_ge(filled, 16 * (E1 + 1))
            for t in range(4):
                load(t, t)
            with sp.Fori(1, DTILES // 4) as i:
                for u in range(4):
                    load(i * 4 + u, u)
            for t in range(DTILES // 4 * 4, DTILES):
                load(t, t % 4)

        @block.gpsimd
        def _(pool):
            def add(t, u):
                pool.wait_ge(y_ready, t + 1)
                for k in range(2):
                    before = pool.value_load(tile_waits[0:1, k, bass.ds(t, 1)], min_val=16, max_val=16 + 16 * HT * DTILES)
                    wait_alone(pool, added[k], before)
                for h in range(HT):
                    pool.indirect_dma_start(out, bass.IndirectOffsetOnAxis(ap=token[u % 2][:, h:h + 1], axis=0),
                                            shares[u % 2][:, h, :], None, compute_op=ALU.add).then_inc(added[u % 2], 16)

            def step(t, u):
                w = pair_tile(t, 2)
                if w is not None:
                    add(w, (u + 2) % 4)

            past_rows = out[B * S:, :].rearrange("(a p h) d -> p a h d", p=P, h=HT)
            for h in range(HT):
                pool.dma_start(past_rows[:, :, h], dispatch.fill[:, :, h, 0:D]).then_inc(added[h], 16)
            pool.wait_ge(plan_ready, 1)
            tile_steps(pool, LAG, step)
            pool.wait_ge(added[0], 16 + 16 * HT * (DTILES - DTILES // 2))
            pool.wait_ge(added[1], 16 + 16 * HT * (DTILES // 2))

        @block.vector
        def _(dve):
            steps = [0]

            def then(ins):
                ins.then_inc(plan_step, 1)
                steps[0] += 1
                dve.wait_ge(plan_step, steps[0])

            then(dve.tensor_tensor(count[:], dispatch.next_row[0:1, :], c.first_row[0:1, :], ALU.subtract))
            then(dve.tensor_copy(end_row[:], dispatch.next_row[0:1, :]))
            then(dve.tensor_tensor(over[:], count[:].unsqueeze(2).broadcast_to([1, E1, MAX_TILES]),
                                   c.tile_sizes[:].unsqueeze(1).broadcast_to([1, E1, MAX_TILES]), ALU.is_gt))
            then(dve.tensor_reduce(tiles[:], over[:], AX_X, ALU.add))
            then(dve.tensor_tensor(upto[:], tiles[:].unsqueeze(1).broadcast_to([1, E1, E1]), c.up_to[:], ALU.mult))
            then(dve.tensor_reduce(ends[:], upto[:], AX_X, ALU.add))
            then(dve.tensor_tensor(past[:], c.tile_number[:].unsqueeze(2).broadcast_to([1, DTILES, E1]),
                                   ends[:].unsqueeze(1).broadcast_to([1, DTILES, E1]), ALU.is_ge))
            then(dve.tensor_reduce(expert[:], past[:], AX_X, ALU.add))
            then(dve.tensor_tensor(past_tiles[:], past[:], tiles[:].unsqueeze(1).broadcast_to([1, DTILES, E1]), ALU.mult))
            then(dve.tensor_reduce(start[:], past_tiles[:], AX_X, ALU.add))
            then(dve.tensor_copy(start_i[:], start[:]))
            then(dve.tensor_single_scalar(half_i[:], start_i[:], 1, op=ALU.arith_shift_right))
            then(dve.tensor_copy(half[:], half_i[:]))
            then(dve.tensor_tensor(waits_f[:, 0], start[:], half[:], ALU.subtract))
            then(dve.tensor_copy(waits_f[:, 1], half[:]))
            then(dve.tensor_tensor(first_f[:], c.tile_number[:], start[:], ALU.subtract))
            then(dve.tensor_scalar(first_f[:], first_f[:], float(TP), None, ALU.mult))
            then(dve.scalar_tensor_tensor(out=first_f[:], in0=expert[:], scalar=float(REGION), in1=first_f[:],
                                          op0=ALU.mult, op1=ALU.add))
            then(dve.tensor_copy(tile_row[:], first_f[:]))
            then(dve.tensor_scalar(tile_expert[:], expert[:], float(E1 - 1), None, ALU.min))
            then(dve.tensor_scalar(tile_waits[:], waits_f[:], 16.0 * HT, 16.0, ALU.mult, ALU.add))
            dve.sem_inc(plan_ready, 1)

            def step(t, u):
                n = pair_tile(t, 0)
                if n is not None:
                    dve.wait_ge(x_transposed, n + 1)
                    if not static(n) or n >= 2:
                        dve.wait_ge(v_mm, n - 1)
                    dve.tensor_copy(xT[u % 2][:], tr[u % 2][:, 0:TP]).then_inc(xT_ready, 1)
                m = pair_tile(t, 1)
                if m is not None:
                    dve.wait_ge(silu_done, m + 1)
                    dve.wait_ge(v_mm, m + 1)
                    if not static(m) or m >= 2:
                        dve.wait_ge(y_mm, m - 1)
                    dve.tensor_tensor(hidden[1 - u % 2][:].rearrange("p k n -> p (k n)"), silu[1 - u % 2][:],
                                      v_bank[1 - u % 2][:], ALU.mult).then_inc(h_ready, 1)
                w = pair_tile(t, 2)
                if w is not None:
                    row = rows[(u + 2) % 4]
                    dve.wait_ge(added[u % 2], 16 + 16 * HT * ((w - u % 2) // 2))
                    dve.tensor_copy(token[u % 2][:], row[:, :, D])
                    dve.wait_ge(y_mm, w + 1)
                    for h in range(HT):
                        last = dve.tensor_scalar(shares[u % 2][:, h, :], y[u % 2][:, bass.ts(h, D)], row[:, h, D + 1:D + 2], None,
                                                 ALU.mult)
                    last.then_inc(y_ready, 1)

            tile_steps(dve, LAG, step)

        @block.scalar
        def _(act):
            def step(t, u):
                n, m = pair_tile(t, 0), pair_tile(t, 1)
                if n is not None:
                    e = act.value_load(tile_expert[0:1, bass.ds(n, 1)], min_val=0, max_val=E1 - 1)
                    if not static(n) or n >= 2:
                        act.wait_ge(v_mm, n - 1)
                    act.copy(w12[u % 2][:], c.w12[:, bass.ds(e, 1)].rearrange("d a i h -> d (a i h)")).then_inc(w12_ready, 1)
                if m is not None:
                    act.wait_ge(u_mm, m + 1)
                    if not static(m) or m >= 2:
                        act.wait_ge(h_ready, m - 1)
                    act.activation(silu[1 - u % 2][:], u_bank[1 - u % 2][:], ACT.Silu).then_inc(silu_done, 1)
                    e = act.value_load(tile_expert[0:1, bass.ds(m, 1)], min_val=0, max_val=E1 - 1)
                    if not static(m) or m >= 2:
                        act.wait_ge(y_mm, m - 1)
                    act.copy(w3[1 - u % 2][:], c.w3[:, bass.ds(e, 1)].rearrange("p a b d -> p (a b d)")).then_inc(w3_ready, 1)

            act.wait_ge(plan_ready, 1)
            tile_steps(act, LAG, step)

        @block.tensor
        def _(pe):
            def step(t, u):
                n = pair_tile(t, 0)
                m = pair_tile(t, 1)
                if m is not None:
                    q = 1 - u % 2
                    pe.wait_ge(xT_ready, m + 1)
                    pe.wait_ge(w12_ready, m + 1)
                    for i, (bank, mm, done) in enumerate(((u_bank, u_mm, silu_done), (v_bank, v_mm, h_ready))):
                        if not static(m) or m >= 2:
                            pe.wait_ge(done, m - 1)
                        for k in range(KH):
                            last = pe.matmul(bank[q][:, bass.ts(k, TP)], w12[q][:, i * HID1 + k * P:i * HID1 + k * P + P],
                                             xT[q][:], start=True, stop=True)
                        last.then_inc(mm, 1)
                if n is not None:
                    pe.wait_ge(loaded[u], 16 * ((n - u) // 4) + 16)
                    if not static(n) or n >= 2:
                        pe.wait_ge(xT_ready, n - 1)
                    for h in range(HT):
                        last = pe.transpose(tr[u % 2][:, bass.ts(h, P)], rows[u][:, h, 0:D], c.ident[:])
                    last.then_inc(x_transposed, 1)
                w = pair_tile(t, 2)
                if w is not None:
                    q = u % 2
                    pe.wait_ge(h_ready, w + 1)
                    pe.wait_ge(w3_ready, w + 1)
                    if not static(w) or w >= 2:
                        pe.wait_ge(y_ready, w - 1)
                    for h in range(HT):
                        for k in range(KH):
                            last = pe.matmul(y[q][:, bass.ts(h, D)], hidden[q][:, k, bass.ts(h, P)], w3[q][:, bass.ts(k, D)],
                                             start=(k == 0), stop=(k == KH - 1))
                    last.then_inc(y_mm, 1)

            tile_steps(pe, LAG, step)


def load_x(nc, sem, a, X):
    x_loaded = sem("x_loaded")
    with nc.Block() as block:
        @block.sync
        def _(sp):
            sp.dma_start(X[:], a["x"].rearrange("(t b) s d -> (b s) t d", b=2)).then_inc(x_loaded, 16)
            sp.wait_ge(x_loaded, 16)


def store_x(nc, sem, X, out):
    x_stored = sem("x_kept")
    with nc.Block() as block:
        @block.sync
        def _(sp):
            sp.dma_start(out[0:B * S, :].rearrange("(t p) d -> p t d", p=P), X[:]).then_inc(x_stored, 16)
            sp.wait_ge(x_stored, 16)


def build(nc, a, out, phases="ABCD"):
    with ExitStack() as ctx:
        def sb(name, shape, dt):
            return ctx.enter_context(nc.sbuf_tensor(name, shape, dt))

        def sem(name):
            return ctx.enter_context(nc.semaphore(name))

        X = sb("X", [P, TILES, D], F32)
        c = Shared()
        dispatch = Dispatch(nc, sb, sem)
        with ExitStack() as pctx:
            load_constants(nc, sb, lambda n, s, d: pctx.enter_context(nc.psum_tensor(n, s, d)), sem, c, a, dispatch)
        if "A" not in phases:
            load_x(nc, sem, a, X)
        for name, phase, args in (("A", attention_of_layer0, (c, a, X)), ("B", mixture_of_layer0, (c, X)),
                                  ("C", attention_and_routing_of_layer1, (c, a, X, dispatch, out)),
                                  ("D", mixture_of_layer1, (c, dispatch, out))):
            if name in phases:
                with ExitStack() as own:
                    phase(nc, lambda n, s, d: own.enter_context(nc.sbuf_tensor(n, s, d)),
                          lambda n, s, d: own.enter_context(nc.psum_tensor(n, s, d)),
                          lambda n: own.enter_context(nc.semaphore(n)), *args)
        if "C" not in phases:
            store_x(nc, sem, X, out)


_INS = ["x", "ctx_768", "g_xattn", "g_ffn", "L0_xattn_wq", "L0_xattn_bq", "L0_xattn_wk", "L0_xattn_bk", "L0_xattn_wv",
        "L0_xattn_bv", "L0_xattn_wo", "L0_xattn_bo", "L0_ffn_proj_w", "L0_ffn_anchors", "L0_ffn_routing_temp",
        "L0_ffn_w1", "L0_ffn_w2", "L1_xattn_Wq", "L1_xattn_bq", "L1_xattn_Wk", "L1_xattn_bk", "L1_xattn_Wv",
        "L1_xattn_bv", "L1_ffn_Wg", "L1_ffn_W1", "L1_ffn_W2", "L1_ffn_W3"]


def shape_constants():
    import numpy as np
    part = np.arange(P)
    head_of_group = ((part[:, None] % 32) // DH == np.arange(4)[None, :]).astype(np.float32)
    head_cols = np.tile(np.repeat(np.eye(H, dtype=np.float32), S, axis=1), (2, 1))
    strip_rows = np.zeros((H, SETS, 4, STRIP), np.float32)
    for h in range(H):
        strip_rows[h, h // 8, h // 2 % 4, DH * (h % 2):DH * (h % 2) + DH] = 1.0
    strip_rows = np.tile(strip_rows.reshape(H, SETS * P), (3, 1))
    expert_cols = np.tile(np.repeat(np.eye(E0, dtype=np.float32), HID0, axis=1), (3, 1))
    return {"const_ident": np.eye(P, dtype=np.float32), "const_head_of_group": head_of_group,
            "const_head_cols": head_cols, "const_expert_cols": expert_cols, "const_strip_rows": strip_rows,
            "const_first_row": (np.arange(E1) * REGION).astype(np.float32),
            "const_earlier": np.triu(np.ones((P, P), np.float32), 1),
            "const_fill_tokens": (B * S + np.arange(E1 + DUMMY_TILES)[None, :, None] * TP + 2 * part[:, None, None]
                                  + np.arange(2)).astype(np.float32),
            "const_tokens": (np.arange(TILES)[None, :] * P + part[:, None]).astype(np.float32),
            "const_tile_sizes": (np.arange(MAX_TILES)[None, :] * TP).astype(np.float32),
            "const_up_to": np.tril(np.ones((E1, E1), np.float32))[None],
            "const_tile_number": np.arange(DTILES)[None, :].astype(np.float32),
            "const_expert_number": np.arange(E1).astype(np.float32)}


def kernel(**inputs):
    import numpy as np
    import concourse.bacc as bacc
    from concourse.bass_utils import run_bass_kernel_spmd

    nc = bacc.Bacc("TRN2", target_bir_lowering=False, num_devices=1)
    arrays = {n: np.ascontiguousarray(inputs[n]) for n in _INS}
    arrays["L0_ffn_routing_temp"] = arrays["L0_ffn_routing_temp"].reshape(1)
    arrays.update(shape_constants())
    aps = {n: nc.dram_tensor(f"in_{n}", v.shape, mybir.dt.from_np(v.dtype), kind="ExternalInput").ap()
           for n, v in arrays.items()}
    out = nc.dram_tensor("out_x", (B * S + (E1 + DUMMY_TILES) * TP, D), F32, kind="ExternalOutput").ap()
    build(nc, aps, out)
    r = run_bass_kernel_spmd(nc, [{f"in_{n}": v for n, v in arrays.items()}], core_ids=[0])
    return r.results[0]["out_x"][:B * S].reshape(B, S, D)
```

```python
from contextlib import ExitStack

import concourse.bass as bass
from concourse import mybir

ALU = mybir.AluOpType
ACT = mybir.ActivationFunctionType
F32 = mybir.dt.float32
BF16 = mybir.dt.bfloat16
I32 = mybir.dt.int32
U32 = mybir.dt.uint32
AX_X = mybir.AxisListType.X

P = 128
B, S, D = 128, 64, 128
DC = 96
TILES = B * S // P
GT = 4
G = TILES // GT
GB = GT * P // S
GW = GT * P
H, DH = 16, 8
HU = H // 2
REC = 64
STRIP = 32
E0, HID0 = 6, 64
C0 = E0 * HID0 // P
E1, HID1 = 8, 256
TP = 2 * P
ROW = D + 2
REGION = B * S + TP
MAX_TILES = B * S // TP
DTILES = 2 * B * S // TP + E1 - 1
DUMMY_TILES = E1 - 1
EPS = 1e-5
SCALE0 = float(DH) ** -0.5
SCALE1 = float(D) ** -0.5
QUANT_TEMP = 0.3
FAR = 1e30


def static(t):
    return isinstance(t, int)


def loop_steps(eng, first_static, looped, last, step):
    period = 2 * GT
    for t in range(first_static):
        step(t, t % period, t // GT)
    with eng.Fori(first_static // period, first_static // period + looped) as i:
        for u in range(period):
            step(i * period + u, u, i * 2 + u // GT)
    for t in range(first_static + looped * period, last):
        step(t, t % period, t // GT)


def wait_alone(eng, semaphore, value):
    eng.wait_ge(semaphore, value)
    eng.nop(nofuse=True)


def inverse_deviation(pool, stats, minus_half, rstd, rstd_step, g):
    pool.tensor_scalar(rstd, stats[:, :, 1], EPS, None, ALU.add).then_inc(rstd_step, 1)
    wait_alone(pool, rstd_step, 2 * g + 1)
    pool.tensor_tensor(rstd, rstd, minus_half, ALU.pow).then_inc(rstd_step, 1)


class Shared:
    pass


def load_constants(nc, sb, psum, sem, c, a, X, dispatch):
    c.first_row = sb("first_row", [P, E1], F32)
    c.earlier_f = sb("earlier_f", [P, P], F32)
    c.earlier = sb("earlier", [P, P], BF16)
    c.ones_bf = sb("ones_bf", [P, P], BF16)
    c.fill_tokens = sb("fill_tokens", [P, E1 + DUMMY_TILES, 2], F32)
    c.tile_sizes = sb("tile_sizes", [1, MAX_TILES], F32)
    c.up_to = sb("up_to", [1, E1, E1], F32)
    c.tile_number = sb("tile_number", [1, DTILES], F32)
    c.ctx_in = [sb(f"ctx_in{i}", [P, GT, DC], F32) for i in range(2)]
    c.loaded = [sem(f"loaded{i}") for i in range(2)]
    c.minus_half = sb("minus_half", [P, GT], F32)
    c.ident = sb("ident", [P, P], F32)
    c.ident_bf = sb("ident_bf", [P, P], BF16)
    c.head_of_group = sb("head_of_group", [P, 4], F32)
    c.head_cols_f = sb("head_cols_f", [2 * H, H * S], F32)
    c.head_cols = sb("head_cols", [2 * H, H * S], BF16)
    c.expert_cols_f = sb("expert_cols_f", [3 * E0, C0, P], F32)
    c.expert_cols = sb("expert_cols", [3 * E0, C0, P], BF16)
    c.expert_number = sb("expert_number", [P, E1], F32)
    c.gates_in = sb("gates_in", [P, 4], F32)
    c.gates = sb("gates", [P, 4], F32)
    c.wq0 = sb("wq0", [D, D], F32)
    c.wk0 = sb("wk0", [DC, D], F32)
    c.wv0 = sb("wv0", [DC, D], F32)
    c.wo0_in = sb("wo0_in", [D, D], F32)
    c.wo0 = sb("wo0", [D, D], F32)
    c.bq0 = sb("bq0", [P, 2], F32)
    c.bk0 = sb("bk0", [P, 2], F32)
    c.bv0 = sb("bv0", [D, 1], F32)
    c.bv0_wide = sb("bv0_wide", [D, P], F32)
    c.bo0_rows = sb("bo0_rows", [P, D], F32)
    c.bo0_gated = sb("bo0_gated", [P, D], F32)
    c.out_bias0 = sb("out_bias0", [P, D], F32)
    c.w_route0_in = sb("w_route0_in", [E0, D], F32)
    c.w_route0 = sb("w_route0", [D, E0], F32)
    c.anchors = sb("anchors", [P, E0, E0], F32)
    c.temp_in = sb("temp_in", [P, 1], F32)
    c.temp = sb("temp", [P, 1], F32)
    c.half_over_temp = sb("half_over_temp", [P, 2], F32)
    c.w1_0 = sb("w1_0", [D, E0, HID0], F32)
    c.w2_0_in = sb("w2_0_in", [P, C0, D], F32)
    c.w2_0 = sb("w2_0", [P, C0, D], F32)
    c.wq1 = sb("wq1", [D, D], F32)
    c.wk1 = sb("wk1", [DC, D], F32)
    c.wv1_in = sb("wv1_in", [DC, D], F32)
    c.wv1 = sb("wv1", [DC, D], F32)
    c.bq1 = sb("bq1", [D, 1], F32)
    c.bk1 = sb("bk1", [D, 1], F32)
    c.bv1_rows = sb("bv1_rows", [P, D], F32)
    c.out_bias1 = sb("out_bias1", [P, D], F32)
    c.w_route1 = sb("w_route1", [D, E1], F32)
    c.w12 = sb("w12", [D, E1, 2, HID1], F32)
    c.w3_in = sb("w3_in", [P, E1, HID1 // P, D], F32)
    c.w3 = sb("w3", [P, E1, HID1 // P, D], F32)
    c.v_heads = [sb(f"v_heads{i}", [P, GB, HU, STRIP], F32) for i in range(2)]
    c.q_blocks = [sb(f"q_blocks{i}", [P, GT, 4, 2, S], F32) for i in range(2)]
    c.parts = sb("parts", [P, REC + 3 * H], BF16)
    c.head_rows_f = sb("head_rows_f", [P, P], F32)
    c.head_rows = sb("head_rows", [P, P], BF16)
    c.probs1 = sb("probs1", [P, GT, P], F32)
    c.values1 = [sb(f"values1_{i}", [P, GT, D + 1], F32) for i in range(2)]

    bank = psum("constants_bank", [P, 512], F32)
    loads = sem("loads")
    tanh_done = sem("tanh_done")
    gated = sem("gated")
    bias_mm = sem("bias_mm")
    bv_wide_done = sem("bv_wide_done")

    def column(row):
        return row.rearrange("(p a) -> p a", a=1)

    def spread(ap, n):
        return ap.rearrange("(a n) -> a n", a=1).broadcast_to([P, n])

    now = [
        (c.ident[:], a["const_ident"]),
        (c.gates_in[:, 0:2], spread(a["g_xattn"], 2)), (c.gates_in[:, 2:4], spread(a["g_ffn"], 2)),
        (c.wk0[:], a["L0_xattn_wk"]), (c.wq0[:], a["L0_xattn_wq"]), (c.wv0[:], a["L0_xattn_wv"]),
        (c.head_of_group[:], a["const_head_of_group"]), (c.head_cols_f[:], a["const_head_cols"]),
        *[(dst[half:half + D // 2, :], a[name].rearrange("(h r) -> r h", h=2))
          for dst, name in ((c.bk0, "L0_xattn_bk"), (c.bq0, "L0_xattn_bq")) for half in (0, D // 2)],
        (c.wo0_in[:], a["L0_xattn_wo"]),
        (c.bv0[:], column(a["L0_xattn_bv"])), (c.bo0_rows[:], spread(a["L0_xattn_bo"], D)),
        (c.head_rows_f[REC:REC + 3 * H, :], a["const_head_rows"]),
        (c.w_route0_in[:], a["L0_ffn_proj_w"]),
    ]
    c.later = [
        (c.expert_cols_f[:], a["const_expert_cols"].rearrange("p (c n) -> p c n", c=C0)),
        (c.expert_number[:], spread(a["const_expert_number"], E1)),
        (c.anchors[:].rearrange("p e d -> p (e d)"), spread(a["L0_ffn_anchors"].rearrange("e d -> (e d)"), E0 * E0)),
        (c.temp_in[:], spread(a["L0_ffn_routing_temp"], 1)),
        (c.w1_0[:], a["L0_ffn_w1"].rearrange("e d h -> d e h")),
        (c.w2_0_in[:], a["L0_ffn_w2"].rearrange("(c a) h d -> (a h) c d", c=C0)),
        (c.wq1[:], a["L1_xattn_Wq"]), (c.wk1[:], a["L1_xattn_Wk"]), (c.wv1_in[:], a["L1_xattn_Wv"]),
        (c.bq1[:], column(a["L1_xattn_bq"])), (c.bk1[:], column(a["L1_xattn_bk"])),
        (c.bv1_rows[:], spread(a["L1_xattn_bv"], D)),
        (c.w_route1[:], a["L1_ffn_Wg"]),
        (c.w12[:, :, 0, :], a["L1_ffn_W1"].rearrange("e d h -> d e h")),
        (c.w12[:, :, 1, :], a["L1_ffn_W2"].rearrange("e d h -> d e h")),
        (c.w3_in[:], a["L1_ffn_W3"].rearrange("e (b h) d -> h e b d", h=P)),
        (c.first_row[:], spread(a["const_first_row"], E1)), (c.earlier_f[:], a["const_earlier"]),
        (c.fill_tokens[:], a["const_fill_tokens"]), (dispatch.tokens[:], a["const_tokens"]),
        (c.tile_sizes[:], a["const_tile_sizes"]), (c.up_to[:], a["const_up_to"]), (c.tile_number[:], a["const_tile_number"]),
    ]
    c.later_loads, c.filled = sem("later_loads"), sem("later_fill")
    c.temp_step = sem("temp_step")

    with nc.Block() as block:
        @block.sync
        def _(sp):
            for g in range(2):
                load_group(sp, c, a, X, g, g)
            for dst, src in now:
                sp.dma_start(dst, src, allow_slow_non_contiguous=True).then_inc(loads, 16)
            sp.wait_ge(loads, 16 * len(now))

        @block.gpsimd
        def _(pool):
            pool.memset(c.parts[:], 0.0)
            for q in c.q_blocks:
                pool.memset(q[:], 0.0)
            pool.memset(c.minus_half[:], -0.5)

        @block.scalar
        def _(act):
            act.wait_ge(loads, 16 * len(now))
            act.activation(c.gates[:], c.gates_in[:], ACT.Tanh).then_inc(tanh_done, 1)

        @block.vector
        def _(dve):
            for v in c.v_heads:
                dve.memset(v[:], 0.0)
            dve.wait_ge(loads, 16 * len(now))
            dve.tensor_copy(c.bv0_wide[:], c.bv0[:, 0:1].broadcast_to([D, P])).then_inc(bv_wide_done, 1)
            dve.tensor_copy(c.head_cols[:], c.head_cols_f[:])
            dve.tensor_copy(c.head_rows[REC:REC + 3 * H, :], c.head_rows_f[REC:REC + 3 * H, :])
            dve.tensor_copy(c.ident_bf[:], c.ident[:])
            dve.wait_ge(tanh_done, 1)
            dve.tensor_scalar(c.wo0[:], c.wo0_in[:], c.gates[:, 0:1], None, ALU.mult).then_inc(gated, 1)
            dve.tensor_scalar(c.bo0_gated[:], c.bo0_rows[:], c.gates[:, 0:1], None, ALU.mult).then_inc(gated, 1)
            dve.wait_ge(bias_mm, 2)
            dve.tensor_copy(c.w_route0[:], bank[:, 256:256 + E0])
            dve.wait_ge(gated, 2)
            dve.tensor_tensor(c.out_bias0[:], bank[:, 0:D], c.bo0_gated[:], ALU.add)

        @block.tensor
        def _(pe):
            pe.wait_ge(loads, 16 * len(now))
            pe.transpose(bank[:, 256:256 + E0], c.w_route0_in[:], c.ident[0:E0, 0:E0]).then_inc(bias_mm, 1)
            pe.wait_ge(bv_wide_done, 1)
            pe.wait_ge(gated, 1)
            pe.matmul(bank[:, 0:D], c.bv0_wide[:], c.wo0[:], start=True, stop=True).then_inc(bias_mm, 1)


def load_group(sp, c, a, X, g, par):
    for dst, src in ((X[:, bass.ts(g, GT), :], a["x"]), (c.ctx_in[par][:], a["ctx_768"])):
        sp.dma_start(dst, src.rearrange("(t b) s d -> (b s) t d", b=2)[:, bass.ts(g, GT), :]).then_inc(c.loaded[par], 16)


def later_zeros(pool, c, dispatch):
    pool.memset(c.probs1[:].rearrange("p t k -> p (t k)"), 0.0)
    for v in c.values1:
        pool.memset(v[:, :, D:D + 1], 1.0)
    pool.memset(c.ones_bf[:], 1.0)
    pool.memset(dispatch.fill[:].rearrange("p a h r -> p (a h r)"), 0.0).then_inc(c.filled, 1)


def later_constants(dve, c, dispatch):
    dve.wait_ge(c.later_loads, 16 * len(c.later))
    dve.tensor_copy(c.earlier[:], c.earlier_f[:])
    dve.tensor_copy(c.expert_cols[:], c.expert_cols_f[:])
    dve.tensor_scalar(c.temp[:], c.temp_in[:], 0.1, None, ALU.max).then_inc(c.temp_step, 1)
    dve.tensor_scalar(c.w3[:].rearrange("p e b d -> p (e b d)"), c.w3_in[:].rearrange("p e b d -> p (e b d)"),
                      c.gates[:, 3:4], None, ALU.mult)
    dve.wait_ge(c.temp_step, 1)
    dve.reciprocal(c.half_over_temp[:, 0:1], c.temp[:]).then_inc(c.temp_step, 1)
    dve.tensor_scalar(c.w2_0[:].rearrange("p c d -> p (c d)"), c.w2_0_in[:].rearrange("p c d -> p (c d)"),
                      c.gates[:, 2:3], None, ALU.mult)
    dve.tensor_scalar(c.wv1[:], c.wv1_in[:], c.gates[0:DC, 1:2], None, ALU.mult)
    dve.tensor_scalar(c.out_bias1[:], c.bv1_rows[:], c.gates[:, 1:2], None, ALU.mult)
    dve.wait_ge(c.temp_step, 2)
    dve.tensor_scalar(c.half_over_temp[:, 1:2], c.half_over_temp[:, 0:1], 0.5, None, ALU.mult)
    dve.wait_ge(c.filled, 1)
    dve.tensor_copy(dispatch.fill[:, :, :, D], c.fill_tokens[:])


def attention_of_layer0(nc, sb, psum, sem, c, a, X, dispatch):
    stats6 = sb("a_stats6", [P, GT, 6], F32)
    stats = sb("a_stats", [P, GT, 2], F32)
    rstd = sb("a_rstd", [P, GT], F32)
    xn = sb("a_xn", [P, GT, D], F32)
    xnT = sb("a_xnT", [D, GW], F32)
    ctx_in, loaded = c.ctx_in, c.loaded
    ctxT = sb("a_ctxT", [DC, GW], F32)
    kT = sb("a_kT", [P, 2, GT, S], F32)
    k_heads = [sb(f"a_k_heads{i}", [P, GT, 2, 4, S], F32) for i in range(2)]
    neg_max = sb("a_neg_max", [P, H], F32)
    parts = c.parts
    rows = sb("a_rows", [REC + 3 * H, P], BF16)
    probs = [sb(f"a_probs{i}", [P, H * S], F32) for i in range(2)]
    probsT = [sb(f"a_probsT{i}", [P, HU, P], F32) for i in range(2)]
    denom = sb("a_denom", [P, H], F32)
    rec = sb("a_rec", [P, H], F32)
    rec_rest = sb("a_rec_rest", [P, H], F32)
    heads_raw = sb("a_heads_raw", [P, P], F32)
    heads_outT = sb("a_heads_outT", [P, P], F32)

    scores = [psum(f"a_scores{i}", [P, 2, 512], F32) for i in range(2)]
    probsT_bank = psum("a_probsT_bank", [P, 512], F32)
    prep = psum("a_prep", [P, 512], F32)
    small = psum("a_small", [P, 512], F32)
    pv = psum("a_pv", [P, 2, P], F32)
    y = small[:, 0:D]
    rows_ps = small[0:REC + 3 * H, D:D + P // 2].bitcast(BF16)

    bn_done, stats_done = sem("a_bn_done"), sem("a_stats_done")
    rstd_step, xn_ready, bias_added = sem("a_rstd_step"), sem("a_xn_ready"), sem("a_bias_added")
    prep_mm, prep_ev, v_odd_ev = sem("a_prep_mm"), sem("a_prep_ev"), sem("a_v_odd_ev")
    q_odd_ev, k_heads_ready = sem("a_q_odd_ev"), sem("a_k_heads")
    scores_mm, max_done, part1_done, parts_ready = sem("a_scores_mm"), sem("a_max"), sem("a_part1"), sem("a_parts")
    sum_done, rec_done, rec1_done = sem("a_sum"), sem("a_rec_done"), sem("a_rec1")
    rest_done, rec2_done, raw_ready = sem("a_rest"), sem("a_rec2"), sem("a_raw_ready")
    rows_mm, rows_ready, sub_mm, exp_done = sem("a_rows_mm"), sem("a_rows_ready"), sem("a_sub_mm"), sem("a_exp")
    pT_mm, pT_ev = sem("a_pT_mm"), sem("a_pT_ev")
    pv_mm, spread_mm, o_ready = sem("a_pv_mm"), sem("a_spread_mm"), sem("a_o_ready")
    y_mm, x_updated = sem("a_y_mm"), sem("a_x_updated")
    PREP = 5
    PREP_AT = ((1,), (2,), (3,), (4,))
    LAST = TILES + 4

    def keys_of_head(par, j):
        return k_heads[par][:, :, :, j, :].rearrange("p t h k -> p h t k")

    def values_of_pairs(par, half, u, at):
        to = c.v_heads[par][half].rearrange("p b (m u) w -> p u (b m) w", u=2)[:, u, :, 2 * DH * u + at:2 * DH * u + at + DH]
        return to, prep[half].rearrange("p (n u w) -> p u n w", u=2, w=DH)[:, u]

    def tile_now(t, lag):
        return None if static(t) and not 0 <= t - lag < TILES else t - lag

    def group_at(g0, more):
        return None if static(g0) and g0 + more >= G else g0 + more

    with nc.Block() as block:
        @block.sync
        def _(sp):
            def load(g, par):
                sp.wait_ge(prep_mm, PREP * (g - 2) + 2)
                load_group(sp, c, a, X, g, par)

            for dst, src in c.later:
                sp.dma_start(dst, src, allow_slow_non_contiguous=True).then_inc(c.later_loads, 16)
            with sp.Fori(1, G // 2) as i:
                load(i * 2, 0)
                load(i * 2 + 1, 1)

        @block.vector
        def _(dve):
            def layer_stats(g, par):
                dve.wait_ge(loaded[par], 32 * ((g - par) // 2) + 32)
                if not static(g) or g >= 1:
                    dve.wait_ge(xn_ready, g)
                for j in range(GT):
                    last = dve.bn_stats(stats6[:, j, :], X[:, g * GT + j, :])
                last.then_inc(bn_done, 1)
                wait_alone(dve, bn_done, g + 1)
                for j in range(GT):
                    last = dve.bn_aggr(stats[:, j, :], stats6[:, j, :])
                last.then_inc(stats_done, 1)

            def layer_norm(g):
                dve.wait_ge(rstd_step, 2 * g + 2)
                if not static(g) or g >= 1:
                    dve.wait_ge(prep_mm, PREP * (g - 1) + 1)
                for j in range(GT):
                    last = dve.tensor_scalar(xn[:, j, :], X[:, g * GT + j, :], stats[:, j, 0:1], rstd[:, j:j + 1],
                                             ALU.subtract, ALU.mult)
                last.then_inc(xn_ready, 1)

            def q_odd(g, par):
                dve.wait_ge(prep_mm, PREP * g + 4)
                if not static(g) or g >= 2:
                    dve.wait_ge(scores_mm, GT * (g - 1))
                for h in range(2):
                    for s in range(2):
                        rows_in = slice(64 + 32 * s, 96 + 32 * s)
                        last = dve.tensor_scalar(c.q_blocks[par][rows_in, :, 2 * h + s, 1, :],
                                                 prep[rows_in, bass.ts(h, GW // 2)].rearrange("p (t q) -> p t q", q=S),
                                                 c.bq0[rows_in, h:h + 1], None, ALU.add)
                last.then_inc(q_odd_ev, 1)

            def v_odd(g, par):
                dve.wait_ge(prep_mm, PREP * g + 5)
                if not static(g) or g >= 2:
                    dve.wait_ge(pv_mm, GT * (g - 1))
                for u in range(2):
                    last = dve.tensor_copy(*values_of_pairs(par, slice(S, P), u, DH))
                last.then_inc(v_odd_ev, 1)

            def step(t, u, g0):
                if static(t) and t == TILES:
                    later_constants(dve, c, dispatch)
                n, m = tile_now(t, 0), tile_now(t, 2)
                if m is not None:
                    dve.wait_ge(exp_done, m + 1)
                    dve.reduce_sum(denom[:], probs[u % 2][:].rearrange("p (h k) -> p h k", k=S), AX_X).then_inc(sum_done, 1)
                if n is not None:
                    dve.wait_ge(scores_mm, n + 1)
                    dve.tensor_reduce(neg_max[:], scores[u % 2][:].rearrange("p a (h k) -> p (a h) k", k=S), AX_X,
                                      ALU.max, negate=True).then_inc(max_done, 1)
                if m is not None:
                    dve.wait_ge(sum_done, m + 1)
                    dve.reciprocal(rec[:], denom[:]).then_inc(rec_done, 1)
                if (n is not None or m is not None) and (not static(t) or t >= 1):
                    dve.wait_ge(rows_mm, t)
                if n is not None:
                    dve.wait_ge(max_done, n + 1)
                    dve.tensor_copy(parts[:, 0:H], neg_max[:]).then_inc(part1_done, 1)
                if m is not None:
                    dve.wait_ge(rec_done, m + 1)
                    dve.tensor_copy(parts[:, REC:REC + H], rec[:]).then_inc(rec1_done, 1)
                if n is not None:
                    dve.wait_ge(part1_done, n + 1)
                    last = dve.tensor_tensor(parts[:, H:2 * H], neg_max[:], parts[:, 0:H], ALU.subtract)
                if m is not None:
                    dve.wait_ge(rec1_done, m + 1)
                    dve.tensor_tensor(rec_rest[:], rec[:], parts[:, REC:REC + H], ALU.subtract).then_inc(rest_done, 1)
                w = tile_now(t, 4)
                if w is not None:
                    if u % GT == 0:
                        dve.wait_ge(bias_added, g0)
                    dve.wait_ge(y_mm, w + 1)
                    dve.tensor_tensor(X[:, w, :], y, X[:, w, :], ALU.add).then_inc(x_updated, 1)
                if m is not None:
                    dve.wait_ge(rest_done, m + 1)
                    dve.tensor_copy(parts[:, REC + H:REC + 2 * H], rec_rest[:]).then_inc(rec2_done, 1)
                    dve.wait_ge(rec2_done, m + 1)
                    last = dve.tensor_tensor(parts[:, REC + 2 * H:REC + 3 * H], rec_rest[:], parts[:, REC + H:REC + 2 * H],
                                             ALU.subtract)
                if n is not None or m is not None:
                    last.then_inc(parts_ready, 1)
                n = tile_now(t, 3)
                if n is not None:
                    dve.wait_ge(spread_mm, n + 1)
                    dve.wait_ge(raw_ready, n + 1)
                    if not static(n) or n >= 1:
                        dve.wait_ge(y_mm, n)
                    dve.tensor_tensor(heads_outT[:], heads_raw[:], pv[:, 1], ALU.mult).then_inc(o_ready, 1)
                if u % GT == 0:
                    g = group_at(g0, 2)
                    if g is not None:
                        layer_stats(g, (u // GT) % 2)
                if u % GT == 1:
                    g = group_at(g0, 2)
                    if g is not None:
                        layer_norm(g)
                if u % GT == 2:
                    g = group_at(g0, 1)
                    if g is not None:
                        q_odd(g, (u // GT + 1) % 2)
                if u % GT == 3:
                    g = group_at(g0, 1)
                    if g is not None:
                        v_odd(g, (u // GT + 1) % 2)

            layer_stats(0, 0)
            layer_norm(0)
            layer_stats(1, 1)
            dve.wait_ge(prep_ev, 3)
            for j in range(4):
                last = dve.tensor_scalar(keys_of_head(0, j), kT[:], c.head_of_group[:, j:j + 1], None, ALU.mult)
            last.then_inc(k_heads_ready, 1)
            q_odd(0, 0)
            v_odd(0, 0)
            layer_norm(1)
            loop_steps(dve, 2 * GT, TILES // (2 * GT) - 2, LAST, step)

        @block.gpsimd
        def _(pool):
            def deviation(g):
                wait_alone(pool, stats_done, g + 1)
                inverse_deviation(pool, stats[:], c.minus_half[:], rstd[:], rstd_step, g)

            def add_bias(g):
                wait_alone(pool, xn_ready, g + 1)
                pool.tensor_tensor(X[:, bass.ts(g, GT), :], X[:, bass.ts(g, GT), :],
                                   c.out_bias0[:].unsqueeze(1).broadcast_to([P, GT, D]), ALU.add).then_inc(bias_added, 1)

            def spread_k(g, par):
                wait_alone(pool, prep_ev, PREP * g + 3)
                if not static(g) or g >= 2:
                    wait_alone(pool, scores_mm, GT * (g - 1))
                for j in range(4):
                    last = pool.tensor_scalar(keys_of_head(par, j), kT[:],
                                              c.head_of_group[:, j:j + 1], None, ALU.mult)
                last.then_inc(k_heads_ready, 1)

            def step(t, u, g0):
                if u % GT == 0:
                    g = group_at(g0, 2)
                    if g is not None:
                        deviation(g)
                if u % GT == 1:
                    g = group_at(g0, 1)
                    if g is not None:
                        spread_k(g, (u // GT + 1) % 2)
                    g = group_at(g0, 2)
                    if g is not None:
                        add_bias(g)

            deviation(0)
            add_bias(0)
            deviation(1)
            add_bias(1)
            loop_steps(pool, 2 * GT, TILES // (2 * GT) - 2, LAST, step)
            later_zeros(pool, c, dispatch)

        @block.scalar
        def _(act):
            def evacuate(g, par, k):
                act.wait_ge(prep_mm, PREP * g + k + 1)
                if k == 0:
                    act.copy(xnT[:], prep[:]).then_inc(prep_ev, 1)
                elif k == 1:
                    act.copy(ctxT[:], prep[0:DC, :]).then_inc(prep_ev, 1)
                elif k == 2:
                    if not static(g) or g >= 1:
                        act.wait_ge(k_heads_ready, g)
                    for h in range(2):
                        last = act.activation(kT[:, h], prep[:, bass.ts(h, GW // 2)], ACT.Identity,
                                              bias=c.bk0[:, h:h + 1])
                    last.then_inc(prep_ev, 1)
                elif k == 3:
                    if not static(g) or g >= 2:
                        act.wait_ge(scores_mm, GT * (g - 1))
                    for h in range(2):
                        for s in range(2):
                            rows_in = slice(32 * s, 32 * s + 32)
                            last = act.activation(c.q_blocks[par][rows_in, :, 2 * h + s, 0, :],
                                                  prep[rows_in, bass.ts(h, GW // 2)].rearrange("p (t q) -> p t q", q=S),
                                                  ACT.Identity, bias=c.bq0[rows_in, h:h + 1])
                    last.then_inc(prep_ev, 1)
                else:
                    if not static(g) or g >= 2:
                        act.wait_ge(pv_mm, GT * (g - 1))
                    for u in range(2):
                        last = act.copy(*values_of_pairs(par, slice(0, S), u, 0))
                    last.then_inc(prep_ev, 1)

            def step(t, u, g0):
                n = tile_now(t, 1)
                if n is not None:
                    act.wait_ge(sub_mm, n + 1)
                    if not static(n) or n >= 2:
                        act.wait_ge(pT_mm, 2 * n - 2)
                    act.activation(probs[(u + 1) % 2][:], scores[(u + 1) % 2][:].rearrange("p a n -> p (a n)"), ACT.Exp,
                                   scale=SCALE0).then_inc(exp_done, 1)

                def keep_transposed(n, half):
                    act.wait_ge(pT_mm, 2 * n + 1 + half)
                    if half == 0 and (not static(n) or n >= 2):
                        act.wait_ge(pv_mm, n - 1)
                    act.copy(probsT[u % 2][:, half * HU // 2:(half + 1) * HU // 2, :].rearrange("p u q -> p (u q)"),
                             probsT_bank[:]).then_inc(pT_ev, 1)

                g = group_at(g0, 1)
                if u % GT == 0 and g is not None:
                    evacuate(g, (u // GT + 1) % 2, 0)
                if tile_now(t, 2) is not None:
                    keep_transposed(t - 2, 0)
                n = tile_now(t, 3)
                if n is not None:
                    act.wait_ge(pv_mm, n + 1)
                    if not static(n) or n >= 1:
                        act.wait_ge(o_ready, n)
                    act.copy(heads_raw[:], pv[:, 0]).then_inc(raw_ready, 1)
                g = group_at(g0, 1)
                if g is not None:
                    for k in PREP_AT[u % GT]:
                        evacuate(g, (u // GT + 1) % 2, k)
                if tile_now(t, 2) is not None:
                    keep_transposed(t - 2, 1)
                if not static(t) or t < TILES + 2:
                    act.wait_ge(rows_mm, t + 1)
                    if not static(t) or t >= 1:
                        if tile_now(t, 1) is not None:
                            act.wait_ge(sub_mm, t)
                        if tile_now(t, 3) is not None:
                            act.wait_ge(spread_mm, t - 2)
                    act.copy(rows[:], rows_ps).then_inc(rows_ready, 1)

            for k in range(PREP):
                evacuate(0, 0, k)
            loop_steps(act, 2 * GT, TILES // (2 * GT) - 2, LAST, step)

        @block.tensor
        def _(pe):
            def prepare(g, par, k):
                if k == 0:
                    if not static(g) or g >= 1:
                        pe.wait_ge(prep_ev, PREP * g)
                        pe.wait_ge(v_odd_ev, g)
                    pe.wait_ge(xn_ready, g + 1)
                    for j in range(GT):
                        last = pe.transpose(prep[:, bass.ts(j, P)], xn[:, j, :], c.ident[:])
                else:
                    pe.wait_ge(prep_ev, PREP * g + k)
                if k == 1:
                    pe.wait_ge(loaded[par], 32 * ((g - par) // 2) + 32)
                    for j in range(GT):
                        last = pe.transpose(prep[0:DC, bass.ts(j, P)], ctx_in[par][:, j, :], c.ident[:])
                if k in (2, 3):
                    w, src = ((c.wk0, ctxT), (c.wq0, xnT))[k - 2]
                    for h in range(2):
                        for odd in range(2):
                            last = pe.matmul(prep[S * odd:S * odd + S, bass.ts(h, GW // 2)], w[:, bass.ts(h, D // 2)],
                                             src[:].rearrange("p (t b q) -> p b t q", b=2, q=S)[:, odd],
                                             start=True, stop=True)
                if k == 4:
                    pe.wait_ge(q_odd_ev, g + 1)
                    pe.wait_ge(k_heads_ready, g + 1)
                    for b in range(GB):
                        for odd in range(2):
                            last = pe.matmul(prep[S * odd:S * odd + S, bass.ts(b, D // 2)], ctxT[:, bass.ts(b, S)],
                                             c.wv0[:].rearrange("p (u h w) -> p h u w", h=2, w=DH)[:, odd],
                                             start=True, stop=True)
                last.then_inc(prep_mm, 1)

            def step(t, u, g0):
                n = tile_now(t, 0)
                if n is not None:
                    if not static(n) or n >= 2:
                        pe.wait_ge(exp_done, n - 1)
                    par, tile = (u // GT) % 2, u % GT
                    for k in range(4):
                        last = pe.matmul(scores[u % 2][:, k // 2, bass.ts(k % 2, 4 * S)],
                                         c.q_blocks[par][:, tile, k].rearrange("p b q -> p (b q)"),
                                         k_heads[par][:, tile, k // 2].rearrange("p j k -> p (j k)"),
                                         start=(k % 2 == 0), stop=True, skip_group_check=True)
                    last.then_inc(scores_mm, 1)
                n = tile_now(t, 1)
                if n is not None:
                    pe.wait_ge(rows_ready, n + 1)
                    for half in range(2):
                        last = pe.matmul(scores[(u + 1) % 2][:, half, :], rows[0:2 * H, :], c.head_cols[:, bass.ts(half, 512)],
                                         start=False, stop=True, skip_group_check=True)
                    last.then_inc(sub_mm, 1)
                g = group_at(g0, 1)
                if u % GT == 0 and g is not None:
                    prepare(g, (u // GT + 1) % 2, 0)
                n = tile_now(t, 4)
                if n is not None:
                    pe.wait_ge(o_ready, n + 1)
                    pe.wait_ge(rows_ready, min(t, TILES + 2) if static(t) else t)
                    if not static(n) or n >= 1:
                        pe.wait_ge(x_updated, n)
                    pe.matmul(y, heads_outT[:], c.wo0[:], start=True, stop=True).then_inc(y_mm, 1)

                def transpose_probs(half):
                    for k in range(HU // 2):
                        last = pe.transpose(probsT_bank[:, bass.ts(k, P)],
                                            probs[u % 2][:, bass.ts(half * HU // 2 + k, P)], c.ident[:])
                    last.then_inc(pT_mm, 1)

                n = tile_now(t, 2)
                if n is not None:
                    pe.wait_ge(exp_done, n + 1)
                    if not static(n) or n >= 1:
                        pe.wait_ge(pT_ev, 2 * n)
                    transpose_probs(0)
                n = tile_now(t, 3)
                if n is not None:
                    pe.wait_ge(rows_ready, n + 3)
                    if not static(n) or n >= 1:
                        pe.wait_ge(o_ready, n)
                    pe.matmul(pv[:, 1], c.head_rows[REC:REC + 3 * H, :], rows[REC:REC + 3 * H, :], start=True,
                              stop=True).then_inc(spread_mm, 1)
                    pe.wait_ge(pT_ev, 2 * n + 2)
                    v_par = ((u + 5) % 8 // GT) % 2
                    if (u + 5) % GT == 0:
                        g = g0 + (u % GT - 3) // GT
                        pe.wait_ge(prep_ev, PREP * g + 5)
                        pe.wait_ge(v_odd_ev, g + 1)
                    for k in range(HU):
                        strip = slice(STRIP * (k // 2), STRIP * (k // 2) + STRIP)
                        for b in range(2):
                            batch = 2 * ((u + 5) % GT) + b
                            last = pe.matmul(pv[strip, 0, bass.ts(b, S)], c.v_heads[v_par][:, batch, k, :],
                                             probsT[(u + 1) % 2][:, k, bass.ts(b, S)], start=(k % 2 == 0 and b == 0),
                                             stop=(k % 2 == 1), skip_group_check=True)
                    last.then_inc(pv_mm, 1)
                g = group_at(g0, 1)
                if g is not None:
                    for k in PREP_AT[u % GT]:
                        prepare(g, (u // GT + 1) % 2, k)
                n = tile_now(t, 2)
                if n is not None:
                    pe.wait_ge(pT_ev, 2 * n + 1)
                    transpose_probs(1)
                if not static(t) or t < TILES + 2:
                    pe.wait_ge(parts_ready, t + 1)
                    if not static(t) or t >= 1:
                        pe.wait_ge(rows_ready, t)
                    if tile_now(t, 4) is not None:
                        pe.wait_ge(x_updated, t - 3)
                    pe.transpose(rows_ps, parts[:], c.ident_bf[:]).then_inc(rows_mm, 1)

            for k in range(PREP):
                prepare(0, 0, k)
            loop_steps(pe, 2 * GT, TILES // (2 * GT) - 2, LAST, step)


def group_steps(eng, lag, step):
    first = -(-lag // 2)
    for g in range(2 * first):
        step(g, g % 2)
    with eng.Fori(first, G // 2 - 1) as i:
        step(i * 2, 0)
        step(i * 2 + 1, 1)
    for g in range(G - 2, G + lag):
        step(g, g % 2)


def group_now(g, lag):
    return None if static(g) and not 0 <= g - lag < G else g - lag


class LayerNorm:

    def __init__(self, name, sb, sem, c, X, own_rows=True, eps_on_vector=False):
        self.c, self.X = c, X
        self.eps_on_vector = eps_on_vector
        if eps_on_vector:
            self.variance = sb(f"{name}_variance", [P, GT], F32)
            self.aggregated = sem(f"{name}_aggregated")
        self.stats6 = sb(f"{name}_stats6", [P, GT, 6], F32)
        self.stats = sb(f"{name}_stats", [P, GT, 2], F32)
        self.rstd = sb(f"{name}_rstd", [P, GT], F32)
        self.minus_mean = sb(f"{name}_minus_mean", [P, GT], F32)
        self.offset_ready = sem(f"{name}_offset_ready")
        if own_rows:
            self.xn = sb(f"{name}_xn", [P, GT, D], F32)
        self.bn_done, self.stats_done = sem(f"{name}_bn_done"), sem(f"{name}_stats_done")
        self.rstd_step, self.xn_ready = sem(f"{name}_rstd_step"), sem(f"{name}_xn_ready")

    def statistics(self, dve, g):
        for j in range(GT):
            self.tile_statistics(dve, g, j)
        self.aggregate(dve, g)

    def tile_statistics(self, dve, g, j):
        dve.bn_stats(self.stats6[:, j, :], self.X[:, g * GT + j, :]).then_inc(self.bn_done, 1)

    def aggregate(self, dve, g):
        if not static(g) or g >= 1:
            dve.wait_ge(self.xn_ready, g)
        wait_alone(dve, self.bn_done, GT * (g + 1))
        for j in range(GT):
            last = dve.bn_aggr(self.stats[:, j, :], self.stats6[:, j, :])
        last.then_inc(self.aggregated if self.eps_on_vector else self.stats_done, 1)

    def add_eps(self, dve, g):
        dve.wait_ge(self.aggregated, g + 1)
        dve.tensor_scalar(self.variance[:], self.stats[:, :, 1], EPS, None, ALU.add).then_inc(self.stats_done, 1)

    def deviation(self, pool, g):
        wait_alone(pool, self.stats_done, g + 1)
        if self.eps_on_vector:
            pool.tensor_tensor(self.rstd[:], self.variance[:], self.c.minus_half[:], ALU.pow).then_inc(self.rstd_step, 2)
            return
        inverse_deviation(pool, self.stats[:], self.c.minus_half[:], self.rstd[:], self.rstd_step, g)

    def rows(self, dve, g, transposed):
        dve.wait_ge(self.rstd_step, 2 * g + 2)
        if not static(g) or g >= 1:
            dve.wait_ge(transposed, g)
        for j in range(GT):
            last = dve.tensor_scalar(self.xn[:, j, :], self.X[:, g * GT + j, :], self.stats[:, j, 0:1],
                                     self.rstd[:, j:j + 1], ALU.subtract, ALU.mult)
        last.then_inc(self.xn_ready, 1)

    def offset(self, dve, g):
        dve.wait_ge(self.rstd_step, 2 * g + 2)
        if not static(g) or g >= 1:
            dve.wait_ge(self.xn_ready, g)
        dve.scalar_tensor_tensor(out=self.minus_mean[:], in0=self.stats[:, :, 0], scalar=-1.0, in1=self.rstd[:],
                                 op0=ALU.mult, op1=ALU.mult).then_inc(self.offset_ready, 1)

    def rows_on_scalar(self, act, g, out):
        act.wait_ge(self.offset_ready, g + 1)
        for j in range(GT):
            last = act.activation(out[:, j, 0:D], self.X[:, g * GT + j, :], ACT.Identity,
                                  bias=self.minus_mean[:, j:j + 1], scale=self.rstd[:, j:j + 1])
        last.then_inc(self.xn_ready, 1)


class TopTwo:

    def __init__(self, name, sb, sem, c, experts, weighed, logits=None):
        self.e, self.c = experts, c
        self.ops = 9 if weighed else 6
        self.logits = sb(f"{name}_logits", [P, GT, 8], F32) if logits is None else logits
        self.sorted = sb(f"{name}_sorted", [P, GT, 8], F32)
        self.index = sb(f"{name}_index", [P, GT, 8], U32)
        self.pick_index = sb(f"{name}_pick_index", [P, 2, GT], F32)
        self.picks = sb(f"{name}_picks", [P, 2, GT, experts], F32)
        self.first, self.second = self.picks[:, 0], self.picks[:, 1]
        self.gap = sb(f"{name}_gap", [P, GT], F32)
        self.tanh = sb(f"{name}_tanh", [P, GT], F32)
        if weighed:
            self.p1, self.p2 = sb(f"{name}_p1", [P, GT], F32), sb(f"{name}_p2", [P, GT], F32)
            self.weights = sb(f"{name}_weights", [P, GT, experts], F32)
        self.op_done = sem(f"{name}_op_done")
        self.gap_ready, self.tanh_ready = sem(f"{name}_gap_ready"), sem(f"{name}_tanh_ready")

    def wide(self, column):
        return column[:].unsqueeze(2).broadcast_to([P, GT, self.e])

    def set_up(self, dve):
        if self.e < 8:
            dve.memset(self.logits[:, :, self.e:], -FAR).then_inc(self.gap_ready, 1)

    def choose(self, dve, g, meanwhile=None):
        for j in range(GT):
            last = dve.max(self.sorted[:, j], self.logits[:, j])
        last.then_inc(self.op_done, 1)
        if meanwhile:
            meanwhile()
        wait_alone(dve, self.op_done, self.ops * g + 1)
        for j in range(GT):
            last = dve.max_index(self.index[:, j], self.sorted[:, j], self.logits[:, j])
        last.then_inc(self.op_done, 1)
        dve.tensor_tensor(self.gap[:], self.sorted[:, :, 0], self.sorted[:, :, 1], ALU.subtract).then_inc(self.gap_ready, 1)
        dve.wait_ge(self.op_done, self.ops * g + 2)
        dve.tensor_copy(self.pick_index[:], self.index[:, :, 0:2].rearrange("p t k -> p k t")).then_inc(self.op_done, 1)
        dve.wait_ge(self.op_done, self.ops * g + 3)
        dve.tensor_tensor(self.picks[:], self.pick_index[:].unsqueeze(3).broadcast_to([P, 2, GT, self.e]),
                          self.c.expert_number[:, 0:self.e].unsqueeze(1).unsqueeze(1).broadcast_to([P, 2, GT, self.e]),
                          ALU.is_equal).then_inc(self.op_done, 1)
        if meanwhile:
            meanwhile()
        dve.wait_ge(self.op_done, self.ops * g + 4)

    def gap_tanh(self, act, g):
        act.wait_ge(self.gap_ready, g + (2 if self.e < 8 else 1))
        act.activation(self.tanh[:], self.gap[:], ACT.Tanh, scale=0.5).then_inc(self.tanh_ready, 1)

    def shares(self, dve, g, p1, p2):
        dve.wait_ge(self.tanh_ready, g + 1)
        dve.tensor_scalar(p1, self.tanh[:], 0.5, 0.5, ALU.mult, ALU.add).then_inc(self.op_done, 1)
        dve.tensor_scalar(p2, self.tanh[:], -0.5, 0.5, ALU.mult, ALU.add).then_inc(self.op_done, 1)

    def weigh(self, dve, g):
        dve.wait_ge(self.op_done, self.ops * g + 6)
        dve.tensor_tensor(self.first, self.first, self.wide(self.p1), ALU.mult).then_inc(self.op_done, 1)
        dve.tensor_tensor(self.second, self.second, self.wide(self.p2), ALU.mult).then_inc(self.op_done, 1)
        dve.wait_ge(self.op_done, self.ops * g + 8)
        dve.tensor_tensor(self.weights[:], self.first, self.second, ALU.add).then_inc(self.op_done, 1)


def mixture_of_layer0(nc, sb, psum, sem, c, X):
    ln = LayerNorm("b", sb, sem, c, X)
    top = TopTwo("b", sb, sem, c, E0, True)
    xnT = [sb(f"b_xnT{i}", [D, GW], F32) for i in range(2)]
    q = sb("b_q", [P, GT, E0], F32)
    q_anchor = sb("b_q_anchor", [P, GT, E0, E0], F32)
    dot = sb("b_dot", [P, GT, E0], F32)
    w_rest = sb("b_w_rest", [P, GT, E0], F32)
    w_parts = sb("b_w_parts", [P, GT, 3, E0], BF16)
    w_rows = sb("b_w_rows", [3 * E0, GW], BF16)
    hidden = [sb(f"b_hidden{i}", [P, C0, GW], F32) for i in range(2)]
    weighted = [sb(f"b_weighted{i}", [P, C0, GW], F32) for i in range(2)]

    tr, z, w_bank, y = (psum(f"b_{n}_bank", [P, 512], F32) for n in ("tr", "z", "w", "y"))
    h_bank = [psum(f"b_h{i}", [P, 512], F32) for i in range(2)]
    spread = [psum(f"b_spread{i}", [P, 512], F32) for i in range(2)]
    w_rows_ps = w_bank[0:3 * E0, 0:GW // 2].bitcast(BF16)

    xn_transposed, xT_ready = sem("b_xn_transposed"), sem("b_xT_ready")
    z_mm, q_ready, dot_step, parts_step = sem("b_z_mm"), sem("b_q_ready"), sem("b_dot_step"), sem("b_parts_step")
    w_mm, w_ready, h_mm, gelu_done = sem("b_w_mm"), sem("b_w_ready"), sem("b_h_mm"), sem("b_gelu_done")
    spread_mm, y_mm, x_updated = sem("b_spread_mm"), sem("b_y_mm"), sem("b_x_updated")
    weighted_ready = sem("b_weighted")
    LAG = 3

    with nc.Block() as block:
        @block.gpsimd
        def _(pool):
            def step(g, par):
                n = group_now(g, -1)
                if n is not None:
                    ln.deviation(pool, n)

            ln.deviation(pool, 0)
            group_steps(pool, LAG, step)

        @block.vector
        def _(dve):
            def route(n):
                dve.wait_ge(q_ready, n + 1)
                dve.tensor_tensor(q_anchor[:], q[:].unsqueeze(2).broadcast_to([P, GT, E0, E0]),
                                  c.anchors[:].unsqueeze(1).broadcast_to([P, GT, E0, E0]), ALU.mult).then_inc(dot_step, 1)
                dve.wait_ge(dot_step, 3 * n + 1)
                dve.reduce_sum(dot[:], q_anchor[:], AX_X).then_inc(dot_step, 1)
                dve.wait_ge(dot_step, 3 * n + 2)
                dve.tensor_scalar(top.logits[:, :, 0:E0], dot[:], float(E0), c.half_over_temp[:, 1:2], ALU.subtract,
                                  ALU.mult).then_inc(dot_step, 1)
                wait_alone(dve, dot_step, 3 * n + 3)
                top.choose(dve, n)

            def split(n, step):
                if step == 0:
                    dve.wait_ge(top.op_done, top.ops * n + top.ops)
                    if not static(n) or n >= 1:
                        dve.wait_ge(w_mm, n)
                else:
                    dve.wait_ge(parts_step, 4 * n + step)
                if step == 0:
                    last = dve.tensor_copy(w_parts[:, :, 0, :], top.weights[:])
                elif step == 1:
                    last = dve.tensor_tensor(w_rest[:], top.weights[:], w_parts[:, :, 0, :], ALU.subtract)
                elif step == 2:
                    last = dve.tensor_copy(w_parts[:, :, 1, :], w_rest[:])
                else:
                    last = dve.tensor_tensor(w_parts[:, :, 2, :], w_rest[:], w_parts[:, :, 1, :], ALU.subtract)
                last.then_inc(parts_step, 1)

            def weigh_hidden(n, par, k):
                dve.wait_ge(spread_mm, C0 * n + k + 1)
                dve.wait_ge(gelu_done, C0 * n + k + 1)
                if k == 0 and (not static(n) or n >= 2):
                    dve.wait_ge(y_mm, n - 1)
                dve.tensor_tensor(weighted[par][:, k, :], hidden[par][:, k, :], spread[(C0 * par + k) % 2][:],
                                  ALU.mult).then_inc(weighted_ready, 1)

            def step(g, par):
                m, n = group_now(g, 1), group_now(g, 2)
                if m is not None:
                    route(m)
                w = group_now(g, 0)
                if w is not None:
                    ln.offset(dve, w)
                if n is not None:
                    weigh_hidden(n, par, 0)
                w = group_now(g, -1)
                if m is not None:
                    top.shares(dve, m, top.p1[:], top.p2[:])
                if w is not None:
                    ln.tile_statistics(dve, w, 0)
                if m is not None:
                    top.weigh(dve, m)
                if n is not None:
                    weigh_hidden(n, par, 1)
                for j in range(3):
                    if m is not None:
                        split(m, j)
                    if w is not None:
                        ln.tile_statistics(dve, w, j + 1)
                if m is not None:
                    split(m, 3)
                if n is not None:
                    weigh_hidden(n, par, 2)
                if w is not None:
                    ln.aggregate(dve, w)
                n = group_now(g, 3)
                if n is not None:
                    dve.wait_ge(y_mm, n + 1)
                    dve.tensor_tensor(X[:, bass.ts(n, GT), :], y[:].rearrange("p (t d) -> p t d", t=GT),
                                      X[:, bass.ts(n, GT), :], ALU.add).then_inc(x_updated, 1)

            top.set_up(dve)
            ln.statistics(dve, 0)
            group_steps(dve, LAG, step)

        @block.scalar
        def _(act):
            def normalise(n):
                if not static(n) or n >= 1:
                    act.wait_ge(xn_transposed, n)
                ln.rows_on_scalar(act, n, ln.xn)

            def gelu(n, par, k):
                act.wait_ge(h_mm, C0 * n + k + 1)
                if k == 0 and (not static(n) or n >= 2):
                    act.wait_ge(weighted_ready, C0 * (n - 1))
                act.activation(hidden[par][:, k, :], h_bank[(C0 * par + k) % 2][:], ACT.Gelu_apprx_tanh).then_inc(gelu_done, 1)

            def step(g, par):
                m, n = group_now(g, 1), group_now(g, 2)
                if m is not None:
                    act.wait_ge(z_mm, m + 1)
                    if not static(m) or m >= 1:
                        act.wait_ge(dot_step, 3 * m)
                    act.activation(q[:].rearrange("p t e -> p (t e)"), z[:, 0:GT * E0], ACT.Tanh,
                                   scale=1.0 / QUANT_TEMP).then_inc(q_ready, 1)
                    gelu(m, 1 - par, 0)
                if n is not None:
                    act.wait_ge(w_mm, n + 1)
                    if not static(n) or n >= 1:
                        act.wait_ge(spread_mm, C0 * n)
                    act.copy(w_rows[:], w_rows_ps).then_inc(w_ready, 1)
                if m is not None:
                    gelu(m, 1 - par, 1)
                    top.gap_tanh(act, m)
                w = group_now(g, 0)
                if w is not None:
                    normalise(w)
                    act.wait_ge(xn_transposed, w + 1)
                    if not static(w) or w >= 2:
                        act.wait_ge(h_mm, C0 * (w - 1))
                    act.copy(xnT[par][:], tr[:]).then_inc(xT_ready, 1)
                if m is not None:
                    gelu(m, 1 - par, 2)
            group_steps(act, LAG, step)

        @block.tensor
        def _(pe):
            def spread_weights(n, par, k):
                if k == 2 or not static(n) or n >= 1:
                    pe.wait_ge(weighted_ready, C0 * n + k - 1)
                pe.matmul(spread[(C0 * par + k) % 2][:], c.expert_cols[:, k, :], w_rows[:],
                          start=True, stop=True).then_inc(spread_mm, 1)

            def hidden_units(n, par, k):
                if C0 * par + k >= 2 or not static(n) or n >= 2:
                    pe.wait_ge(gelu_done, C0 * n + k - 1)
                pe.matmul(h_bank[(C0 * par + k) % 2][:], c.w1_0[:, 2 * k:2 * k + 2, :].rearrange("d e h -> d (e h)"),
                          xnT[par][:], start=True, stop=True).then_inc(h_mm, 1)

            def step(g, par):
                m, n = group_now(g, 1), group_now(g, 2)
                if m is not None:
                    pe.wait_ge(xT_ready, m + 1)
                    if not static(m) or m >= 1:
                        pe.wait_ge(q_ready, m)
                    for j in range(GT):
                        last = pe.matmul(z[:, bass.ts(j, E0)], xnT[1 - par][:, bass.ts(j, P)], c.w_route0[:], start=True, stop=True)
                    last.then_inc(z_mm, 1)
                    hidden_units(m, 1 - par, 0)
                if n is not None:
                    pe.wait_ge(parts_step, 4 * n + 4)
                    if not static(n) or n >= 1:
                        pe.wait_ge(w_ready, n)
                    for j in range(GT):
                        last = pe.transpose(w_rows_ps[:, bass.ts(j, P)], w_parts[:, j].rearrange("p a e -> p (a e)"),
                                            c.ident_bf[:])
                    last.then_inc(w_mm, 1)
                if m is not None:
                    hidden_units(m, 1 - par, 1)
                if n is not None:
                    pe.wait_ge(w_ready, n + 1)
                    spread_weights(n, par, 0)
                    spread_weights(n, par, 1)
                o = group_now(g, 3)
                if o is not None:
                    pe.wait_ge(weighted_ready, C0 * o + C0)
                    if not static(o) or o >= 1:
                        pe.wait_ge(x_updated, o)
                    for j in range(GT):
                        for k in range(C0):
                            last = pe.matmul(y[:, bass.ts(j, P)], weighted[1 - par][:, k, bass.ts(j, P)], c.w2_0[:, k, :],
                                             start=(k == 0), stop=(k == C0 - 1))
                    last.then_inc(y_mm, 1)
                w = group_now(g, 0)
                if w is not None:
                    pe.wait_ge(ln.xn_ready, w + 1)
                    if not static(w) or w >= 1:
                        pe.wait_ge(xT_ready, w)
                    for j in range(GT):
                        last = pe.transpose(tr[:, bass.ts(j, P)], ln.xn[:, j, :], c.ident[:])
                    last.then_inc(xn_transposed, 1)
                if n is not None:
                    spread_weights(n, par, 2)
                if m is not None:
                    hidden_units(m, 1 - par, 2)

            group_steps(pe, LAG, step)


class Dispatch:

    def __init__(self, nc, sb, sem):
        self.rows = nc.dram_tensor("sorted_rows", (E1 * REGION + DUMMY_TILES * TP, ROW), F32).ap()
        self.next_row = sb("next_row", [P, E1], F32)
        self.fill = sb("fill", [P, E1 + DUMMY_TILES, 2, ROW], F32)
        self.tokens = sb("tokens", [P, TILES], F32)
        self.sent = [sem(f"sent{i}") for i in range(2)]
        self.x_stored = sem("x_stored")
        self.count = sb("plan_count", [1, E1], F32)
        self.over = sb("plan_over", [1, E1, MAX_TILES], F32)
        self.tiles = sb("plan_tiles", [1, E1], F32)
        self.upto = sb("plan_upto", [1, E1, E1], F32)
        self.ends = sb("plan_ends", [1, E1], F32)
        self.past = sb("plan_past", [1, DTILES, E1], F32)
        self.expert = sb("plan_expert", [1, DTILES], F32)
        self.past_tiles = sb("plan_past_tiles", [1, DTILES, E1], F32)
        self.start = sb("plan_start", [1, DTILES], F32)
        self.first_f = sb("plan_first_f", [1, DTILES], F32)
        self.end_row = sb("plan_end_row", [1, E1], I32)
        self.tile_expert = sb("plan_tile_expert", [1, DTILES], I32)
        self.tile_row = sb("plan_tile_row", [1, DTILES], I32)
        self.tile_start = sb("plan_tile_start", [1, DTILES], I32)
        self.plan_step, self.end_row_ready, self.filled = sem("plan_step"), sem("end_row_ready"), sem("filled")

    def plan_tiles(self, dve, c):
        steps = [0]

        def then(ins):
            ins.then_inc(self.plan_step, 1)
            steps[0] += 1
            dve.wait_ge(self.plan_step, steps[0])

        dve.tensor_copy(self.end_row[:], self.next_row[0:1, :]).then_inc(self.end_row_ready, 1)
        then(dve.tensor_tensor(self.count[:], self.next_row[0:1, :], c.first_row[0:1, :], ALU.subtract))
        then(dve.tensor_tensor(self.over[:], self.count[:].unsqueeze(2).broadcast_to([1, E1, MAX_TILES]),
                               c.tile_sizes[:].unsqueeze(1).broadcast_to([1, E1, MAX_TILES]), ALU.is_gt))
        then(dve.tensor_reduce(self.tiles[:], self.over[:], AX_X, ALU.add))
        then(dve.tensor_tensor(self.upto[:], self.tiles[:].unsqueeze(1).broadcast_to([1, E1, E1]), c.up_to[:], ALU.mult))
        then(dve.tensor_reduce(self.ends[:], self.upto[:], AX_X, ALU.add))
        then(dve.tensor_tensor(self.past[:], c.tile_number[:].unsqueeze(2).broadcast_to([1, DTILES, E1]),
                               self.ends[:].unsqueeze(1).broadcast_to([1, DTILES, E1]), ALU.is_ge))
        then(dve.tensor_reduce(self.expert[:], self.past[:], AX_X, ALU.add))
        then(dve.tensor_tensor(self.past_tiles[:], self.past[:], self.tiles[:].unsqueeze(1).broadcast_to([1, DTILES, E1]), ALU.mult))
        then(dve.tensor_reduce(self.start[:], self.past_tiles[:], AX_X, ALU.add))
        then(dve.tensor_copy(self.tile_start[:], self.start[:]))
        then(dve.tensor_tensor(self.first_f[:], c.tile_number[:], self.start[:], ALU.subtract))
        then(dve.tensor_scalar(self.first_f[:], self.first_f[:], float(TP), None, ALU.mult))
        then(dve.scalar_tensor_tensor(out=self.first_f[:], in0=self.expert[:], scalar=float(REGION), in1=self.first_f[:],
                                      op0=ALU.mult, op1=ALU.add))
        then(dve.tensor_copy(self.tile_row[:], self.first_f[:]))
        then(dve.tensor_scalar(self.tile_expert[:], self.expert[:], float(E1 - 1), None, ALU.min))

    def fill_up(self, eng, experts):
        eng.wait_ge(self.end_row_ready, 1)
        for e in experts:
            end = eng.value_load(self.end_row[0:1, e:e + 1], min_val=e * REGION, max_val=e * REGION + B * S)
            eng.dma_start(self.rows[bass.ds(end, TP), :].rearrange("(p h) d -> p h d", h=TP // P),
                          self.fill[:, e]).then_inc(self.filled, 16)


def attention_and_routing_of_layer1(nc, sb, psum, sem, c, a, X, dispatch, out):
    ln = LayerNorm("c", sb, sem, c, X, eps_on_vector=True)
    ctx_in = [sb(f"c_ctx{i}", [P, GT, DC], F32) for i in range(2)]
    xnT = sb("c_xnT", [D, GW], F32)
    ctxT = sb("c_ctxT", [DC, GW], F32)
    qT = sb("c_qT", [D, GW], F32)
    kT = sb("c_kT", [D, GW], F32)
    neg_max = sb("c_neg_max", [P, GT], F32)
    shifted = sb("c_shifted", [P, GT, S], F32)
    probs = c.probs1
    probsT = sb("c_probsT", [P, GT, P], F32)
    values = c.values1
    rec = sb("c_rec", [P, GT], F32)

    tr, q_bank, k_bank, v_bank, s_bank, pT_bank = (psum(f"c_{n}_bank", [P, 512], F32) for n in ("tr", "q", "k", "v", "s", "pT"))
    out_bank = psum("c_out_bank", [P, 2, 512], F32)
    outs = [out_bank[:, j // 2, (D + 1) * (j % 2):(D + 1) * (j % 2 + 1)] for j in range(GT)]

    loaded = [sem(f"c_loaded{i}") for i in range(2)]
    xn_transposed, xT_ready = sem("c_xn_transposed"), sem("c_xT_ready")
    ctx_transposed, ctxT_ready = sem("c_ctx_transposed"), sem("c_ctxT_ready")
    q_mm, k_mm, v_mm = sem("c_q_mm"), sem("c_k_mm"), sem("c_v_mm")
    q_ready, k_ready, v_ready = sem("c_q_ready"), sem("c_k_ready"), sem("c_v_ready")
    s_mm, max_done, shifted_ready, exp_done = sem("c_s_mm"), sem("c_max_done"), sem("c_shifted"), sem("c_exp_done")
    pT_mm, pT_ready, out_mm = sem("c_pT_mm"), sem("c_pT_ready"), sem("c_out_mm")
    rec_done, x_updated = sem("c_rec_done"), sem("c_x_updated")
    ln2 = LayerNorm("r", sb, sem, c, X, own_rows=False, eps_on_vector=True)
    send = [[sb(f"r_send{i}_{k}", [P, GT, ROW], F32) for k in range(2)] for i in range(2)]
    xrT = sb("r_xrT", [D, GW], F32)
    chosen = sb("r_chosen", [P, GT + 1, E1], BF16)
    place = sb("r_place", [P, GT, E1], F32)
    picked = sb("r_picked", [P, 2, GT, E1], F32)
    slot_f = sb("r_slot_f", [P, 2, GT], F32)
    slots = [sb(f"r_slots{i}", [P, 2, GT], U32) for i in range(2)]
    z = out_bank[:, 0, 2 * (D + 1):2 * (D + 1) + GT * E1]
    ranks = out_bank[:, 1, 2 * (D + 1):2 * (D + 1) + (GT + 1) * E1]
    top = TopTwo("r", sb, sem, c, E1, False, z.rearrange("p (t e) -> p t e", e=E1))
    xr_transposed, xrT_ready, second_row_ready = sem("r_xr_transposed"), sem("r_xrT_ready"), sem("r_second_row")
    z_mm, chosen_ready, ranks_mm, place_step = (sem(f"r_{n}") for n in ("z_mm", "chosen", "ranks_mm", "place_step"))
    buffer_free = sem("r_buffer_free")
    set_up, next_row_done = sem("r_set_up"), sem("r_next_row")
    PLACE_STEPS = 4
    LAG = 5

    with nc.Block() as block:
        @block.sync
        def _(sp):
            def load(g, par):
                if not static(g) or g >= 2:
                    sp.wait_ge(ctx_transposed, g - 1)
                sp.dma_start(ctx_in[par][:],
                             a["ctx_768"].rearrange("(t b) s d -> (b s) t d", b=2)[:, bass.ts(g, GT), :]).then_inc(loaded[par], 16)

            def store(g):
                sp.wait_ge(x_updated, g + 1)
                sp.dma_start(out[0:B * S, :].rearrange("(t p) d -> p t d", p=P)[:, bass.ts(g, GT), :],
                             X[:, bass.ts(g, GT), :]).then_inc(dispatch.x_stored, 16)

            load(0, 0)
            load(1, 1)
            sp.dma_start(dispatch.rows[E1 * REGION:, :].rearrange("(a p h) d -> p a h d", p=P, h=TP // P),
                         dispatch.fill[:, E1:]).then_inc(dispatch.filled, 16)
            with sp.Fori(1, G // 2) as i:
                load(i * 2, 0)
                load(i * 2 + 1, 1)
                store(i * 2 - 2)
                store(i * 2 - 1)
            store(G - 2)
            store(G - 1)
            dispatch.fill_up(sp, range(0, E1, 2))
            sp.wait_ge(dispatch.filled, 16 * (E1 + 1))
            for k in range(2):
                sp.wait_ge(dispatch.sent[k], 16 * 2 * GT * (G // 2))
            sp.wait_ge(dispatch.x_stored, 16 * G)

        @block.gpsimd
        def _(pool):
            def scatter(n, par, ks):
                if ks[0] == 0:
                    pool.wait_ge(second_row_ready, n + 1)
                    wait_alone(pool, place_step, PLACE_STEPS * n + PLACE_STEPS)
                for k in ks:
                    for j in range(GT):
                        pool.indirect_dma_start(dispatch.rows, bass.IndirectOffsetOnAxis(ap=slots[par][:, k, j:j + 1], axis=0),
                                                send[par][k][:, j, :], None).then_inc(dispatch.sent[par], 16)

            def step(g, par):
                n = group_now(g, 5)
                if n is not None:
                    scatter(n, 1 - par, (0, 1))
                n = group_now(g, 3)
                if n is not None:
                    ln2.deviation(pool, n)
                n = group_now(g, -2)
                if n is not None:
                    ln.deviation(pool, n)

            pool.memset(chosen[:].rearrange("p t e -> p (t e)"), 0.0).then_inc(set_up, 1)
            ln.deviation(pool, 0)
            ln.deviation(pool, 1)
            group_steps(pool, LAG, step)

        @block.vector
        def _(dve):
            def places(r, par):
                dve.wait_ge(ranks_mm, r + 1)
                dve.wait_ge(next_row_done, r + 1)
                dve.tensor_tensor(place[:], ranks[:, 0:GT * E1].rearrange("p (t e) -> p t e", e=E1),
                                  dispatch.next_row[:].unsqueeze(1).broadcast_to([P, GT, E1]), ALU.add).then_inc(place_step, 1)
                dve.wait_ge(place_step, PLACE_STEPS * r + 1)
                dve.tensor_tensor(dispatch.next_row[:], dispatch.next_row[:], ranks[:, GT * E1:(GT + 1) * E1],
                                  ALU.add).then_inc(next_row_done, 1)
                dve.tensor_tensor(picked[:], top.picks[:], place[:].unsqueeze(1).broadcast_to([P, 2, GT, E1]),
                                  ALU.mult).then_inc(place_step, 1)
                dve.wait_ge(place_step, PLACE_STEPS * r + 2)
                dve.tensor_reduce(slot_f[:], picked[:], AX_X, ALU.add).then_inc(place_step, 1)
                dve.wait_ge(place_step, PLACE_STEPS * r + 3)
                dve.tensor_copy(slots[par][:], slot_f[:]).then_inc(place_step, 1)

            def step(g, par):
                w, tiles_done = group_now(g, -2), [0]

                def next_tile():
                    if w is not None:
                        ln.tile_statistics(dve, w, tiles_done[0])
                        tiles_done[0] += 1

                n = group_now(g, 3)
                if n is not None:
                    dve.wait_ge(out_mm, n + 1)
                    dve.reciprocal(rec[:].rearrange("p (a b) -> p a b", a=2),
                                   out_bank[:, :, D:2 * (D + 1):D + 1]).then_inc(rec_done, 1)
                    next_tile()
                    dve.wait_ge(rec_done, n + 1)
                    for j in range(GT):
                        last = dve.scalar_tensor_tensor(out=X[:, n * GT + j, :], in0=outs[j][:, 0:D], scalar=rec[:, j:j + 1],
                                                        in1=X[:, n * GT + j, :], op0=ALU.mult, op1=ALU.add)
                    last.then_inc(x_updated, 1)
                n = group_now(g, 2)
                if n is not None:
                    dve.wait_ge(s_mm, n + 1)
                    dve.tensor_reduce(neg_max[:], s_bank[:, 0:GT * S].rearrange("p (t k) -> p t k", k=S), AX_X, ALU.max,
                                      negate=True).then_inc(max_done, 1)
                    next_tile()
                    dve.wait_ge(max_done, n + 1)
                    if not static(n) or n >= 1:
                        dve.wait_ge(exp_done, n)
                    dve.tensor_tensor(shifted[:], s_bank[:, 0:GT * S].rearrange("p (t k) -> p t k", k=S),
                                      neg_max[:].unsqueeze(2).broadcast_to([P, GT, S]), ALU.add).then_inc(shifted_ready, 1)
                n = group_now(g, 3)
                if n is not None:
                    wait_alone(dve, x_updated, n + 1)
                    ln2.statistics(dve, n)
                r = group_now(g, 4)
                if r is not None:
                    if not static(r) or r >= 1:
                        dve.wait_ge(place_step, PLACE_STEPS * r)
                    wait_alone(dve, z_mm, r + 1)
                    top.choose(dve, r, next_tile)
                    if not static(r) or r >= 1:
                        dve.wait_ge(ranks_mm, r)
                    if static(r) and r == 0:
                        dve.wait_ge(set_up, 1)
                    dve.tensor_tensor(chosen[:, 0:GT, :], top.first, top.second, ALU.add).then_inc(chosen_ready, 1)
                n = group_now(g, 3)
                if n is not None:
                    ln2.add_eps(dve, n)
                n = group_now(g, -1)
                if n is not None:
                    ln.rows(dve, n, xn_transposed)
                n = w
                if n is not None:
                    while tiles_done[0] < GT:
                        next_tile()
                    ln.aggregate(dve, n)
                if r is not None:
                    top.shares(dve, r, send[par][0][:, :, D + 1], send[par][1][:, :, D + 1])
                if n is not None:
                    ln.add_eps(dve, n)
                if r is not None:
                    places(r, par)
                n = group_now(g, 3)
                if n is not None:
                    ln2.offset(dve, n)
                    if not static(n) or n >= 2:
                        dve.wait_ge(dispatch.sent[1 - par], 16 * 2 * GT * ((n + par - 1) // 2))
                    for k in range(2):
                        last = dve.tensor_copy(send[1 - par][k][:, :, D], dispatch.tokens[:, bass.ts(n, GT)])
                    last.then_inc(buffer_free, 1)
                n = group_now(g, 1)
                if n is not None:
                    dve.wait_ge(v_mm, n + 1)
                    if not static(n) or n >= 2:
                        dve.wait_ge(out_mm, n - 1)
                    dve.tensor_tensor(values[1 - par][:, :, 0:D], v_bank[:].rearrange("p (t d) -> p t d", t=GT),
                                      c.out_bias1[:].unsqueeze(1).broadcast_to([P, GT, D]), ALU.add).then_inc(v_ready, 1)

            dve.tensor_copy(dispatch.next_row[:], c.first_row[:]).then_inc(next_row_done, 1)
            ln.statistics(dve, 0)
            ln.add_eps(dve, 0)
            ln.rows(dve, 0, xn_transposed)
            ln.statistics(dve, 1)
            ln.add_eps(dve, 1)
            group_steps(dve, LAG, step)
            dispatch.plan_tiles(dve, c)

        @block.scalar
        def _(act):
            def step(g, par):
                r = group_now(g, 4)
                if r is not None:
                    act.wait_ge(ln2.xn_ready, r + 1)
                    act.copy(send[par][1][:, :, 0:D], send[par][0][:, :, 0:D]).then_inc(second_row_ready, 1)
                    act.wait_ge(xr_transposed, r + 1)
                    if not static(r) or r >= 1:
                        act.wait_ge(z_mm, r)
                    act.copy(xrT[:], tr[:]).then_inc(xrT_ready, 1)
                n = group_now(g, 2)
                if n is not None:
                    act.wait_ge(shifted_ready, n + 1)
                    if not static(n) or n >= 1:
                        act.wait_ge(pT_mm, n)
                    for b in range(2):
                        half = slice(S * b, S * b + S)
                        last = act.activation(probs[half, :, half], shifted[half], ACT.Exp, scale=SCALE1)
                    last.then_inc(exp_done, 1)
                m = group_now(g, 1)
                if m is not None:
                    act.wait_ge(q_mm, m + 1)
                    if not static(m) or m >= 1:
                        act.wait_ge(s_mm, m)
                    act.activation(qT[:], q_bank[:], ACT.Identity, bias=c.bq1[:, 0:1]).then_inc(q_ready, 1)
                w = group_now(g, 0)
                if w is not None:
                    act.wait_ge(xn_transposed, w + 1)
                    if not static(w) or w >= 1:
                        act.wait_ge(q_mm, w)
                    act.copy(xnT[:], tr[:]).then_inc(xT_ready, 1)
                if m is not None:
                    act.wait_ge(k_mm, m + 1)
                    act.activation(kT[:], k_bank[:], ACT.Identity, bias=c.bk1[:, 0:1]).then_inc(k_ready, 1)
                if r is not None:
                    top.gap_tanh(act, r)
                if n is not None:
                    act.wait_ge(pT_mm, n + 1)
                    if not static(n) or n >= 1:
                        act.wait_ge(out_mm, n)
                    act.copy(probsT[:].rearrange("p t q -> p (t q)"), pT_bank[:]).then_inc(pT_ready, 1)
                if w is not None:
                    act.wait_ge(ctx_transposed, w + 1)
                    if not static(w) or w >= 1:
                        act.wait_ge(v_mm, w)
                    act.copy(ctxT[:], tr[0:DC, :]).then_inc(ctxT_ready, 1)
                n = group_now(g, 3)
                if n is not None:
                    act.wait_ge(buffer_free, n + 1)
                    ln2.rows_on_scalar(act, n, send[1 - par][0])

            group_steps(act, LAG, step)
            dispatch.fill_up(act, range(1, E1, 2))

        @block.tensor
        def _(pe):
            def scores(n):
                pe.wait_ge(q_ready, n + 1)
                pe.wait_ge(k_ready, n + 1)
                if not static(n) or n >= 1:
                    pe.wait_ge(shifted_ready, n)
                for j in range(GT):
                    for b in range(2):
                        cols = bass.ts(2 * j + b, S)
                        last = pe.matmul(s_bank[S * b:S * b + S, bass.ts(j, S)], qT[:, cols], kT[:, cols],
                                         start=True, stop=True)
                last.then_inc(s_mm, 1)

            def step(g, par):
                n = group_now(g, 3)
                if n is not None:
                    pe.wait_ge(pT_ready, n + 1)
                    pe.wait_ge(v_ready, n + 1)
                    if not static(n) or n >= 1:
                        pe.wait_ge(x_updated, n)
                    if not static(n) or n >= 2:
                        pe.wait_ge(next_row_done, n)
                    for j in range(GT):
                        last = pe.matmul(outs[j], probsT[:, j, :], values[1 - par][:, j, :], start=True, stop=True)
                    last.then_inc(out_mm, 1)
                n = group_now(g, 2)
                if n is not None:
                    scores(n)
                r = group_now(g, 4)
                if r is not None:
                    pe.wait_ge(ln2.xn_ready, r + 1)
                    pe.wait_ge(ctxT_ready, min(g, G) if static(g) else g)
                    if static(g) and g > G:
                        pe.wait_ge(xrT_ready, r)
                    for j in range(GT):
                        last = pe.transpose(tr[:, bass.ts(j, P)], send[par][0][:, j, 0:D], c.ident[:])
                    last.then_inc(xr_transposed, 1)
                m = group_now(g, 1)
                if m is not None:
                    pe.wait_ge(xT_ready, m + 1)
                    if not static(m) or m >= 1:
                        pe.wait_ge(q_ready, m)
                        pe.wait_ge(k_ready, m)
                        pe.wait_ge(v_ready, m)
                    pe.matmul(q_bank[:], c.wq1[:], xnT[:], start=True, stop=True).then_inc(q_mm, 1)
                if r is not None:
                    pe.wait_ge(xrT_ready, r + 1)
                    pe.wait_ge(x_updated, min(g - 2, G) if static(g) else g - 2)
                    if not static(r) or r >= 1:
                        pe.wait_ge(place_step, PLACE_STEPS * r)
                    for j in range(GT):
                        last = pe.matmul(z[:, bass.ts(j, E1)], xrT[:, bass.ts(j, P)], c.w_route1[:], start=True, stop=True)
                    last.then_inc(z_mm, 1)
                w = group_now(g, 0)
                if w is not None:
                    pe.wait_ge(ln.xn_ready, w + 1)
                    if r is not None:
                        pe.wait_ge(xrT_ready, r + 1)
                    elif w >= 1:
                        pe.wait_ge(ctxT_ready, w)
                    for j in range(GT):
                        last = pe.transpose(tr[:, bass.ts(j, P)], ln.xn[:, j, :], c.ident[:])
                    last.then_inc(xn_transposed, 1)
                if m is not None:
                    pe.wait_ge(ctxT_ready, m + 1)
                    pe.matmul(k_bank[:], c.wk1[:], ctxT[:], start=True, stop=True).then_inc(k_mm, 1)
                    for j in range(GT):
                        last = pe.matmul(v_bank[:, bass.ts(j, P)], ctxT[:, bass.ts(j, P)], c.wv1[:], start=True, stop=True)
                    last.then_inc(v_mm, 1)
                if r is not None:
                    pe.wait_ge(chosen_ready, r + 1)
                    pe.matmul(ranks, c.earlier[:], chosen[:].rearrange("p t e -> p (t e)"), start=True, stop=False,
                              skip_group_check=True)
                    for j in range(GT):
                        last = pe.matmul(ranks[:, (j + 1) * E1:(GT + 1) * E1], c.ones_bf[:],
                                         chosen[:, j, :].unsqueeze(1).broadcast_to([P, GT - j, E1]), start=False,
                                         stop=(j == GT - 1), skip_group_check=True)
                    last.then_inc(ranks_mm, 1)
                if n is not None:
                    pe.wait_ge(exp_done, n + 1)
                    if not static(n) or n >= 1:
                        pe.wait_ge(pT_ready, n)
                    for j in range(GT):
                        last = pe.transpose(pT_bank[:, bass.ts(j, P)], probs[:, j, :], c.ident[:])
                    last.then_inc(pT_mm, 1)
                if w is not None:
                    pe.wait_ge(xT_ready, w + 1)
                    pe.wait_ge(loaded[par], 16 * ((w - par) // 2) + 16)
                    for j in range(GT):
                        last = pe.transpose(tr[0:DC, bass.ts(j, P)], ctx_in[par][:, j, :], c.ident[:])
                    last.then_inc(ctx_transposed, 1)

            group_steps(pe, LAG, step)


def tile_steps(eng, lag, step):
    for t in range(4):
        step(t, t)
    with eng.Fori(1, DTILES // 4) as i:
        for u in range(4):
            step(i * 4 + u, u)
    for t in range(DTILES // 4 * 4, DTILES + lag):
        step(t, t % 4)


def pair_tile(t, lag):
    return None if static(t) and not 0 <= t - lag < DTILES else t - lag


def mixture_of_layer1(nc, sb, psum, sem, c, dispatch, out):
    KH = HID1 // P
    HT = TP // P
    rows = [sb(f"d_rows{i}", [P, HT, ROW], F32) for i in range(4)]
    xT = [sb(f"d_xT{i}", [D, TP], F32) for i in range(2)]
    w12 = [sb(f"d_w12_{i}", [D, 2 * HID1], F32) for i in range(2)]
    w3 = [sb(f"d_w3_{i}", [P, HID1 // P * D], F32) for i in range(4)]
    silu = [sb(f"d_silu{i}", [P, KH * TP], F32) for i in range(2)]
    hidden = [sb(f"d_hidden{i}", [P, KH, TP], F32) for i in range(2)]
    shares = [sb(f"d_y{i}", [P, HT, D], F32) for i in range(2)]
    token = [sb(f"d_token{i}", [P, HT], U32) for i in range(2)]

    tr, u_bank, v_bank, y = ([psum(f"d_{n}{i}", [P, 512], F32) for i in range(2)] for n in ("tr", "u", "v", "y_bank"))

    loaded = [sem(f"d_loaded{i}") for i in range(4)]
    x_transposed, xT_ready, w12_ready, w3_ready = (sem(f"d_{n}") for n in ("x_transposed", "xT_ready", "w12_ready", "w3_ready"))
    u_mm, v_mm, silu_done, h_ready, y_mm, y_ready = (sem(f"d_{n}") for n in ("u_mm", "v_mm", "silu_done", "h_ready", "y_mm", "y_ready"))
    added, may_add = [sem(f"d_added{i}") for i in range(2)], sem("d_may_add")
    LAG = 2
    LOAD_AHEAD = 3

    with nc.Block() as block:
        @block.sync
        def _(sp):
            def load(t, u):
                first = sp.value_load(dispatch.tile_row[0:1, bass.ds(t, 1)], min_val=0, max_val=E1 * REGION + (DUMMY_TILES - 1) * TP)
                if not static(t) or t >= 4:
                    sp.wait_ge(y_ready, t - 3)
                sp.dma_start(rows[u][:], dispatch.rows[bass.ds(first, TP), :].rearrange("(p h) d -> p h d", h=HT)
                             ).then_inc(loaded[u], 16)

            def permit(w):
                before = sp.value_load(dispatch.tile_start[0:1, bass.ds(w, 1)], min_val=0, max_val=DTILES)
                sp.wait_ge(added[0], (before + 1) // 2 * (16 * HT) + 16)
                sp.wait_ge(added[1], before // 2 * (16 * HT) + 16)
                sp.sem_inc(may_add, 1)

            def step(t, u):
                if pair_tile(t, 0) is not None:
                    load(t, u)
                w = pair_tile(t, LOAD_AHEAD)
                if w is not None:
                    permit(w)

            tile_steps(sp, LOAD_AHEAD, step)

        @block.gpsimd
        def _(pool):
            def add(t, u):
                pool.wait_ge(y_ready, t + 1)
                wait_alone(pool, may_add, t + 1)
                for h in range(HT):
                    pool.indirect_dma_start(out, bass.IndirectOffsetOnAxis(ap=token[u % 2][:, h:h + 1], axis=0),
                                            shares[u % 2][:, h, :], None, compute_op=ALU.add).then_inc(added[u % 2], 16)

            def step(t, u):
                w = pair_tile(t, 2)
                if w is not None:
                    add(w, (u + 2) % 4)

            past_rows = out[B * S:, :].rearrange("(a p h) d -> p a h d", p=P, h=HT)
            for h in range(HT):
                pool.dma_start(past_rows[:, :, h], dispatch.fill[:, :, h, 0:D]).then_inc(added[h], 16)
            tile_steps(pool, LAG, step)
            pool.wait_ge(added[0], 16 + 16 * HT * (DTILES - DTILES // 2))
            pool.wait_ge(added[1], 16 + 16 * HT * (DTILES // 2))

        @block.vector
        def _(dve):
            def step(t, u):
                n = pair_tile(t, 0)
                if n is not None:
                    dve.wait_ge(x_transposed, n + 1)
                    if not static(n) or n >= 2:
                        dve.wait_ge(v_mm, n - 1)
                    dve.tensor_copy(xT[u % 2][:], tr[u % 2][:, 0:TP]).then_inc(xT_ready, 1)
                m = pair_tile(t, 1)
                if m is not None:
                    dve.wait_ge(silu_done, m + 1)
                    dve.wait_ge(v_mm, m + 1)
                    if not static(m) or m >= 2:
                        dve.wait_ge(y_mm, m - 1)
                    dve.tensor_tensor(hidden[1 - u % 2][:].rearrange("p k n -> p (k n)"), silu[1 - u % 2][:],
                                      v_bank[1 - u % 2][:], ALU.mult).then_inc(h_ready, 1)
                w = pair_tile(t, 2)
                if w is not None:
                    row = rows[(u + 2) % 4]
                    dve.wait_ge(added[u % 2], 16 + 16 * HT * ((w - u % 2) // 2))
                    dve.tensor_copy(token[u % 2][:], row[:, :, D])
                    dve.wait_ge(y_mm, w + 1)
                    for h in range(HT):
                        last = dve.tensor_scalar(shares[u % 2][:, h, :], y[u % 2][:, bass.ts(h, D)], row[:, h, D + 1:D + 2], None,
                                                 ALU.mult)
                    last.then_inc(y_ready, 1)

            tile_steps(dve, LAG, step)

        @block.scalar
        def _(act):
            def step(t, u):
                n, m = pair_tile(t, 0), pair_tile(t, 1)
                if m is not None:
                    act.wait_ge(u_mm, m + 1)
                    if not static(m) or m >= 2:
                        act.wait_ge(h_ready, m - 1)
                    act.activation(silu[1 - u % 2][:], u_bank[1 - u % 2][:], ACT.Silu).then_inc(silu_done, 1)
                if n is not None:
                    e = act.value_load(dispatch.tile_expert[0:1, bass.ds(n, 1)], min_val=0, max_val=E1 - 1)
                    if not static(n) or n >= 2:
                        act.wait_ge(v_mm, n - 1)
                    act.copy(w12[u % 2][:], c.w12[:, bass.ds(e, 1)].rearrange("d a i h -> d (a i h)")).then_inc(w12_ready, 1)
                    if not static(n) or n >= 4:
                        act.wait_ge(y_mm, n - 3)
                    act.copy(w3[u][:], c.w3[:, bass.ds(e, 1)].rearrange("p a b d -> p (a b d)")).then_inc(w3_ready, 1)

            tile_steps(act, LAG, step)

        @block.tensor
        def _(pe):
            def step(t, u):
                n = pair_tile(t, 0)
                m = pair_tile(t, 1)
                if m is not None:
                    q = 1 - u % 2
                    pe.wait_ge(xT_ready, m + 1)
                    pe.wait_ge(w12_ready, m + 1)
                    for i, (bank, mm, done) in enumerate(((u_bank, u_mm, silu_done), (v_bank, v_mm, h_ready))):
                        if not static(m) or m >= 2:
                            pe.wait_ge(done, m - 1)
                        for k in range(KH):
                            last = pe.matmul(bank[q][:, bass.ts(k, TP)], w12[q][:, i * HID1 + k * P:i * HID1 + k * P + P],
                                             xT[q][:], start=True, stop=True)
                        last.then_inc(mm, 1)
                if n is not None:
                    pe.wait_ge(loaded[u], 16 * ((n - u) // 4) + 16)
                    if not static(n) or n >= 2:
                        pe.wait_ge(xT_ready, n - 1)
                    for h in range(HT):
                        last = pe.transpose(tr[u % 2][:, bass.ts(h, P)], rows[u][:, h, 0:D], c.ident[:])
                    last.then_inc(x_transposed, 1)
                w = pair_tile(t, 2)
                if w is not None:
                    q = u % 2
                    pe.wait_ge(h_ready, w + 1)
                    pe.wait_ge(w3_ready, w + 1)
                    if not static(w) or w >= 2:
                        pe.wait_ge(y_ready, w - 1)
                    for h in range(HT):
                        for k in range(KH):
                            last = pe.matmul(y[q][:, bass.ts(h, D)], hidden[q][:, k, bass.ts(h, P)], w3[(u + 2) % 4][:, bass.ts(k, D)],
                                             start=(k == 0), stop=(k == KH - 1))
                    last.then_inc(y_mm, 1)

            tile_steps(pe, LAG, step)


def build(nc, a, out):
    with ExitStack() as ctx:
        def sb(name, shape, dt):
            return ctx.enter_context(nc.sbuf_tensor(name, shape, dt))

        def sem(name):
            return ctx.enter_context(nc.semaphore(name))

        X = sb("X", [P, TILES, D], F32)
        c = Shared()
        dispatch = Dispatch(nc, sb, sem)
        with ExitStack() as pctx:
            load_constants(nc, sb, lambda n, s, d: pctx.enter_context(nc.psum_tensor(n, s, d)), sem, c, a, X, dispatch)
        for phase, args in ((attention_of_layer0, (c, a, X, dispatch)), (mixture_of_layer0, (c, X)),
                            (attention_and_routing_of_layer1, (c, a, X, dispatch, out)),
                            (mixture_of_layer1, (c, dispatch, out))):
            with ExitStack() as own:
                phase(nc, lambda n, s, d: own.enter_context(nc.sbuf_tensor(n, s, d)),
                      lambda n, s, d: own.enter_context(nc.psum_tensor(n, s, d)),
                      lambda n: own.enter_context(nc.semaphore(n)), *args)


_INS = ["x", "ctx_768", "g_xattn", "g_ffn", "L0_xattn_wq", "L0_xattn_bq", "L0_xattn_wk", "L0_xattn_bk", "L0_xattn_wv",
        "L0_xattn_bv", "L0_xattn_wo", "L0_xattn_bo", "L0_ffn_proj_w", "L0_ffn_anchors", "L0_ffn_routing_temp",
        "L0_ffn_w1", "L0_ffn_w2", "L1_xattn_Wq", "L1_xattn_bq", "L1_xattn_Wk", "L1_xattn_bk", "L1_xattn_Wv",
        "L1_xattn_bv", "L1_ffn_Wg", "L1_ffn_W1", "L1_ffn_W2", "L1_ffn_W3"]


def shape_constants():
    import numpy as np
    part = np.arange(P)
    head_of_group = ((part[:, None] % 32) // DH == np.arange(4)[None, :]).astype(np.float32)
    head_cols = np.tile(np.repeat(np.eye(H, dtype=np.float32), S, axis=1), (2, 1))
    head_rows = np.tile(np.repeat(np.eye(H, dtype=np.float32), DH, axis=1), (3, 1))
    expert_cols = np.tile(np.repeat(np.eye(E0, dtype=np.float32), HID0, axis=1), (3, 1))
    return {"const_ident": np.eye(P, dtype=np.float32), "const_head_of_group": head_of_group,
            "const_head_cols": head_cols, "const_expert_cols": expert_cols, "const_head_rows": head_rows,
            "const_first_row": (np.arange(E1) * REGION).astype(np.float32),
            "const_earlier": np.triu(np.ones((P, P), np.float32), 1),
            "const_fill_tokens": (B * S + np.arange(E1 + DUMMY_TILES)[None, :, None] * TP + 2 * part[:, None, None]
                                  + np.arange(2)).astype(np.float32),
            "const_tokens": (np.arange(TILES)[None, :] * P + part[:, None]).astype(np.float32),
            "const_tile_sizes": (np.arange(MAX_TILES)[None, :] * TP).astype(np.float32),
            "const_up_to": np.tril(np.ones((E1, E1), np.float32))[None],
            "const_tile_number": np.arange(DTILES)[None, :].astype(np.float32),
            "const_expert_number": np.arange(E1).astype(np.float32)}


def kernel(**inputs):
    import numpy as np
    import concourse.bacc as bacc
    from concourse.bass_utils import run_bass_kernel_spmd

    nc = bacc.Bacc("TRN2", target_bir_lowering=False, num_devices=1)
    arrays = {n: np.ascontiguousarray(inputs[n]) for n in _INS}
    arrays["L0_ffn_routing_temp"] = arrays["L0_ffn_routing_temp"].reshape(1)
    arrays.update(shape_constants())
    aps = {n: nc.dram_tensor(f"in_{n}", v.shape, mybir.dt.from_np(v.dtype), kind="ExternalInput").ap()
           for n, v in arrays.items()}
    out = nc.dram_tensor("out_x", (B * S + (E1 + DUMMY_TILES) * TP, D), F32, kind="ExternalOutput").ap()
    build(nc, aps, out)
    r = run_bass_kernel_spmd(nc, [{f"in_{n}": v for n, v in arrays.items()}], core_ids=[0])
    return r.results[0]["out_x"][:B * S].reshape(B, S, D)
```
